# Optimizing a Trainium2 kernel written in Bass

```python
import numpy as np
import jax
import jax.numpy as jnp

def _softmax(x, axis=-1):
    return jax.nn.softmax(x, axis=axis)

def _gelu(x):
    return jax.nn.gelu(x, approximate=True)

def _silu(x):
    return jax.nn.silu(x)

def _sigmoid(x):
    return jax.nn.sigmoid(x)

def _layernorm(x, axis=-1, eps=1e-05):
    m = jnp.mean(x, axis=axis, keepdims=True)
    v = jnp.var(x, axis=axis, keepdims=True)
    return (x - m) / jnp.sqrt(v + eps)

def _scatter_add(tgt, idx, src, axis=0):
    return tgt.at[idx].add(src)

def _segment_sum(src, seg, n):
    return jax.ops.segment_sum(src, seg, n)
kernel_name = 'mk_early_fusion_d2_tok_img1024_r4_3ce176'

def setup_inputs(seed: int=0):
    np.random.seed(seed)
    _w = jnp.asarray

    def _rec_inputs():
        import jax
        import jax.numpy as jnp
        _rk = jax.random.key(seed)
        x = 7.22013e-05 + 1.00017 * jax.random.normal(jax.random.fold_in(_rk, 1), (8, 64, 256, 4), jnp.float32)
        txt = -1.32754e-10 + 0.999995 * jax.random.normal(jax.random.fold_in(_rk, 2), (8, 32, 256), jnp.float32)
        return (x, txt)
    x, txt = _rec_inputs()

    def _L0_tok_setup():
        import jax, jax.numpy as jnp
        import numpy as np
        B, F, L, H, D = (8, 64, 256, 4, 64)
        MODEL = H * F
        WIN = 128

        def _local_mask():
            m = np.ones((L, L), dtype=bool)
            m = np.tril(m, WIN - 1)
            m = np.triu(m, -(WIN - 1))
            return jnp.asarray(m)

        def _flatten(y):
            n = y.shape[0]
            return y.transpose(0, 2, 3, 1).reshape(n, L, -1)
        key = jax.random.key(seed)
        ks = jax.random.split(key, 12)
        s = lambda n: 1.0 / np.sqrt(n)
        xav = np.sqrt(6.0 / (L + L))
        return {'x': jax.random.normal(ks[0], (B, F, L, H), jnp.float32), 'Wq_w': jax.random.normal(ks[1], (D, F), jnp.float32) * s(F), 'Wq_b': jnp.zeros((D,), jnp.float32), 'Wk_w': jax.random.normal(ks[2], (D, F), jnp.float32) * s(F), 'Wk_b': jnp.zeros((D,), jnp.float32), 'Wv_w': jax.random.normal(ks[3], (D, F), jnp.float32) * s(F), 'Wv_b': jnp.zeros((D,), jnp.float32), 'w_bias': jax.random.uniform(ks[4], (L, L), jnp.float32, -xav, xav), 'out_w': jax.random.normal(ks[5], (H * D, MODEL), jnp.float32) * s(H * D), 'out_b': jnp.zeros((MODEL,), jnp.float32), 'ln_g': jnp.ones((MODEL,), jnp.float32), 'ln_b': jnp.zeros((MODEL,), jnp.float32), 'local_mask': _local_mask()}
    _L0_tok_all = _L0_tok_setup()
    _L0_tok_in = {k: v for k, v in _L0_tok_all.items() if k in ('Wq_w', 'Wq_b', 'Wk_w', 'Wk_b', 'Wv_w', 'Wv_b', 'w_bias', 'out_w', 'out_b', 'ln_g', 'ln_b', 'local_mask')}
    del _L0_tok_all

    def _L0_attn_setup():
        import jax, jax.numpy as jnp
        import numpy as np
        B, T, D = (4, 512, 256)
        H, DK = (8, 64)
        EPS = 1e-06

        def _xavier(key, shape):
            fan_in, fan_out = (shape[1], shape[0])
            lim = float(np.sqrt(6.0 / (fan_in + fan_out)))
            return jax.random.uniform(key, shape, jnp.float32, -lim, lim)

        def _phi(u):
            return jax.nn.elu(u) + 1.0
        key = jax.random.key(seed)
        ks = jax.random.split(key, 7)
        x = jax.random.normal(ks[0], (B, T, D), jnp.float32)
        W_Q = _xavier(ks[1], (H * DK, D))
        W_K = _xavier(ks[2], (H * DK, D))
        W_V = _xavier(ks[3], (H * DK, D))
        W_g_w = _xavier(ks[4], (H * DK, D))
        W_g_b = jax.random.normal(ks[5], (H * DK,), jnp.float32) * 0.02
        W_O = _xavier(ks[6], (D, H * DK))
        decay_log = jnp.zeros((H,), jnp.float32)
        return {'x': x, 'W_Q': W_Q, 'W_K': W_K, 'W_V': W_V, 'W_g_w': W_g_w, 'W_g_b': W_g_b, 'W_O': W_O, 'decay_log': decay_log}
    _L0_attn_all = _L0_attn_setup()
    _L0_attn_in = {k: v for k, v in _L0_attn_all.items() if k in ('W_Q', 'W_K', 'W_V', 'W_g_w', 'W_g_b', 'W_O', 'decay_log')}
    del _L0_attn_all

    def _L0_ffn_setup():
        import jax, jax.numpy as jnp
        import numpy as np
        IN_FEATURES = 256
        ACT_BITS = 4

        def _hadamard(size: int) -> np.ndarray:
            h = np.array([[1.0]], dtype=np.float64)
            while h.shape[0] < size:
                h = np.block([[h, h], [h, -h]])
            return (h / np.sqrt(size)).astype(np.float32)

        def _quantize_activations(x, bits=ACT_BITS):
            pos = 2 ** (bits - 1) - 1
            neg = 2 ** (bits - 1)
            scale = jnp.clip(jnp.max(jnp.abs(jax.lax.stop_gradient(x)), axis=-1, keepdims=True), 1e-05) / pos
            q = jnp.clip(jnp.round(x / scale), -neg, pos) * scale
            return x + jax.lax.stop_gradient(q - x)

        def _ternary_quantize_ste(w):
            scale = jnp.clip(jnp.mean(jnp.abs(jax.lax.stop_gradient(w)), axis=1, keepdims=True), 1e-05)
            n = w / scale
            tern = jnp.where(n > 0.5, 1.0, jnp.where(n < -0.5, -1.0, 0.0))
            q = tern * scale
            return w + jax.lax.stop_gradient(q - w)
        key = jax.random.key(seed)
        k1, k2 = jax.random.split(key)
        x = jax.random.normal(k1, (8, 2048, IN_FEATURES), dtype=jnp.float32)
        bound = 1.0 / np.sqrt(IN_FEATURES)
        weight = jax.random.uniform(k2, (256, IN_FEATURES), dtype=jnp.float32, minval=-bound, maxval=bound)
        return {'x': x, 'weight': weight}
    _L0_ffn_all = _L0_ffn_setup()
    _L0_ffn_in = {k: v for k, v in _L0_ffn_all.items() if k in ('weight',)}
    del _L0_ffn_all

    def _L1_attn_setup():
        import jax, jax.numpy as jnp
        import numpy as np
        B, N, C = (8, 1024, 256)
        key = jax.random.key(seed)
        k1, k2, k3 = jax.random.split(key, 3)
        x = jax.random.normal(k1, (B, N, C), dtype=jnp.float32)
        w_qkv = jax.random.normal(k2, (3 * C, C), dtype=jnp.float32) * C ** (-0.5)
        w_conv1 = jax.random.normal(k3, (C,), dtype=jnp.float32) * C ** (-0.5)
        return {'x': x, 'w_qkv': w_qkv, 'w_conv1': w_conv1}
    _L1_attn_all = _L1_attn_setup()
    _L1_attn_in = {k: v for k, v in _L1_attn_all.items() if k in ('w_qkv', 'w_conv1')}
    del _L1_attn_all

    def _L1_ffn_setup():
        import jax, jax.numpy as jnp
        import numpy as np
        D = 256
        H = 192
        E = 8
        K = 2
        NS = 2
        ROUTE_SCALE = 1.0

        def _gated_mlp(x, w1, w2):
            h = x @ w1.T
            y, g = jnp.split(h, 2, axis=-1)
            return y * jax.nn.silu(g) @ w2.T
        key = jax.random.key(seed)
        ks = jax.random.split(key, 6)
        s = 0.02
        return {'x': jax.random.normal(ks[0], (2, 256, D), jnp.float32), 'gate_w': jax.random.normal(ks[1], (E, D), jnp.float32) * s, 'W1': jax.random.normal(ks[2], (E, 2 * H, D), jnp.float32) * s, 'W2': jax.random.normal(ks[3], (E, D, H), jnp.float32) * s, 'Ws1': jax.random.normal(ks[4], (2 * NS * H, D), jnp.float32) * s, 'Ws2': jax.random.normal(ks[5], (D, NS * H), jnp.float32) * s}
    _L1_ffn_all = _L1_ffn_setup()
    _L1_ffn_in = {k: v for k, v in _L1_ffn_all.items() if k in ('gate_w', 'W1', 'W2', 'Ws1', 'Ws2')}
    del _L1_ffn_all
    return {'x': x, 'txt': txt, 'L0_tok_Wq_w': _L0_tok_in['Wq_w'], 'L0_tok_Wq_b': _L0_tok_in['Wq_b'], 'L0_tok_Wk_w': _L0_tok_in['Wk_w'], 'L0_tok_Wk_b': _L0_tok_in['Wk_b'], 'L0_tok_Wv_w': _L0_tok_in['Wv_w'], 'L0_tok_Wv_b': _L0_tok_in['Wv_b'], 'L0_tok_w_bias': _L0_tok_in['w_bias'], 'L0_tok_out_w': _L0_tok_in['out_w'], 'L0_tok_out_b': _L0_tok_in['out_b'], 'L0_tok_ln_g': _L0_tok_in['ln_g'], 'L0_tok_ln_b': _L0_tok_in['ln_b'], 'L0_tok_local_mask': _L0_tok_in['local_mask'], 'L0_attn_W_Q': _L0_attn_in['W_Q'], 'L0_attn_W_K': _L0_attn_in['W_K'], 'L0_attn_W_V': _L0_attn_in['W_V'], 'L0_attn_W_g_w': _L0_attn_in['W_g_w'], 'L0_attn_W_g_b': _L0_attn_in['W_g_b'], 'L0_attn_W_O': _L0_attn_in['W_O'], 'L0_attn_decay_log': _L0_attn_in['decay_log'], 'L0_ffn_weight': _L0_ffn_in['weight'], 'L1_attn_w_qkv': _L1_attn_in['w_qkv'], 'L1_attn_w_conv1': _L1_attn_in['w_conv1'], 'L1_ffn_gate_w': _L1_ffn_in['gate_w'], 'L1_ffn_W1': _L1_ffn_in['W1'], 'L1_ffn_W2': _L1_ffn_in['W2'], 'L1_ffn_Ws1': _L1_ffn_in['Ws1'], 'L1_ffn_Ws2': _L1_ffn_in['Ws2']}

def reference(x, txt, L0_tok_Wq_w, L0_tok_Wq_b, L0_tok_Wk_w, L0_tok_Wk_b, L0_tok_Wv_w, L0_tok_Wv_b, L0_tok_w_bias, L0_tok_out_w, L0_tok_out_b, L0_tok_ln_g, L0_tok_ln_b, L0_tok_local_mask, L0_attn_W_Q, L0_attn_W_K, L0_attn_W_V, L0_attn_W_g_w, L0_attn_W_g_b, L0_attn_W_O, L0_attn_decay_log, L0_ffn_weight, L1_attn_w_qkv, L1_attn_w_conv1, L1_ffn_gate_w, L1_ffn_W1, L1_ffn_W2, L1_ffn_Ws1, L1_ffn_Ws2):
    import jax
    import jax.numpy as jnp

    def _L0_tok_ref(x, Wq_w, Wq_b, Wk_w, Wk_b, Wv_w, Wv_b, w_bias, out_w, out_b, ln_g, ln_b, local_mask):
        import jax, jax.numpy as jnp
        import numpy as np
        B, F, L, H, D = (8, 64, 256, 4, 64)
        MODEL = H * F
        WIN = 128

        def _local_mask():
            m = np.ones((L, L), dtype=bool)
            m = np.tril(m, WIN - 1)
            m = np.triu(m, -(WIN - 1))
            return jnp.asarray(m)

        def _flatten(y):
            n = y.shape[0]
            return y.transpose(0, 2, 3, 1).reshape(n, L, -1)

        def proj(w, b):
            y = jnp.einsum('nclh,dc->ndlh', x, w) + b[None, :, None, None]
            return _flatten(y)
        q = proj(Wq_w, Wq_b)
        k = proj(Wk_w, Wk_b)
        v = proj(Wv_w, Wv_b)
        wb = w_bias * local_mask.astype(w_bias.dtype)
        ew = jnp.exp(wb)
        ek = jnp.exp(k)
        num = jnp.einsum('ts,nsd->ntd', ew, ek * v)
        den = jnp.einsum('ts,nsd->ntd', ew, ek)
        y = jax.nn.sigmoid(q) * num / den
        h = y @ out_w + out_b + _flatten(x)
        mu = jnp.mean(h, axis=-1, keepdims=True)
        var = jnp.mean(jnp.square(h - mu), axis=-1, keepdims=True)
        return (h - mu) * jax.lax.rsqrt(var + 1e-05) * ln_g + ln_b

    def _L0_attn_ref(x, W_Q, W_K, W_V, W_g_w, W_g_b, W_O, decay_log):
        import jax, jax.numpy as jnp
        import numpy as np
        B, T, D = (4, 512, 256)
        H, DK = (8, 64)
        EPS = 1e-06

        def _xavier(key, shape):
            fan_in, fan_out = (shape[1], shape[0])
            lim = float(np.sqrt(6.0 / (fan_in + fan_out)))
            return jax.random.uniform(key, shape, jnp.float32, -lim, lim)

        def _phi(u):
            return jax.nn.elu(u) + 1.0
        b, t, d = x.shape
        q = _phi((x @ W_Q.T).reshape(b, t, H, DK))
        k = _phi((x @ W_K.T).reshape(b, t, H, DK))
        v = (x @ W_V.T).reshape(b, t, H, DK)
        gamma = jax.nn.sigmoid(decay_log)
        g4 = gamma[None, :, None, None]
        g3 = gamma[None, :, None]
        qT = jnp.moveaxis(q, 1, 0)
        kT = jnp.moveaxis(k, 1, 0)
        vT = jnp.moveaxis(v, 1, 0)
        S0 = jnp.zeros((b, H, DK, DK), x.dtype)
        z0 = jnp.zeros((b, H, DK), x.dtype)

        def step(carry, inp):
            S, z = carry
            qt, kt, vt = inp
            S = g4 * S + jnp.einsum('bhi,bhj->bhij', kt, vt)
            z = g3 * z + kt
            num = jnp.einsum('bhij,bhi->bhj', S, qt)
            den = jnp.sum(z * qt, axis=-1, keepdims=True) + EPS
            return ((S, z), num / den)
        _, ys = jax.lax.scan(step, (S0, z0), (qT, kT, vT))
        outputs = jnp.moveaxis(ys, 0, 1)
        gate = jax.nn.sigmoid(x @ W_g_w.T + W_g_b).reshape(b, t, H, DK)
        y = (outputs * gate).reshape(b, t, H * DK)
        return y @ W_O.T

    def _L0_ffn_ref(x, weight):
        import jax, jax.numpy as jnp
        import numpy as np
        IN_FEATURES = 256
        ACT_BITS = 4

        def _hadamard(size: int) -> np.ndarray:
            h = np.array([[1.0]], dtype=np.float64)
            while h.shape[0] < size:
                h = np.block([[h, h], [h, -h]])
            return (h / np.sqrt(size)).astype(np.float32)

        def _quantize_activations(x, bits=ACT_BITS):
            pos = 2 ** (bits - 1) - 1
            neg = 2 ** (bits - 1)
            scale = jnp.clip(jnp.max(jnp.abs(jax.lax.stop_gradient(x)), axis=-1, keepdims=True), 1e-05) / pos
            q = jnp.clip(jnp.round(x / scale), -neg, pos) * scale
            return x + jax.lax.stop_gradient(q - x)

        def _ternary_quantize_ste(w):
            scale = jnp.clip(jnp.mean(jnp.abs(jax.lax.stop_gradient(w)), axis=1, keepdims=True), 1e-05)
            n = w / scale
            tern = jnp.where(n > 0.5, 1.0, jnp.where(n < -0.5, -1.0, 0.0))
            q = tern * scale
            return w + jax.lax.stop_gradient(q - w)
        H = jnp.asarray(_hadamard(IN_FEATURES))
        xh = x @ H
        xq = _quantize_activations(xh)
        wq = _ternary_quantize_ste(weight)
        return jnp.einsum('bsi,oi->bso', xq, wq)

    def _L1_attn_ref(x, w_qkv, w_conv1):
        import jax, jax.numpy as jnp
        import numpy as np
        B, N, C = (8, 1024, 256)
        b, n, c = x.shape
        scale = c ** (-0.5)
        qkv = jnp.einsum('bnc,dc->bnd', x, w_qkv)
        q = qkv[..., :c]
        k = qkv[..., c:2 * c]
        v = qkv[..., 2 * c:]
        agent = jnp.einsum('bnc,c->bn', q, w_conv1)
        agent_attn = jax.nn.softmax(jnp.einsum('bn,bnc->bc', agent * scale, k), axis=-1)
        agent_v = jax.nn.softmax(jnp.einsum('bc,bnc->bn', agent_attn, v), axis=-1)
        agent_v = jnp.einsum('bn,bnc->bc', agent_v, v)
        agent_tok = jax.nn.softmax(agent[:, :, None], axis=-1)
        return agent_tok * agent_v[:, None, :]

    def _L1_ffn_ref(x, gate_w, W1, W2, Ws1, Ws2):
        import jax, jax.numpy as jnp
        import numpy as np
        D = 256
        H = 192
        E = 8
        K = 2
        NS = 2
        ROUTE_SCALE = 1.0

        def _gated_mlp(x, w1, w2):
            h = x @ w1.T
            y, g = jnp.split(h, 2, axis=-1)
            return y * jax.nn.silu(g) @ w2.T
        x_shape = x.shape
        xf = x.reshape(-1, D)
        T = xf.shape[0]
        scores = jax.nn.softmax((xf @ gate_w.T).astype(jnp.float32), axis=-1)
        top_vals, top_idx = jax.lax.top_k(scores, K)
        weights = (top_vals * ROUTE_SCALE).astype(x.dtype)
        w_dense = jnp.zeros((T, E), x.dtype).at[jnp.arange(T)[:, None], top_idx].set(weights)
        h = jnp.einsum('td,ehd->teh', xf, W1)
        y, g = jnp.split(h, 2, axis=-1)
        eo = jnp.einsum('teh,edh->ted', y * jax.nn.silu(g), W2)
        z = jnp.einsum('te,ted->td', w_dense, eo)
        z = z + _gated_mlp(xf, Ws1, Ws2)
        return z.reshape(x_shape)
    h = _L0_tok_ref(x, L0_tok_Wq_w, L0_tok_Wq_b, L0_tok_Wk_w, L0_tok_Wk_b, L0_tok_Wv_w, L0_tok_Wv_b, L0_tok_w_bias, L0_tok_out_w, L0_tok_out_b, L0_tok_ln_g, L0_tok_ln_b, L0_tok_local_mask)
    h = jnp.concatenate([h, txt], axis=1)
    h = h + _L0_attn_ref(_layernorm(h, axis=-1), L0_attn_W_Q, L0_attn_W_K, L0_attn_W_V, L0_attn_W_g_w, L0_attn_W_g_b, L0_attn_W_O, L0_attn_decay_log)
    h = h + _L0_ffn_ref(_layernorm(h, axis=-1), L0_ffn_weight)
    h = h + _L1_attn_ref(_layernorm(h, axis=-1), L1_attn_w_qkv, L1_attn_w_conv1)
    h = h + _L1_ffn_ref(_layernorm(h, axis=-1), L1_ffn_gate_w, L1_ffn_W1, L1_ffn_W2, L1_ffn_Ws1, L1_ffn_Ws2)
    return h

_drawn_inputs = setup_inputs


def setup_inputs(seed=0):
    import zlib

    import numpy as np

    out = dict(_drawn_inputs(seed))
    spreads = {'L0_tok_Wq_b': (0.0, 0.573),
     'L0_tok_Wk_b': (0.0, 0.8),
     'L0_tok_Wv_b': (0.0, 0.1),
     'L0_tok_out_b': (0.0, 0.1),
     'L0_tok_ln_g': (1.0, 0.2),
     'L0_tok_ln_b': (0.0, 0.1),
     'L0_attn_decay_log': (0.0, 0.374)}
    factors = {'L0_tok_w_bias': 5.788,
     'L0_attn_W_Q': 3.134,
     'L0_attn_W_g_b': 6.143,
     'L1_attn_w_conv1': 2.995,
     'L1_ffn_gate_w': 8.0,
     'L1_ffn_W1': 8.0,
     'L1_ffn_W2': 8.0,
     'L1_ffn_Ws1': 3.165,
     'L1_ffn_Ws2': 3.139}
    for name, (base, spread) in spreads.items():
        noise = np.random.default_rng([zlib.crc32(name.encode()), seed]).standard_normal(out[name].shape)
        drawn = base * np.exp(spread * noise) if base else spread * noise
        out[name] = jnp.asarray(drawn.astype(out[name].dtype))
    for name, factor in factors.items():
        out[name] = (out[name] * factor).astype(out[name].dtype)
    return out
```

```python
from contextlib import ExitStack

import concourse.bass as bass
from concourse import mybir

F32 = mybir.dt.float32
F32R = mybir.dt.float32r
BF16 = mybir.dt.bfloat16
U8 = mybir.dt.uint8
ALU = mybir.AluOpType
ACT = mybir.ActivationFunctionType
AX = mybir.AxisListType

P = 128
B, F, L, H0 = 8, 64, 256, 4
TXT = 32
D = 256
T = L + TXT
NT = 3
TP = NT * P
ROWS = (P, P, TXT)
HA, DK = 8, 64
DA = HA * DK
E, HE, HS = 8, 192, 384
NJ = E + HS // HE
LN_EPS = 1e-5
ATT_EPS = 1e-6
ACT_POS, ACT_NEG = 7.0, 8.0
ROUND = 12582912.0
FC = D // P


def ge(eng, sem, value):
    if isinstance(value, int) and value <= 0:
        return
    eng.wait_ge(sem, value)


class Steps:

    def __init__(self, eng, sem, start):
        self.eng, self.sem, self.n = eng, sem, start

    def __call__(self, ins):
        self.n = self.n + 1
        ins.then_inc(self.sem, 1)
        self.eng.wait_ge(self.sem, self.n)


def skewed(eng, step):
    step(-2, True, False, False)
    step(-1, True, True, False)
    step(0, True, True, True)
    with eng.Fori(1, B - 2) as b:
        step(b, True, True, True)
    step(B - 2, False, True, True)
    step(B - 1, False, False, True)


def row_broadcast(ap, n):
    return ap.rearrange("(a n) -> a n", a=1).to_broadcast([P, n])


def token_mixer(nc, g, ins):
    with ExitStack() as ctx:
        def sb(name, shape, dt=F32):
            return ctx.enter_context(nc.sbuf_tensor(name, shape, dt))

        def sem(name):
            return ctx.enter_context(nc.semaphore(name))

        ps = g["ps"]
        hres = g["hres"]
        ident = g["ident"]
        stage = sb("stage", [P, FC, 4 * DA])
        wqkv = sb("a_wqkv", [F + 1, 3 * F])
        ewt = sb("a_ewt", [P, 2, L])
        mask8 = sb("a_mask8", [P, 2, L], U8)
        maskf = sb("a_maskf", [P, 2, L])
        outw = sb("a_outw", [P, FC, D])
        outb = sb("a_outb", [P, D])
        lng = sb("a_lng", [P, D])
        lnb = sb("a_lnb", [P, D])
        xt = sb("a_xt", [F + 1, H0, L])
        xfl = sb("a_xfl", [P, 2, D])
        xb = sb("a_xb", [P, 2, D])
        nk = sb("a_nk", [P, 2, 2, 2 * D])
        eq = sb("a_eq", [P, 2, 2, D])
        den = sb("a_den", [P, 2, D])
        rden = sb("a_rden", [P, 2, D])
        y = sb("a_y", [P, 2, D])
        yt = sb("a_yt", [P, FC, L])
        hp = sb("a_hp", [P, 2, D])
        hn = sb("a_hn", [P, 2, D])
        stats = sb("a_stats", [P, 2, 6])
        mv = sb("a_mv", [P, 2, 2])
        ve = sb("a_ve", [P, 2, 1])
        tick = sb("a_tick", [P, 1])
        rstd = sb("a_rstd", [P, 2, 1])
        gam = sb("a_gam", [P, HA])
        lgam = sb("a_lgam", [P, HA])
        age = sb("a_age", [P, T])
        agm = sb("a_agm", [P, T])
        draw = sb("a_draw", [P, HA])
        gbraw = sb("a_gbraw", [64, DA])

        w_in = sem("a_w_in")
        ew_in = sem("a_ew_in")
        x_in = sem("a_x_in")
        xf_in = sem("a_xf_in")
        txt_in = sem("a_txt_in")
        attw_in = sem("a_attw_in")
        moew_in = sem("a_moew_in")
        ones_set = sem("a_ones_set")
        text_zeroed = sem("a_text_zeroed")
        mask_applied = sem("a_mask_applied")
        ew_ready = sem("a_ew_ready")
        qkv_done = sem("a_qkv_done")
        exps_done = sem("a_exps_done")
        ekv_done = sem("a_ekv_done")
        nd_done = sem("a_nd_done")
        y_done = sem("a_y_done")
        turned = sem("a_turned")
        yt_done = sem("a_yt_done")
        out_done = sem("a_out_done")
        hp_done = sem("a_hp_done")
        xb_done = sem("a_xb_done")
        var_done = sem("a_var_done")
        rstd_done = sem("a_rstd_done")
        y_steps = sem("a_y_steps")
        ln_steps = sem("a_ln_steps")
        hi_done = sem("a_hi_done")
        lo_done = sem("a_lo_done")
        gb_steps = sem("a_gb_steps")
        gam_in = sem("a_gam_in")
        gam_steps = sem("a_gam_steps")
        gam_ready = sem("a_gam_ready")
        age_steps = sem("a_age_steps")
        decay_set = sem("a_decay_set")
        pool_done = sem("a_pool_done")

        qkv = ps[:, 0:4, :].rearrange("p (l a) (c j) -> p l (a c) j", l=2, c=2)

        def part(i):
            return qkv[:, :, :, i * F:(i + 1) * F]

        def heads(ap):
            return ap.rearrange("p l (h d) -> p l h d", h=H0)

        block = ctx.enter_context(nc.Block())

        @block.sync
        def _(sp):
            x_t, x_flat = ins["x_t"], ins["x_flat"]

            def load_x(b):
                if isinstance(b, int):
                    xs = x_t[b]
                else:
                    xs = x_t[bass.ds(b, 1)].rearrange("a c h l -> (a c) h l")
                ge(sp, qkv_done, b)
                sp.dma_start(xt[0:F], xs).then_inc(x_in, 16)

            def load_flat(b):
                fs = x_flat[b] if isinstance(b, int) else x_flat[bass.ds(b, 1)].rearrange("a l f -> (a l) f")
                ge(sp, xb_done, b)
                sp.dma_start(xfl[:], fs.rearrange("(t p) f -> p t f", p=P)).then_inc(xf_in, 16)

            load_x(0)
            for i, n in enumerate("qkv"):
                sp.dma_start(wqkv[0:F, i * F:(i + 1) * F], ins[f"w{n}_t"]).then_inc(w_in, 16)
                sp.dma_start(wqkv[F:F + 1, i * F:(i + 1) * F],
                             ins[f"b{n}"].rearrange("(a n) -> a n", a=1)).then_inc(w_in, 16)
            sp.dma_start(ewt[:], ins["w_bias_t"].rearrange("(s p) t -> p s t", p=P)).then_inc(ew_in, 16)
            sp.dma_start(mask8[:], ins["mask_t"].rearrange("(s p) t -> p s t", p=P)).then_inc(ew_in, 16)
            sp.dma_start(outb[:], row_broadcast(ins["out_b"], D)).then_inc(w_in, 16)
            sp.dma_start(outw[:], ins["out_w"].rearrange("(c p) n -> p c n", p=P)).then_inc(w_in, 16)
            sp.dma_start(lng[:], row_broadcast(ins["ln_g"], D)).then_inc(w_in, 16)
            sp.dma_start(lnb[:], row_broadcast(ins["ln_b"], D)).then_inc(w_in, 16)
            load_flat(0)
            load_x(1)
            sp.dma_start(draw[:], row_broadcast(ins["decay_log"], HA)).then_inc(gam_in, 16)
            for i, n in enumerate(("W_Q_t", "W_K_t", "W_V_t", "W_g_t")):
                sp.dma_start(stage[:, :, i * DA:(i + 1) * DA],
                             ins[n].rearrange("(c p) n -> p c n", p=P)).then_inc(attw_in, 16)
            for r in (0, 32):
                sp.dma_start(gbraw[r:r + 1, :],
                             ins["W_g_b"].rearrange("(a n) -> a n", a=1)).then_inc(attw_in, 16)
            load_x(2)
            with sp.Fori(3, B) as b:
                load_x(b)
                load_flat(b - 2)
            load_flat(B - 2)
            load_flat(B - 1)
            sp.dma_start(g["wo"][:], ins["W_O_t"].rearrange("(c p) n -> p c n", p=P)).then_inc(moew_in, 16)
            for e in range(E):
                sp.dma_start(g["w1raw"][:, :, e * 2 * HE:(e + 1) * 2 * HE],
                             ins["W1_t"][e].rearrange("(c p) n -> p c n", p=P)).then_inc(moew_in, 16)
                sp.dma_start(g["w2"][:, :, e, :],
                             ins["W2_t"][e].rearrange("(c p) n -> p c n", p=HE // 2)).then_inc(moew_in, 16)
            for j in range(NJ - E):
                for gate in range(2):
                    sp.dma_start(g["w1raw"][:, :, (2 * (E + j) + gate) * HE:(2 * (E + j) + gate + 1) * HE],
                                 ins["Ws1_t"].rearrange("(c p) n -> p c n", p=P)[
                                     :, :, gate * HS + j * HE:gate * HS + (j + 1) * HE]).then_inc(moew_in, 16)
                sp.dma_start(g["w2"][:, :, E + j, :],
                             ins["Ws2_t"][j * HE:(j + 1) * HE].rearrange("(c p) n -> p c n", p=HE // 2)
                             ).then_inc(moew_in, 16)
            sp.wait_ge(moew_in, 16 * (1 + 2 * E + 3 * (NJ - E)))
            sp.wait_ge(txt_in, 16 * B)

        @block.tensor
        def _(pe):
            def qkv_products(b):
                ge(pe, x_in, 16 * b + 16)
                if isinstance(b, int) and b == 0:
                    pe.wait_ge(ones_set, 1)
                    pe.wait_ge(w_in, 16 * 10)
                ge(pe, ekv_done, b)
                ge(pe, exps_done, b)
                for lt in range(2):
                    for h in range(H0):
                        mm = nc.tensor.matmul(qkv[:, lt, h, 0:3 * F], xt[:, h, lt * P:(lt + 1) * P],
                                              wqkv[:, :], start=True, stop=True)
                mm.then_inc(qkv_done, 1)

            def turn(b):
                pe.wait_ge(y_done, b + 1)
                if isinstance(b, int) and b == 0:
                    pe.wait_ge(g["ident_ready"], 1)
                ge(pe, yt_done, b)
                for fc in range(FC):
                    for t in range(2):
                        mm = nc.tensor.transpose(ps[:, 6, fc * L + t * P:fc * L + (t + 1) * P],
                                                 y[:, t, fc * P:(fc + 1) * P], ident[:])
                mm.then_inc(turned, 1)

            def sums(b):
                if isinstance(b, int) and b == 0:
                    pe.wait_ge(ew_ready, 1)
                pe.wait_ge(ekv_done, b + 1)
                pe.wait_ge(exps_done, b + 1)
                ge(pe, y_done, b)
                for t in range(2):
                    for s in range(2):
                        mm = nc.tensor.matmul(ps[:, 4 + t, :], ewt[:, s, t * P:(t + 1) * P],
                                              nk[:, b % 2, s, :], start=s == 0, stop=s == 1)
                mm.then_inc(nd_done, 1)

            def project(b):
                pe.wait_ge(yt_done, b + 1)
                ge(pe, hp_done, b)
                for t in range(2):
                    for fc in range(FC):
                        mm = nc.tensor.matmul(ps[:, 7, t * D:(t + 1) * D], yt[:, fc, t * P:(t + 1) * P],
                                              outw[:, fc, :], start=fc == 0, stop=fc == FC - 1)
                mm.then_inc(out_done, 1)

            def step(b, s1, s2, s3):
                if s1:
                    qkv_products(b + 2)
                if s3:
                    turn(b)
                if s2:
                    sums(b + 1)
                if s3:
                    project(b)

            skewed(pe, step)

        @block.scalar
        def _(act):
            act.wait_ge(mask_applied, 1)
            nc.scalar.activation(ewt[:], maskf[:], ACT.Exp).then_inc(ew_ready, 1)

            def exps(b):
                act.wait_ge(qkv_done, b + 1)
                ge(act, nd_done, b - 1)
                nc.scalar.activation(heads(nk[:, b % 2, :, D:2 * D]) if isinstance(b, int) else
                                     nk[:, b % 2, :, D:2 * D].rearrange("p l (h d) -> p l h d", h=H0),
                                     part(1), ACT.Exp)
                ge(act, y_done, b - 1)
                nc.scalar.activation(heads(eq[:, b % 2]), part(0), ACT.Exp, scale=-1.0).then_inc(exps_done, 1)

            def copy_yt(b):
                act.wait_ge(turned, b + 1)
                ge(act, out_done, b)
                nc.scalar.copy(yt[:].rearrange("p c l -> p (c l)"), ps[:, 6, :]).then_inc(yt_done, 1)

            def step(b, s1, s2, s3):
                if s3:
                    copy_yt(b)
                if s1:
                    exps(b + 2)

            skewed(act, step)
            act.wait_ge(attw_in, 16 * 6)
            act.wait_ge(gb_steps, 1)
            nc.scalar.copy(g["gb"][0:1, :], gbraw[0:1, :]).then_inc(gb_steps, 1)
            nc.scalar.copy(g["gbh"][32:33, :], gbraw[32:33, :]).then_inc(gb_steps, 1)
            act.wait_ge(gam_in, 16)
            nc.scalar.activation(gam[:], draw[:], ACT.Exp, scale=-1.0).then_inc(gam_steps, 1)
            act.wait_ge(gam_steps, 4)
            nc.scalar.activation(lgam[:], gam[:], ACT.Ln).then_inc(gam_ready, 1)
            act.wait_ge(gam_ready, 1)
            act.wait_ge(age_steps, 3)
            for h in range(HA):
                nc.scalar.activation(g["decay"][:, h, 0:T], agm[:], ACT.Exp,
                                     scale=lgam[:, h:h + 1]).then_inc(decay_set, 1)

        @block.vector
        def _(dve):
            nc.vector.memset(xt[F:F + 1], 1.0).then_inc(ones_set, 1)
            for b in range(B):
                ms = nc.vector.memset(hres[:, NT * b + 2, :], 0.0)
            ms.then_inc(text_zeroed, 1)
            dve.wait_ge(ew_in, 32)
            nc.vector.tensor_copy(maskf[:], mask8[:]).then_inc(y_steps, 1)
            dve.wait_ge(y_steps, 1)
            nc.vector.tensor_tensor(maskf[:], maskf[:], ewt[:], ALU.mult).then_inc(mask_applied, 1)

            def weigh(b):
                dve.wait_ge(exps_done, b + 1)
                ge(dve, nd_done, b - 1)
                nc.vector.tensor_tensor(heads(nk[:, b % 2, :, 0:D]), heads(nk[:, b % 2, :, D:2 * D]),
                                        part(2), ALU.mult).then_inc(ekv_done, 1)

            def divide(b):
                step = Steps(dve, y_steps, b * 2 + 1)
                dve.wait_ge(nd_done, b + 1)
                step(nc.vector.scalar_tensor_tensor(out=den[:], in0=eq[:, b % 2], scalar=1.0,
                                                    in1=ps[:, 4:6, D:2 * D], op0=ALU.add, op1=ALU.mult))
                step(nc.vector.reciprocal(rden[:], den[:]))
                ge(dve, turned, b)
                nc.vector.tensor_tensor(y[:], ps[:, 4:6, 0:D], rden[:], ALU.mult).then_inc(y_done, 1)

            def norm(b):
                step = Steps(dve, ln_steps, b * 6)
                dve.wait_ge(out_done, b + 1)
                dve.wait_ge(xb_done, b + 1)
                nc.vector.tensor_tensor(hp[:].rearrange("p t f -> p (t f)"), ps[:, 7, :],
                                        xb[:].rearrange("p t f -> p (t f)"), ALU.add).then_inc(hp_done, 1)
                dve.wait_ge(hp_done, b + 1)
                for t in range(2):
                    step(nc.vector.bn_stats(stats[:, t, :], hp[:, t, :]))
                nc.vector.memset(tick[:], 0.0)
                for t in range(2):
                    last = nc.vector.bn_aggr(mv[:, t, :], stats[:, t, :])
                step(last)
                nc.vector.tensor_scalar(ve[:], mv[:, :, 1:2], LN_EPS, None, ALU.add).then_inc(var_done, 1)
                dve.wait_ge(rstd_done, b + 1)
                for t in range(2):
                    step(nc.vector.tensor_scalar(hn[:, t, :], hp[:, t, :], mv[:, t, 0:1], rstd[:, t, :],
                                                 ALU.subtract, ALU.mult))
                gb = lng[:].rearrange("p (a f) -> p a f", a=1).to_broadcast([P, 2, D])
                bb = lnb[:].rearrange("p (a f) -> p a f", a=1).to_broadcast([P, 2, D])
                step(nc.vector.tensor_tensor(hn[:], hn[:], gb, ALU.mult))
                nc.vector.tensor_tensor(hres[:, bass.ds(b * NT, 2), :] if not isinstance(b, int) else
                                        hres[:, b * NT:b * NT + 2, :], hn[:], bb, ALU.add)

            def step(b, s1, s2, s3):
                if s1:
                    weigh(b + 2)
                if s2:
                    divide(b + 1)
                if s3:
                    norm(b)

            skewed(dve, step)
            dve.wait_ge(hi_done, 1)
            nc.vector.tensor_tensor(g["wa_lo"][:], stage[:], g["wa_hi"][:].bitcast(F32),
                                    ALU.subtract).then_inc(lo_done, 1)
            dve.wait_ge(gb_steps, 3)
            nc.vector.tensor_tensor(g["gb"][32:33, :], gbraw[32:33, :], g["gbh"][32:33, :].bitcast(F32),
                                    ALU.subtract)
            dve.wait_ge(gam_steps, 1)
            step = Steps(dve, gam_steps, 1)
            step(nc.vector.tensor_scalar(gam[:], gam[:], 1.0, None, ALU.add))
            step(nc.vector.reciprocal(gam[:], gam[:]))
            step(nc.vector.tensor_scalar(gam[:], gam[:], 1e-18, None, ALU.max))

        @block.gpsimd
        def _(pool):
            pool.wait_ge(text_zeroed, 1)
            for b in range(B):
                pool.dma_start(hres[0:TXT, NT * b + 2, :], ins["txt"][b]).then_inc(txt_in, 16)
            nc.gpsimd.iota(age[:], [[1, T]], base=0, channel_multiplier=-1,
                           allow_small_or_imprecise_dtypes=True).then_inc(age_steps, 1)
            pool.wait_ge(age_steps, 1)
            nc.gpsimd.tensor_scalar(agm[:], age[:], 0.0, None, ALU.max).then_inc(age_steps, 1)
            nc.gpsimd.memset(g["gb"][:].bitcast(F32), 0.0).then_inc(gb_steps, 1)
            nc.gpsimd.memset(g["ones64"][:].bitcast(F32), 1.0).then_inc(age_steps, 1)

            def add_bias(b):
                pool.wait_ge(xf_in, 16 * b + 16)
                if isinstance(b, int) and b == 0:
                    pool.wait_ge(w_in, 16 * 10)
                ge(pool, hp_done, b)
                ob = outb[:].rearrange("p (a f) -> p a f", a=1).to_broadcast([P, 2, D])
                nc.gpsimd.tensor_tensor(xb[:], xfl[:], ob, ALU.add).then_inc(xb_done, 1)

            def root(b):
                pool.wait_ge(var_done, b + 1)
                nc.gpsimd.tensor_tensor(rstd[:], ve[:], g["mhalf"][:, 0:2].rearrange("p (t a) -> p t a", a=1),
                                        ALU.pow).then_inc(rstd_done, 1)

            add_bias(0)
            root(0)
            with pool.Fori(1, B) as b:
                add_bias(b)
                root(b)
            pool.wait_ge(attw_in, 16 * 6)
            nc.gpsimd.tensor_copy(g["wa_hi"][:], stage[:]).then_inc(hi_done, 1)
            for h in range(HA):
                pool.wait_ge(decay_set, h + 1)
                nc.gpsimd.affine_select(out=g["decay"][:, h, 0:T], in_=g["decay"][:, h, 0:T],
                                        compare_op=ALU.is_ge, fill=0.0, base=0, pattern=[[1, T]],
                                        channel_multiplier=-1).then_inc(pool_done, 1)
                pool.wait_ge(pool_done, 3 * h + 1)
                nc.gpsimd.tensor_copy(g["decay"][:, h, T:T + P + TXT],
                                      g["decay"][:, h, 0:P + TXT]).then_inc(pool_done, 1)
                nc.gpsimd.tensor_copy(g["decay"][:, h, T + P + TXT:T + P + 2 * TXT],
                                      g["decay"][:, h, 0:TXT]).then_inc(pool_done, 1)


def setup(nc, g):
    with ExitStack() as ctx:
        zeroed = ctx.enter_context(nc.semaphore("zeroed"))
        block = ctx.enter_context(nc.Block())

        @block.gpsimd
        def _(pool):
            nc.gpsimd.memset(g["mhalf"][:], -0.5)
            nc.gpsimd.memset(g["ident"][:], 0.0).then_inc(zeroed, 1)
            pool.wait_ge(zeroed, 1)
            nc.gpsimd.affine_select(out=g["ident"][:], in_=g["ident"][:], compare_op=ALU.not_equal,
                                    fill=1.0, base=0, pattern=[[-1, P]],
                                    channel_multiplier=1).then_inc(g["ident_ready"], 1)


def norm_stats(nc, dve, step, src, stats, mv, ve, tick, var_done):
    for t in range(NT):
        last = nc.vector.bn_stats(stats[:, t, :], src(t))
    step(last)
    nc.vector.memset(tick[:], 0.0)
    for t in range(NT):
        last = nc.vector.bn_aggr(mv[:, t, :], stats[:, t, :])
    step(last)
    nc.vector.tensor_scalar(ve[:], mv[:, :, 1:2], LN_EPS, None, ALU.add).then_inc(var_done, 1)


def res(g, b, t):
    if isinstance(b, int):
        return g["hres"][:, NT * b + t, :]
    return g["hres"][:, bass.ds(b * NT + t, 1), :].rearrange("p a f -> p (a f)")


def split_products(nc, out, x_hi, x_lo, w_hi, w_lo, start, stop):
    nc.tensor.matmul(out, x_hi, w_hi, start=start, stop=False)
    nc.tensor.matmul(out, x_hi, w_lo, start=False, stop=False)
    return nc.tensor.matmul(out, x_lo, w_hi, start=False, stop=stop)


def linear_attention(nc, g):
    with ExitStack() as ctx:
        def sb(name, shape, dt=F32):
            return ctx.enter_context(nc.sbuf_tensor(name, shape, dt))

        def sem(name):
            return ctx.enter_context(nc.semaphore(name))

        ps, hres, ident = g["ps"], g["hres"], g["ident"]
        wa_hi, wa_lo, wo = g["wa_hi"], g["wa_lo"], g["wo"]
        NP = HA // 2
        VW = DK + 1
        AW = T + P + 2 * TXT
        stats = sb("b_stats", [P, NT, 6])
        mv = sb("b_mv", [P, NT, 2])
        ve = sb("b_ve", [P, NT, 1])
        rstd = sb("b_rstd", [P, NT, 1])
        tick = sb("b_tick", [P, 1])
        xn = sb("b_xn", [P, NT, D])
        x_hi = sb("b_x_hi", [P, FC, TP], F32R)
        x_lo = sb("b_x_lo", [P, FC, TP], F32R)
        qk = sb("b_qk", [P, 2 * NP, TP])
        rl = sb("b_rl", [P, 2, T])
        ex = sb("b_ex", [P, 2, T])
        v = sb("b_v", [P, NT, HA, VW])
        sg = sb("b_sg", [P, NT, DA])
        a = sb("b_a", [P, 2, AW])
        dn = sb("b_dn", [P, NT, 2, 1])
        rd = sb("b_rd", [P, NT, 2, 1])
        y = sb("b_y", [P, NT, DA])
        yt = sb("b_yt", [P, NP, T])

        filled = sem("b_filled")
        ln_steps = sem("b_ln_steps")
        var_done = sem("b_var_done")
        rstd_done = sem("b_rstd_done")
        xn_done = sem("b_xn_done")
        x_turned = sem("b_x_turned")
        hi_done = sem("b_hi_done")
        lo_done = sem("b_lo_done")
        qk_done = sem("b_qk_done")
        relu_done = sem("b_relu_done")
        exp_done = sem("b_exp_done")
        phi_done = sem("b_phi_done")
        vg_done = sem("b_vg_done")
        vg_read = sem("b_vg_read")
        score_done = sem("b_score_done")
        masked = sem("b_masked")
        av_done = sem("b_av_done")
        den_steps = sem("b_den_steps")
        y_done = sem("b_y_done")
        gated = sem("b_gated")
        y_turned = sem("b_y_turned")
        yt_read = sem("b_yt_read")
        wo_done = sem("b_wo_done")
        res_done = sem("b_res_done")

        def pair_sums(j):
            return ps[:, 6 + j % 2, 0:NT * 2 * VW].rearrange("p (t h d) -> p t h d", t=NT, h=2)

        block = ctx.enter_context(nc.Block())

        @block.tensor
        def _(pe):
            def turn_x(b):
                pe.wait_ge(xn_done, b + 1)
                ge(pe, hi_done, b)
                ge(pe, lo_done, b)
                for fc in range(FC):
                    for t in range(NT):
                        mm = nc.tensor.transpose(ps[:, fc, t * P:(t + 1) * P],
                                                 xn[:, t, fc * P:(fc + 1) * P], ident[:])
                mm.then_inc(x_turned, 1)

            def projections(b):
                pe.wait_ge(hi_done, b + 1)
                pe.wait_ge(lo_done, b + 1)
                for k in range(2 * NP):
                    if k < 2:
                        ge(pe, vg_read, 2 * NT * b - 1 + k)
                        ge(pe, res_done, 2 * (b - 2) + k + 1)
                    else:
                        pe.wait_ge(phi_done, 2 * NP * b + k - 1)
                    for fc in range(FC):
                        cols = slice(k * P, (k + 1) * P)
                        mm = split_products(nc, ps[:, 2 + k % 2, 0:T], wa_hi[:, fc, cols], wa_lo[:, fc, cols],
                                            x_hi[:, fc, 0:T], x_lo[:, fc, 0:T], fc == 0, fc == FC - 1)
                    mm.then_inc(qk_done, 1)
                for k in range(2 * NT):
                    if k < 2:
                        pe.wait_ge(phi_done, 2 * NP * b + 2 * NP - 1 + k)
                    else:
                        pe.wait_ge(vg_read, 2 * NT * b + k - 1)
                    t, gate = k % NT, k >= NT
                    cols = slice((3 if gate else 2) * DA, (4 if gate else 3) * DA)
                    for fc in range(FC):
                        rows = slice(t * P, (t + 1) * P)
                        mm = split_products(nc, ps[:, 2 + k % 2, :], x_hi[:, fc, rows], x_lo[:, fc, rows],
                                            wa_hi[:, fc, cols], wa_lo[:, fc, cols],
                                            fc == 0, fc == FC - 1 and not gate)
                    if gate:
                        mm = nc.tensor.matmul(ps[:, 2 + k % 2, :], g["ones64"][:], g["gb"][:],
                                              start=False, stop=True)
                    mm.then_inc(vg_done, 1)

            def scores(b, h):
                if h < 2:
                    ge(pe, yt_read, NP * b - 1 + h)
                else:
                    pe.wait_ge(masked, HA * b + h - 1)
                rows = slice(DK * (h % 2), DK * (h % 2) + DK)
                j, col = h // 2, 0
                for s in range(NT):
                    n = T - s * P
                    mm = nc.tensor.matmul(ps[:, 4 + h % 2, col:col + n],
                                          qk[rows, NP + j, s * P:(s + 1) * P],
                                          qk[rows, j, s * P:T], start=True, stop=True)
                    col += n
                mm.then_inc(score_done, 1)

            def values(b, h):
                pe.wait_ge(masked, HA * b + h + 1)
                j = h // 2
                if h % 2 == 0:
                    ge(pe, y_done, NP * b + j - 1)
                for t in range(NT):
                    col = (t * 2 + h % 2) * VW
                    m = ROWS[t]
                    for s in range(t + 1):
                        at = (0, T, T + T - P)[s] + (t - s) * P
                        kk = ROWS[s]
                        mm = nc.tensor.matmul(ps[0:m, 6 + j % 2, col:col + VW], a[0:kk, h % 2, at:at + m],
                                              v[0:kk, s, h, :], start=s == 0, stop=s == t)
                if h % 2:
                    mm.then_inc(av_done, 1)

            def attend(b):
                pe.wait_ge(phi_done, 2 * NP * (b + 1))
                pe.wait_ge(vg_read, 2 * NT * (b + 1))
                scores(b, 0)
                scores(b, 1)
                for h in range(HA):
                    values(b, h)
                    if h + 2 < HA:
                        scores(b, h + 2)

            def turn_y(b):
                for j in range(NP):
                    pe.wait_ge(gated, NP * b + j + 1)
                    if j >= 2:
                        pe.wait_ge(yt_read, NP * b + j - 1)
                    for t in range(NT):
                        m = ROWS[t]
                        mm = nc.tensor.transpose(ps[:, 4 + j % 2, t * P:t * P + m],
                                                 y[0:m, t, j * P:(j + 1) * P], ident[0:m, 0:m])
                    mm.then_inc(y_turned, 1)

            def output(b, last):
                pe.wait_ge(yt_read, NP * (b + 1))
                pe.wait_ge(vg_read, 2 * NT * (b + 1 + (not last)))
                for t in range(NT):
                    m = ROWS[t]
                    o = ps[0:m, 2 + t // 2, (t % 2) * D:(t % 2) * D + D]
                    for j in range(NP):
                        mm = nc.tensor.matmul(o, yt[:, j, t * P:t * P + m], wo[:, j, :],
                                              start=j == 0, stop=j == NP - 1)
                mm.then_inc(wo_done, 1)

            def step(b, s1, s2, s3):
                if s3:
                    if isinstance(b, int) and b == 0:
                        pe.wait_ge(filled, 3)
                    attend(b)
                if s2:
                    projections(b + 1)
                if s1:
                    turn_x(b + 2)
                if s3:
                    turn_y(b)
                    output(b, not s2)

            skewed(pe, step)

        @block.scalar
        def _(act):
            def evacuate(b):
                for k in range(2 * NP):
                    act.wait_ge(qk_done, 2 * NP * b + k + 1)
                    nc.scalar.activation(rl[:, k % 2, :], ps[:, 2 + k % 2, 0:T], ACT.Relu,
                                         scale=-1.0).then_inc(relu_done, 1)
                    act.wait_ge(relu_done, 2 * NP * b + k + 1)
                    ge(act, phi_done, 2 * NP * b + k - 1)
                    nc.scalar.activation(ex[:, k % 2, :], rl[:, k % 2, :], ACT.Exp,
                                         scale=-1.0).then_inc(exp_done, 1)
                for k in range(2 * NT):
                    act.wait_ge(vg_done, 2 * NT * b + k + 1)
                    if k < NT:
                        nc.scalar.copy(v[:, k, :, 0:DK],
                                       ps[:, 2 + k % 2, :].rearrange("p (h d) -> p h d", h=HA)
                                       ).then_inc(vg_read, 1)
                    else:
                        if k == NT:
                            ge(act, gated, NP * b)
                        nc.scalar.activation(sg[:, k - NT, :], ps[:, 2 + k % 2, :],
                                             ACT.Sigmoid).then_inc(vg_read, 1)

            def split_x(b):
                act.wait_ge(x_turned, b + 1)
                ge(act, vg_done, 2 * NT * b)
                nc.scalar.copy(x_hi[:], ps[:, 0:2, 0:TP]).then_inc(hi_done, 1)

            def copy_y(b):
                for j in range(NP):
                    act.wait_ge(y_turned, NP * b + j + 1)
                    if j == 0:
                        ge(act, wo_done, b)
                    nc.scalar.copy(yt[:, j, :], ps[:, 4 + j % 2, 0:T]).then_inc(yt_read, 1)

            def step(b, s1, s2, s3):
                if s2:
                    evacuate(b + 1)
                if s1:
                    split_x(b + 2)
                if s3:
                    copy_y(b)

            skewed(act, step)

        @block.vector
        def _(dve):
            nc.vector.memset(v[:, :, :, DK:VW], 1.0).then_inc(filled, 1)
            nc.vector.memset(qk[:, :, T:TP], 0.0).then_inc(filled, 1)
            for k in (6, 7):
                ms = nc.vector.memset(ps[:, k, 2 * 2 * VW:NT * 2 * VW], 0.0)
            ms.then_inc(filled, 1)

            def norm(b):
                step = Steps(dve, ln_steps, 2 * b)
                norm_stats(nc, dve, step, lambda t: res(g, b, t), stats, mv, ve, tick, var_done)
                dve.wait_ge(rstd_done, b + 1)
                ge(dve, x_turned, b)
                for t in range(NT):
                    last = nc.vector.tensor_scalar(xn[:, t, :], res(g, b, t), mv[:, t, 0:1], rstd[:, t, :],
                                                   ALU.subtract, ALU.mult)
                last.then_inc(xn_done, 1)

            def sums(b, j):
                step = Steps(dve, den_steps, 2 * (NP * b + j))
                dve.wait_ge(av_done, NP * b + j + 1)
                step(nc.vector.tensor_scalar(dn[:], pair_sums(j)[:, :, :, DK:VW], ATT_EPS, None, ALU.add))
                step(nc.vector.reciprocal(rd[:], dn[:]))
                if j == 0:
                    ge(dve, y_turned, NP * b)
                nc.vector.tensor_tensor(y[:, :, j * P:(j + 1) * P].rearrange("p t (h d) -> p t h d", h=2),
                                        pair_sums(j)[:, :, :, 0:DK], rd[:].to_broadcast([P, NT, 2, DK]),
                                        ALU.mult).then_inc(y_done, 1)

            def decay(b):
                for h in range(HA):
                    dve.wait_ge(score_done, HA * b + h + 1)
                    ge(dve, av_done, NP * b + h // 2)
                    nc.vector.tensor_tensor(a[:, h % 2, :], ps[:, 4 + h % 2, 0:AW], g["decay"][:, h, :],
                                            ALU.mult).then_inc(masked, 1)
                    if h % 2 and h > 1:
                        sums(b, h // 2 - 1)
                sums(b, NP - 1)

            def phi(b):
                for k in range(2 * NP):
                    dve.wait_ge(exp_done, 2 * NP * b + k + 1)
                    if k == 0:
                        ge(dve, score_done, HA * b)
                    nc.vector.scalar_tensor_tensor(out=qk[:, k, 0:T], in0=ps[:, 2 + k % 2, 0:T], scalar=0.0,
                                                   in1=ex[:, k % 2, :], op0=ALU.max,
                                                   op1=ALU.add).then_inc(phi_done, 1)

            def split_x(b):
                dve.wait_ge(hi_done, b + 1)
                nc.vector.tensor_tensor(x_lo[:], ps[:, 0:2, 0:TP], x_hi[:].bitcast(F32),
                                        ALU.subtract).then_inc(lo_done, 1)

            def residual(b):
                dve.wait_ge(wo_done, b + 1)
                for t in range(NT):
                    m = ROWS[t]
                    r = res(g, b, t)[0:m]
                    ins = nc.vector.tensor_tensor(r, ps[0:m, 2 + t // 2, (t % 2) * D:(t % 2) * D + D], r, ALU.add)
                    if t:
                        ins.then_inc(res_done, 1)

            def step(b, s1, s2, s3):
                if s1:
                    norm(b + 2)
                if s3:
                    decay(b)
                if s2:
                    phi(b + 1)
                if s1:
                    split_x(b + 2)
                if s3:
                    residual(b)

            skewed(dve, step)

        @block.gpsimd
        def _(pool):
            def step(b, s1, s2, s3):
                if s1:
                    pool.wait_ge(var_done, b + 3)
                    nc.gpsimd.tensor_tensor(rstd[:], ve[:], g["mhalf"][:, 0:NT].rearrange("p (t a) -> p t a", a=1),
                                            ALU.pow).then_inc(rstd_done, 1)
                if s3:
                    for j in range(NP):
                        pool.wait_ge(y_done, NP * b + j + 1)
                        yj = y[:, :, j * P:(j + 1) * P]
                        nc.gpsimd.tensor_tensor(yj, yj, sg[:, :, j * P:(j + 1) * P], ALU.mult).then_inc(gated, 1)

            skewed(pool, step)


def feed_forward(nc, g, ins):
    with ExitStack() as ctx:
        def sb(name, shape, dt=F32):
            return ctx.enter_context(nc.sbuf_tensor(name, shape, dt))

        def sem(name):
            return ctx.enter_context(nc.semaphore(name))

        ps, hres, ident = g["ps"], g["hres"], g["ident"]
        x3 = g["x3"]
        hraw = sb("c_hraw", [P, FC, D])
        had = sb("c_had", [P, FC, D], F32R)
        wf = sb("c_wf", [P, FC, D])
        wabs = sb("c_wabs", [P, FC])
        wsc = sb("c_wsc", [P, FC])
        wlim = sb("c_wlim", [P, FC, 2])
        tneg = sb("c_tneg", [P, FC, D])
        tern = sb("c_tern", [P, FC, D], BF16)
        tern_t = sb("c_tern_t", [P, FC, D], BF16)
        diag = sb("c_diag", [P, FC, P])
        ones = sb("c_ones", [P, P])
        identb = sb("c_identb", [P, P], BF16)
        wrow = sb("c_wrow", [P, D])
        wq1 = sb("c_wq1", [P, FC, D])
        w1c = sb("c_w1c", [P, FC])
        w1b = sb("c_w1b", [P, FC, P])
        ub = sb("c_ub", [P, D])
        roundc = sb("c_roundc", [P, 1])
        stats = sb("c_stats", [P, NT, 6])
        mv = sb("c_mv", [P, NT, 2])
        ve = sb("c_ve", [P, NT, 1])
        rstd = sb("c_rstd", [P, NT, 1])
        stats3 = sb("c_stats3", [P, NT, 6])
        mv3 = sb("c_mv3", [P, NT, 2])
        ve3 = sb("c_ve3", [P, NT, 1])
        rstd3 = sb("c_rstd3", [P, NT, 1])
        tick = sb("c_tick", [P, 1])
        xn = sb("c_xn", [P, NT, D])
        x_hi = sb("c_x_hi", [P, FC, TP], F32R)
        x_lo = sb("c_x_lo", [P, FC, TP], F32R)
        am = sb("c_am", [P, NT])
        xsc = sb("c_xsc", [P, NT])
        xinv = sb("c_xinv", [P, NT])
        qm = sb("c_qm", [P, NT, D])
        qi = sb("c_qi", [P, NT, D], BF16)
        q_t = sb("c_q_t", [P, FC, TP], BF16)
        fo = sb("c_fo", [P, NT, D])
        x3s = sb("c_x3s", [P, NT, D])
        junk = sb("c_junk", [P, NT, D])
        ags = sb("c_ags", [P, NT])

        w_in = sem("c_w_in")
        prep = sem("c_prep")
        pool_prep = sem("c_pool_prep")
        tern_ready = sem("c_tern_ready")
        tern_turned = sem("c_tern_turned")
        rows_done = sem("c_rows_done")
        rows_read = sem("c_rows_read")
        ternt_ready = sem("c_ternt_ready")
        ln_steps = sem("c_ln_steps")
        var_done = sem("c_var_done")
        rstd_done = sem("c_rstd_done")
        xn_done = sem("c_xn_done")
        x_turned = sem("c_x_turned")
        hi_done = sem("c_hi_done")
        lo_done = sem("c_lo_done")
        had_done = sem("c_had_done")
        q_steps = sem("c_q_steps")
        scaled = sem("c_scaled")
        inv_done = sem("c_inv_done")
        q_done = sem("c_q_done")
        q_turned = sem("c_q_turned")
        qt_done = sem("c_qt_done")
        ff_done = sem("c_ff_done")
        fo_done = sem("c_fo_done")
        fw_done = sem("c_fw_done")
        h2_done = sem("c_h2_done")
        ln3_steps = sem("c_ln3_steps")
        var3_done = sem("c_var3_done")
        rstd3_done = sem("c_rstd3_done")
        x3_done = sem("c_x3_done")
        ag_done = sem("c_ag_done")
        asum_done = sem("c_asum_done")
        acol_done = sem("c_acol_done")
        w_split = sem("c_w_split")

        def tiles(k):
            return ps[:, k:k + 2, :].rearrange("p k c -> p (k c)")[:, 0:NT * D].rearrange(
                "p (t f) -> p t f", t=NT)

        q_turn = ps[:, 4, :].bitcast(BF16)

        block = ctx.enter_context(nc.Block())

        @block.sync
        def _(sp):
            for n, t in (("hadamard", hraw), ("ffn_w", wf), ("Wq1", wq1)):
                sp.dma_start(t[:], ins[n].rearrange("(c p) n -> p c n", p=P)).then_inc(w_in, 16)
            for c in range(FC):
                sp.dma_start(w1c[:, c:c + 1], ins["w_conv1"].rearrange("(c p a) -> c p a", p=P, a=1)[c]
                             ).then_inc(w_in, 16)
            for n, t in (("Wk1_t", g["wk_t"]), ("Wv1", g["wv"]), ("Wv1_t", g["wv_t"]), ("gate_t", g["gate"])):
                sp.dma_start(t[:], ins[n].rearrange("(c p) n -> p c n", p=P)).then_inc(w_in, 16)
            sp.wait_ge(w_in, 16 * (7 + FC))

        @block.tensor
        def _(pe):
            pe.wait_ge(tern_ready, 1)
            for ic in range(FC):
                for oc in range(FC):
                    mm = nc.tensor.transpose(q_turn[:, ic * D + oc * P:ic * D + oc * P + P],
                                             tern[:, oc, ic * P:(ic + 1) * P], identb[:])
            mm.then_inc(tern_turned, 1)
            pe.wait_ge(pool_prep, 3)
            for oc in range(FC):
                nc.tensor.matmul(ps[:, 7, oc * P:(oc + 1) * P], ones[:], diag[:, oc, :], start=True, stop=True)
            for c in range(FC):
                mm = nc.tensor.matmul(ps[:, 6, 0:D], w1b[:, c, :], wq1[:, c, :], start=c == 0, stop=c == FC - 1)
            mm.then_inc(rows_done, 1)
            pe.wait_ge(rows_read, 2)

            def turn_x(b):
                pe.wait_ge(xn_done, b + 1)
                ge(pe, hi_done, b)
                ge(pe, lo_done, b)
                for fc in range(FC):
                    for t in range(NT):
                        mm = nc.tensor.transpose(ps[:, fc, t * P:(t + 1) * P],
                                                 xn[:, t, fc * P:(fc + 1) * P], ident[:])
                mm.then_inc(x_turned, 1)

            def rotate(b):
                pe.wait_ge(hi_done, b + 1)
                pe.wait_ge(lo_done, b + 1)
                ge(pe, q_done, b)
                for t in range(NT):
                    for fc in range(FC):
                        for n, x in enumerate((x_hi, x_lo)):
                            mm = nc.tensor.matmul(tiles(2)[:, t, :], x[:, fc, t * P:(t + 1) * P], had[:, fc, :],
                                                  start=fc + n == 0, stop=fc + n == 2)
                mm.then_inc(had_done, 1)

            def turn_q(b):
                pe.wait_ge(q_done, b + 1)
                ge(pe, qt_done, b)
                for fc in range(FC):
                    for t in range(NT):
                        mm = nc.tensor.transpose(q_turn[:, fc * TP + t * P:fc * TP + (t + 1) * P],
                                                 qi[:, t, fc * P:(fc + 1) * P], identb[:])
                mm.then_inc(q_turned, 1)

            def ternary(b):
                pe.wait_ge(qt_done, b + 1)
                ge(pe, fo_done, b)
                for t in range(NT):
                    for fc in range(FC):
                        mm = nc.tensor.matmul(tiles(5)[:, t, :], q_t[:, fc, t * P:(t + 1) * P], tern_t[:, fc, :],
                                              start=fc == 0, stop=fc == FC - 1)
                mm.then_inc(ff_done, 1)

            def agent_sums(b):
                pe.wait_ge(ag_done, b + 1)
                ge(pe, acol_done, b)
                for ic in range(FC):
                    for t in range(NT):
                        m = ROWS[t]
                        mm = nc.tensor.matmul(ps[:, 7, ic:ic + 1], x3s[0:m, t, ic * P:(ic + 1) * P],
                                              ags[0:m, t:t + 1], start=t == 0, stop=t == NT - 1)
                mm.then_inc(asum_done, 1)

            def step(b, s1, s2, s3):
                if s2:
                    if isinstance(b, int) and b == -1:
                        pe.wait_ge(ternt_ready, 1)
                    rotate(b + 1)
                if s1:
                    turn_x(b + 2)
                if s2:
                    turn_q(b + 1)
                    ternary(b + 1)
                if s3:
                    agent_sums(b)

            skewed(pe, step)

        @block.scalar
        def _(act):
            act.wait_ge(tern_turned, 1)
            nc.scalar.copy(tern_t[:], q_turn[:, 0:FC * D].rearrange("p (c f) -> p c f", c=FC)).then_inc(ternt_ready, 1)
            act.wait_ge(rows_done, 1)
            nc.scalar.copy(wrow[:], ps[:, 7, 0:D]).then_inc(rows_read, 1)
            nc.scalar.copy(ub[:], ps[:, 6, 0:D]).then_inc(rows_read, 1)
            act.wait_ge(prep, 1)

            def step(b, s1, s2, s3):
                if s2:
                    act.wait_ge(inv_done, b + 2)
                    for t in range(NT):
                        last = nc.scalar.activation(qm[:, t, :], tiles(2)[:, t, :], ACT.Identity,
                                                    bias=roundc[:], scale=xinv[:, t:t + 1])
                    last.then_inc(scaled, 1)
                if s1:
                    act.wait_ge(x_turned, b + 3)
                    ge(act, had_done, b + 2)
                    nc.scalar.copy(x_hi[:], ps[:, 0:2, 0:TP]).then_inc(hi_done, 1)
                if s2:
                    act.wait_ge(q_turned, b + 2)
                    ge(act, ff_done, b + 1)
                    nc.scalar.copy(q_t[:], q_turn[:, 0:FC * TP].rearrange("p (c f) -> p c f", c=FC)
                                   ).then_inc(qt_done, 1)
                    act.wait_ge(ff_done, b + 2)
                    ge(act, h2_done, b + 1)
                    for t in range(NT):
                        last = nc.scalar.mul(fo[:, t, :], tiles(5)[:, t, :], xsc[:, t:t + 1])
                    last.then_inc(fo_done, 1)

            skewed(act, step)

        @block.vector
        def _(dve):
            dve.wait_ge(w_in, 16 * (7 + FC))
            dve.wait_ge(pool_prep, 1)
            nc.vector.memset(roundc[:], ROUND).then_inc(prep, 1)
            step = Steps(dve, prep, 1)
            nc.vector.tensor_copy(had[:], hraw[:])
            nc.vector.tensor_copy(identb[:], ident[:])
            step(nc.vector.tensor_reduce(wabs[:], wf[:], AX.X, ALU.add, apply_absolute_value=True))
            step(nc.vector.tensor_scalar(wsc[:], wabs[:], 1.0 / D, 1e-5, ALU.mult, ALU.max))
            for s, f in enumerate((0.5, -0.5)):
                last = nc.vector.tensor_scalar(wlim[:, :, s], wsc[:], f, None, ALU.mult)
            step(last)
            for c in range(FC):
                last = nc.vector.tensor_scalar(tneg[:, c, :], wf[:, c, :], wlim[:, c, 1:2], None, ALU.is_lt)
            step(last)
            for c in range(FC):
                last = nc.vector.scalar_tensor_tensor(out=tern[:, c, :], in0=wf[:, c, :], scalar=wlim[:, c, 0:1],
                                                      in1=tneg[:, c, :], op0=ALU.is_gt, op1=ALU.subtract)
            last.then_inc(tern_ready, 1)
            for c in range(FC):
                nc.vector.tensor_scalar(diag[:, c, :], ident[:], wsc[:, c:c + 1], None, ALU.mult)
                last = nc.vector.tensor_scalar(w1b[:, c, :], ones[:], w1c[:, c:c + 1], None, ALU.mult)
                last.then_inc(pool_prep, 1)
            dve.wait_ge(rows_read, 2)

            def norm(b):
                step = Steps(dve, ln_steps, 2 * b)
                norm_stats(nc, dve, step, lambda t: res(g, b, t), stats, mv, ve, tick, var_done)
                dve.wait_ge(rstd_done, b + 1)
                ge(dve, x_turned, b)
                for t in range(NT):
                    last = nc.vector.tensor_scalar(xn[:, t, :], res(g, b, t), mv[:, t, 0:1], rstd[:, t, :],
                                                   ALU.subtract, ALU.mult)
                last.then_inc(xn_done, 1)

            def split_x(b):
                dve.wait_ge(hi_done, b + 1)
                nc.vector.tensor_tensor(x_lo[:], ps[:, 0:2, 0:TP], x_hi[:].bitcast(F32),
                                        ALU.subtract).then_inc(lo_done, 1)

            def scale(b):
                step = Steps(dve, q_steps, 3 * b)
                dve.wait_ge(had_done, b + 1)
                step(nc.vector.tensor_reduce(am[:], tiles(2), AX.X, ALU.max, apply_absolute_value=True))
                ge(dve, fo_done, b)
                step(nc.vector.tensor_scalar(xsc[:], am[:], 1e-5, 1.0 / ACT_POS, ALU.max, ALU.mult))
                nc.vector.reciprocal(xinv[:], xsc[:]).then_inc(inv_done, 1)

            def quantise(b):
                step = Steps(dve, q_steps, 3 * b + 2)
                dve.wait_ge(scaled, b + 1)
                step(nc.vector.tensor_scalar(qm[:], qm[:], ROUND + ACT_POS, ROUND - ACT_NEG, ALU.min, ALU.max))
                nc.vector.tensor_scalar(qi[:], qm[:], ROUND, None, ALU.subtract).then_inc(q_done, 1)

            def add(b):
                dve.wait_ge(fw_done, b + 1)
                r = hres[:, NT * b:NT * b + NT, :] if isinstance(b, int) else hres[:, bass.ds(b * NT, NT), :]
                nc.vector.tensor_tensor(r, r, fo[:], ALU.add).then_inc(h2_done, 1)

            def agents(b):
                step = Steps(dve, ln3_steps, 2 * b)
                dve.wait_ge(h2_done, b + 1)
                norm_stats(nc, dve, step, lambda t: res(g, b, t), stats3, mv3, ve3, tick, var3_done)
                dve.wait_ge(rstd3_done, b + 1)
                ge(dve, asum_done, b)
                for t in range(NT):
                    last = nc.vector.tensor_scalar(x3s[:, t, :], res(g, b, t), mv3[:, t, 0:1], rstd3[:, t, :],
                                                   ALU.subtract, ALU.mult)
                last.then_inc(x3_done, 1)
                dve.wait_ge(x3_done, b + 1)
                for t in range(NT):
                    last = nc.vector.tensor_tensor_reduce(junk[:, t, :], x3s[:, t, :], ub[:], 1.0, 0.0, ALU.mult,
                                                          ALU.add, ags[:, t:t + 1])
                last.then_inc(ag_done, 1)
                all3 = x3[:, NT * b:NT * b + NT, :] if isinstance(b, int) else x3[:, bass.ds(b * NT, NT), :]
                nc.vector.tensor_copy(all3, x3s[:])
                dve.wait_ge(ag_done, b + 1)
                a3 = g["ag"][:, NT * b:NT * b + NT] if isinstance(b, int) else g["ag"][:, bass.ds(b * NT, NT)]
                nc.vector.tensor_copy(a3, ags[:])
                dve.wait_ge(asum_done, b + 1)
                ac = g["acol"][:, b, :] if isinstance(b, int) else g["acol"][:, bass.ds(b, 1), :].rearrange(
                    "p a c -> p (a c)")
                nc.vector.tensor_scalar(ac, ps[:, 7, 0:FC], float(D) ** -0.5, None,
                                        ALU.mult).then_inc(acol_done, 1)

            def step(b, s1, s2, s3):
                if s2:
                    scale(b + 1)
                if s1:
                    norm(b + 2)
                if s2:
                    quantise(b + 1)
                if s1:
                    split_x(b + 2)
                if s3:
                    agents(b)
                if s2:
                    add(b + 1)

            skewed(dve, step)

        @block.gpsimd
        def _(pool):
            nc.gpsimd.memset(ones[:], 1.0).then_inc(pool_prep, 1)
            w1 = g["w1raw"]

            def step(b, s1, s2, s3):
                mh = g["mhalf"][:, 0:NT].rearrange("p (t a) -> p t a", a=1)
                if s1:
                    pool.wait_ge(var_done, b + 3)
                    nc.gpsimd.tensor_tensor(rstd[:], ve[:], mh, ALU.pow).then_inc(rstd_done, 1)
                if s3:
                    pool.wait_ge(var3_done, b + 1)
                    nc.gpsimd.tensor_tensor(rstd3[:], ve3[:], mh, ALU.pow).then_inc(rstd3_done, 1)
                if s2:
                    pool.wait_ge(fo_done, b + 2)
                    wr = wrow[:].rearrange("p (a f) -> p a f", a=1).to_broadcast([P, NT, D])
                    nc.gpsimd.tensor_tensor(fo[:], fo[:], wr, ALU.mult).then_inc(fw_done, 1)

            skewed(pool, step)
            for c in range(FC):
                for k in range(NJ // 2):
                    cols = slice(k * 4 * HE, (k + 1) * 4 * HE)
                    n = 2 * (c * (NJ // 2) + k)
                    nc.gpsimd.tensor_copy(g["w1_hi"][:, c, cols], w1[:, c, cols]).then_inc(w_split, 1)
                    pool.wait_ge(w_split, n + 1)
                    nc.gpsimd.tensor_tensor(g["w1_lo"][:, c, cols], w1[:, c, cols],
                                            g["w1_hi"][:, c, cols].bitcast(F32), ALU.subtract).then_inc(w_split, 1)


def agent_attention(nc, g):
    with ExitStack() as ctx:
        def sb(name, shape, dt=F32):
            return ctx.enter_context(nc.sbuf_tensor(name, shape, dt))

        def sem(name):
            return ctx.enter_context(nc.semaphore(name))

        ps, hres, ident, x3 = g["ps"], g["hres"], g["ident"], g["x3"]
        sel = sb("e_sel", [B, B, P])
        mx = sb("e_mx", [B, 2])
        ex = sb("e_ex", [B, D])
        su = sb("e_su", [B, 2])
        rs = sb("e_rs", [B, 2])
        attn_t = sb("e_attn_t", [P, FC, B])
        w8 = sb("e_w8", [B, D])
        junk = sb("e_junk", [P, 4, D])
        score = sb("e_score", [P, B, NT])
        pr = sb("e_pr", [B, T])
        pt = sb("e_pt", [P, NT, B])
        px = sb("e_px", [P, FC, B])
        av = sb("e_av", [B, D])
        zero = sb("e_zero", [P, NT * B])
        tok = sb("e_tok", [P, NT * B])
        rtok = sb("e_rtok", [P, NT * B])
        sel_ready = sem("e_sel_ready")
        pe_done = sem("e_pe_done")
        act_done = sem("e_act_done")
        dve_done = sem("e_dve_done")
        scored = sem("e_scored")
        block = ctx.enter_context(nc.Block())

        @block.gpsimd
        def _(pool):
            nc.gpsimd.memset(sel[:], 0.0).then_inc(sel_ready, 1)
            pool.wait_ge(sel_ready, 1)
            nc.gpsimd.affine_select(out=sel[:], in_=sel[:], compare_op=ALU.not_equal, fill=1.0, base=0,
                                    pattern=[[-1, B], [0, P]], channel_multiplier=1).then_inc(sel_ready, 1)

        def spread(row):
            for b in range(B):
                mm = nc.tensor.matmul(ps[:, b // 2, (b % 2) * D:(b % 2) * D + D], sel[:, b, :], row[:],
                                      start=True, stop=True)
            return mm

        @block.tensor
        def _(pe):
            for c in range(FC):
                mm = nc.tensor.matmul(ps[0:B, 4, 0:D], g["acol"][:, :, c], g["wk_t"][:, c, :],
                                      start=c == 0, stop=c == FC - 1)
            mm.then_inc(pe_done, 1)
            pe.wait_ge(act_done, 1)
            for c in range(FC):
                mm = nc.tensor.transpose(ps[:, 5, c * B:(c + 1) * B], ex[:, c * P:(c + 1) * P], ident[0:B, 0:B])
            mm.then_inc(pe_done, 1)
            pe.wait_ge(dve_done, 3)
            for c in range(FC):
                mm = nc.tensor.matmul(ps[0:B, 6, 0:D], attn_t[:, c, :], g["wv"][:, c, :],
                                      start=c == 0, stop=c == FC - 1)
            mm.then_inc(pe_done, 1)
            pe.wait_ge(dve_done, 4)
            pe.wait_ge(sel_ready, 2)
            spread(w8).then_inc(pe_done, 1)
            pe.wait_ge(scored, NT * B)
            for t in range(NT):
                m = ROWS[t]
                mm = nc.tensor.transpose(ps[0:B, 7, t * P:t * P + m], score[0:m, :, t], ident[0:m, 0:m])
            mm.then_inc(pe_done, 1)
            pe.wait_ge(act_done, 2)
            for t in range(NT):
                m = ROWS[t]
                mm = nc.tensor.transpose(ps[0:m, 4, t * B:(t + 1) * B], pr[:, t * P:t * P + m], ident[0:B, 0:B])
            mm.then_inc(pe_done, 1)
            pe.wait_ge(dve_done, 7)
            for b in range(B):
                for c in range(FC):
                    for t in range(NT):
                        m = ROWS[t]
                        mm = nc.tensor.matmul(ps[:, 5, c * B + b:c * B + b + 1],
                                              x3[0:m, NT * b + t, c * P:(c + 1) * P], pt[0:m, t, b:b + 1],
                                              start=t == 0, stop=t == NT - 1)
            mm.then_inc(pe_done, 1)
            pe.wait_ge(dve_done, 8)
            for c in range(FC):
                mm = nc.tensor.matmul(ps[0:B, 6, 0:D], px[:, c, :], g["wv_t"][:, c, :],
                                      start=c == 0, stop=c == FC - 1)
            mm.then_inc(pe_done, 1)
            pe.wait_ge(dve_done, 9)
            spread(av).then_inc(pe_done, 1)

        @block.scalar
        def _(act):
            act.wait_ge(dve_done, 1)
            nc.scalar.activation(ex[:], ps[0:B, 4, 0:D], ACT.Exp, bias=mx[:, 0:1],
                                 accum_out=su[:, 0:1]).then_inc(act_done, 1)
            act.wait_ge(dve_done, 5)
            nc.scalar.activation(pr[:], ps[0:B, 7, 0:T], ACT.Exp, bias=mx[:, 1:2],
                                 accum_out=su[:, 1:2]).then_inc(act_done, 1)
            act.wait_ge(scored, NT * B + 1)
            nc.scalar.activation(tok[:], zero[:], ACT.Exp).then_inc(act_done, 1)

        @block.vector
        def _(dve):
            dve.wait_ge(pe_done, 1)
            nc.vector.tensor_reduce(mx[:, 0:1], ps[0:B, 4, 0:D], AX.X, ALU.max, negate=True).then_inc(dve_done, 1)
            dve.wait_ge(act_done, 1)
            nc.vector.reciprocal(rs[:, 0:1], su[:, 0:1]).then_inc(dve_done, 1)
            dve.wait_ge(pe_done, 2)
            nc.vector.tensor_copy(attn_t[:].rearrange("p c b -> p (c b)"), ps[:, 5, 0:FC * B]).then_inc(dve_done, 1)
            dve.wait_ge(pe_done, 3)
            dve.wait_ge(dve_done, 2)
            nc.vector.tensor_scalar(w8[:], ps[0:B, 6, 0:D], rs[:, 0:1], None, ALU.mult).then_inc(dve_done, 1)
            dve.wait_ge(pe_done, 4)
            for b in range(B):
                for t in range(NT):
                    i = NT * b + t
                    if i >= 4:
                        dve.wait_ge(scored, i - 3)
                    nc.vector.tensor_tensor_reduce(junk[:, i % 4, :], x3[:, i, :],
                                                   ps[:, b // 2, (b % 2) * D:(b % 2) * D + D], 1.0, 0.0,
                                                   ALU.mult, ALU.add, score[:, b, t:t + 1]).then_inc(scored, 1)
            nc.vector.tensor_tensor(zero[:], g["ag"][:], g["ag"][:], ALU.subtract).then_inc(scored, 1)
            dve.wait_ge(pe_done, 5)
            nc.vector.tensor_reduce(mx[:, 1:2], ps[0:B, 7, 0:T], AX.X, ALU.max, negate=True).then_inc(dve_done, 1)
            dve.wait_ge(act_done, 2)
            nc.vector.reciprocal(rs[:, 1:2], su[:, 1:2]).then_inc(dve_done, 1)
            dve.wait_ge(pe_done, 6)
            for t in range(NT):
                m = ROWS[t]
                last = nc.vector.tensor_copy(pt[0:m, t, :], ps[0:m, 4, t * B:(t + 1) * B])
            last.then_inc(dve_done, 1)
            dve.wait_ge(pe_done, 7)
            nc.vector.tensor_copy(px[:].rearrange("p c b -> p (c b)"), ps[:, 5, 0:FC * B]).then_inc(dve_done, 1)
            dve.wait_ge(pe_done, 8)
            dve.wait_ge(dve_done, 6)
            nc.vector.tensor_scalar(av[:], ps[0:B, 6, 0:D], rs[:, 1:2], None, ALU.mult).then_inc(dve_done, 1)
            dve.wait_ge(act_done, 3)
            nc.vector.reciprocal(rtok[:], tok[:]).then_inc(dve_done, 1)
            dve.wait_ge(dve_done, 10)
            nc.vector.tensor_tensor(tok[:], tok[:], rtok[:], ALU.mult).then_inc(dve_done, 1)
            dve.wait_ge(dve_done, 11)
            dve.wait_ge(pe_done, 9)
            for b in range(B):
                for t in range(NT):
                    i = NT * b + t
                    m = ROWS[t]
                    nc.vector.scalar_tensor_tensor(out=hres[0:m, i, :],
                                                   in0=ps[0:m, b // 2, (b % 2) * D:(b % 2) * D + D],
                                                   scalar=tok[0:m, i:i + 1], in1=hres[0:m, i, :],
                                                   op0=ALU.mult, op1=ALU.add)


def phase_cd(nc, g, ins, out):
    with ExitStack() as ctx:
        def sb(name, shape, dt=F32):
            return ctx.enter_context(nc.sbuf_tensor(name, shape, dt))

        g["w1_hi"] = sb("w1_hi", [P, FC, NJ * 2 * HE], F32R)
        g["w1_lo"] = sb("w1_lo", [P, FC, NJ * 2 * HE], F32R)
        g["gate"] = sb("gate", [P, FC, E])
        with ExitStack() as agent:
            def sba(name, shape, dt=F32):
                return agent.enter_context(nc.sbuf_tensor(name, shape, dt))

            g["x3"] = sba("x3", [P, NT * B, D])
            g["ag"] = sba("ag", [P, NT * B])
            g["acol"] = sba("acol", [P, B, FC])
            g["wk_t"] = sba("wk_t", [P, FC, D])
            g["wv"] = sba("wv", [P, FC, D])
            g["wv_t"] = sba("wv_t", [P, FC, D])
            feed_forward(nc, g, ins)
            agent_attention(nc, g)
        experts(nc, g, out)


def top_two(nc, step, score, bufs, w):
    n = score.shape[1]
    mx, ex, p, c, one, two, rank = bufs

    def over(t):
        return t[:].to_broadcast([P, n, E])

    step(nc.vector.tensor_reduce(mx[:, :, 0], score, AX.X, ALU.max))
    step(nc.vector.tensor_tensor(ex[:], score, over(mx), ALU.subtract))
    yield
    step(nc.vector.tensor_reduce(mx[:, :, 0], p[:], AX.X, ALU.add))
    step(nc.vector.reciprocal(mx[:, :, 0], mx[:, :, 0]))
    step(nc.vector.tensor_tensor(p[:], p[:], over(mx), ALU.mult))
    for k, pick in enumerate((one, two)):
        step(nc.vector.tensor_reduce(mx[:, :, 0], p[:] if k == 0 else ex[:], AX.X, ALU.max))
        step(nc.vector.tensor_tensor(c[:], p[:] if k == 0 else ex[:], over(mx), ALU.is_equal))
        step(nc.vector.tensor_tensor(c[:], c[:], rank[:], ALU.mult))
        step(nc.vector.tensor_reduce(mx[:, :, 0], c[:], AX.X, ALU.max))
        step(nc.vector.tensor_tensor(pick[:], c[:], over(mx), ALU.is_equal))
        if k == 0:
            step(nc.vector.scalar_tensor_tensor(out=ex[:], in0=one[:], scalar=-2.0, in1=p[:],
                                                op0=ALU.mult, op1=ALU.add))
    step(nc.vector.tensor_tensor(c[:], one[:], two[:], ALU.add))
    step(nc.vector.tensor_tensor(w, p[:], c[:], ALU.mult))


ROUTE_STEPS = 18


def experts(nc, g, out):
    with ExitStack() as ctx:
        def sb(name, shape, dt=F32):
            return ctx.enter_context(nc.sbuf_tensor(name, shape, dt))

        def sem(name):
            return ctx.enter_context(nc.semaphore(name))

        ps, hres, ident = g["ps"], g["hres"], g["ident"]
        w1_hi, w1_lo, w2 = g["w1_hi"], g["w1_lo"], g["w2"]
        stats = sb("d_stats", [P, NT, 6])
        mv = sb("d_mv", [P, NT, 2])
        ve = sb("d_ve", [P, NT, 1])
        rstd = sb("d_rstd", [P, NT, 1])
        tick = sb("d_tick", [P, 1])
        xn = sb("d_xn", [P, NT, D])
        x_hi = sb("d_x_hi", [P, FC, TP], F32R)
        x_lo = sb("d_x_lo", [P, FC, TP], F32R)
        g_hi = sb("d_g_hi", [P, FC, E], F32R)
        g_lo = sb("d_g_lo", [P, FC, E], F32R)
        mx = sb("d_mx", [P, NT, 1])
        ex = sb("d_ex", [P, NT, E])
        pr = sb("d_pr", [P, NT, E])
        cc = sb("d_cc", [P, NT, E])
        one = sb("d_one", [P, NT, E])
        two = sb("d_two", [P, NT, E])
        rank = sb("d_rank", [P, NT, E])
        wt = sb("d_wt", [P, NT, NJ])
        si = sb("d_si", [P, 2, HE])
        hg = sb("d_hg", [P, 2, 2 * P])
        ht = sb("d_ht", [HE // 2, 2, 2, P])
        jobs = [(t, j) for t in range(NT) for j in range(NJ)]
        n = len(jobs)

        g_steps = sem("d_g_steps")
        rank_ready = sem("d_rank_ready")
        ln_steps = sem("d_ln_steps")
        var_done = sem("d_var_done")
        rstd_done = sem("d_rstd_done")
        xn_done = sem("d_xn_done")
        x_turned = sem("d_x_turned")
        hi_done = sem("d_hi_done")
        lo_done = sem("d_lo_done")
        score_done = sem("d_score_done")
        route_steps = sem("d_route_steps")
        exp_done = sem("d_exp_done")
        routed = sem("d_routed")
        h_done = sem("d_h_done")
        silu_done = sem("d_silu_done")
        hg_done = sem("d_hg_done")
        h_turned = sem("d_h_turned")
        ht_done = sem("d_ht_done")
        z_done = sem("d_z_done")
        z_read = sem("d_z_read")
        stored = sem("d_stored")

        block = ctx.enter_context(nc.Block())

        @block.sync
        def _(sp):
            def store(b):
                sp.wait_ge(z_read, NT * (b + 1))
                o = out[b] if isinstance(b, int) else out[bass.ds(b, 1)].rearrange("a t f -> (a t) f")
                for t in range(NT):
                    m = ROWS[t]
                    sp.dma_start(o[t * P:t * P + m, :], res(g, b, t)[0:m]).then_inc(stored, 16)

            store(0)
            with sp.Fori(1, B) as b:
                store(b)
            sp.wait_ge(stored, 16 * NT * B)

        @block.tensor
        def _(pe):
            pe.wait_ge(g_steps, 2)

            def prepare(b):
                pe.wait_ge(xn_done, b + 1)
                ge(pe, ht_done, n * b)
                for fc in range(FC):
                    for t in range(NT):
                        mm = nc.tensor.transpose(ps[:, fc, t * P:(t + 1) * P],
                                                 xn[:, t, fc * P:(fc + 1) * P], ident[:])
                mm.then_inc(x_turned, 1)
                pe.wait_ge(lo_done, b + 1)
                for t in range(NT):
                    for fc in range(FC):
                        rows = slice(t * P, (t + 1) * P)
                        mm = split_products(nc, ps[:, 2, t * E:(t + 1) * E], x_hi[:, fc, rows], x_lo[:, fc, rows],
                                            g_hi[:, fc, :], g_lo[:, fc, :], fc == 0, fc == FC - 1)
                mm.then_inc(score_done, 1)

            def hidden(b, i):
                t, j = jobs[i]
                ge(pe, hg_done, n * b + i - 1)
                for fc in range(FC):
                    rows = slice(t * P, (t + 1) * P)
                    cols = slice(j * 2 * HE, (j + 1) * 2 * HE)
                    mm = split_products(nc, ps[:, 3 + i % 2, 0:2 * HE], x_hi[:, fc, rows], x_lo[:, fc, rows],
                                        w1_hi[:, fc, cols], w1_lo[:, fc, cols], fc == 0, fc == FC - 1)
                mm.then_inc(h_done, 1)

            def turn(b, i):
                pe.wait_ge(hg_done, n * b + i + 1)
                ge(pe, ht_done, n * b + i - 1)
                for k in range(2):
                    mm = nc.tensor.transpose(ps[0:HE // 2, 5 * (i % 2), k * P:(k + 1) * P],
                                             hg[:, i % 2, k * P:k * P + HE // 2], ident[:])
                mm.then_inc(h_turned, 1)

            def second(b, i):
                t, j = jobs[i]
                pe.wait_ge(ht_done, n * b + i + 1)
                if j == 0:
                    ge(pe, z_read, NT * b + (0, -1, 1)[t])
                for k in range(2):
                    mm = nc.tensor.matmul(ps[:, 6 + t % 2, 0:D], ht[:, i % 2, k, :], w2[:, k, j, :],
                                          start=j + k == 0, stop=j == NJ - 1 and k == 1)
                mm.then_inc(z_done, 1)

            def step(b, s1, s2, s3):
                if s3:
                    for i in range(n + 2):
                        if i < n:
                            hidden(b, i)
                        if 1 <= i <= n:
                            turn(b, i - 1)
                        if i >= 2:
                            second(b, i - 2)
                if s2:
                    prepare(b + 1)

            skewed(pe, step)

        @block.scalar
        def _(act):
            def step(b, s1, s2, s3):
                if s3:
                    for i in range(n + 1):
                        if i < n:
                            act.wait_ge(h_done, n * b + i + 1)
                            nc.scalar.activation(si[:, i % 2, :], ps[:, 3 + i % 2, HE:2 * HE],
                                                 ACT.Silu).then_inc(silu_done, 1)
                        if i >= 1:
                            act.wait_ge(h_turned, n * b + i)
                            ge(act, z_done, n * b + i - 2)
                            k = (i - 1) % 2
                            nc.scalar.copy(ht[:, k].rearrange("p k m -> p (k m)"),
                                           ps[0:HE // 2, 5 * k, 0:2 * P]).then_inc(ht_done, 1)
                if s2:
                    act.wait_ge(x_turned, b + 2)
                    nc.scalar.copy(x_hi[:], ps[:, 0:2, 0:TP]).then_inc(hi_done, 1)
                    act.wait_ge(route_steps, ROUTE_STEPS * (b + 1) + 2)
                    nc.scalar.activation(pr[:], ex[:], ACT.Exp).then_inc(exp_done, 1)

            skewed(act, step)

        @block.vector
        def _(dve):
            nc.vector.tensor_copy(g_hi[:], g["gate"][:]).then_inc(g_steps, 1)
            nc.vector.memset(wt[:, :, E:NJ], 1.0)
            dve.wait_ge(g_steps, 1)
            nc.vector.tensor_tensor(g_lo[:], g["gate"][:], g_hi[:].bitcast(F32), ALU.subtract).then_inc(g_steps, 1)
            dve.wait_ge(rank_ready, 1)

            def prepare(b):
                step = Steps(dve, ln_steps, 2 * b)
                norm_stats(nc, dve, step, lambda t: res(g, b, t), stats, mv, ve, tick, var_done)
                dve.wait_ge(rstd_done, b + 1)
                for t in range(NT):
                    last = nc.vector.tensor_scalar(xn[:, t, :], res(g, b, t), mv[:, t, 0:1], rstd[:, t, :],
                                                   ALU.subtract, ALU.mult)
                last.then_inc(xn_done, 1)
                dve.wait_ge(hi_done, b + 1)
                nc.vector.tensor_tensor(x_lo[:], ps[:, 0:2, 0:TP], x_hi[:].bitcast(F32),
                                        ALU.subtract).then_inc(lo_done, 1)
                dve.wait_ge(score_done, b + 1)
                step = Steps(dve, route_steps, ROUTE_STEPS * b)
                score = ps[:, 2, 0:NT * E].rearrange("p (t e) -> p t e", t=NT)
                route = top_two(nc, step, score, (mx, ex, pr, cc, one, two, rank), wt[:, :, 0:E])
                next(route)
                dve.wait_ge(exp_done, b + 1)
                for _ in route:
                    pass

            def step(b, s1, s2, s3):
                if s3:
                    for i in range(n + 2):
                        if i < n:
                            t, j = jobs[i]
                            dve.wait_ge(silu_done, n * b + i + 1)
                            ge(dve, h_turned, n * b + i - 1)
                            nc.vector.scalar_tensor_tensor(
                                out=hg[:, i % 2, :].rearrange("p (k m) -> p k m", k=2)[:, :, 0:HE // 2],
                                in0=ps[:, 3 + i % 2, 0:HE].rearrange("p (k m) -> p k m", k=2),
                                scalar=wt[:, t, j:j + 1],
                                in1=si[:, i % 2, :].rearrange("p (k m) -> p k m", k=2),
                                op0=ALU.mult, op1=ALU.mult).then_inc(hg_done, 1)
                        if i >= 2 and jobs[i - 2][1] == NJ - 1:
                            t = jobs[i - 2][0]
                            m = ROWS[t]
                            dve.wait_ge(z_done, n * b + i - 1)
                            r = res(g, b, t)[0:m]
                            nc.vector.tensor_tensor(r, ps[0:m, 6 + t % 2, 0:D], r, ALU.add).then_inc(z_read, 1)
                if s2:
                    prepare(b + 1)

            skewed(dve, step)

        @block.gpsimd
        def _(pool):
            for e in range(E):
                ms = nc.gpsimd.memset(rank[:, :, e:e + 1], float(E - e))
            ms.then_inc(rank_ready, 1)

            def step(b, s1, s2, s3):
                if s2:
                    pool.wait_ge(var_done, b + 2)
                    nc.gpsimd.tensor_tensor(rstd[:], ve[:], g["mhalf"][:, 0:NT].rearrange("p (t a) -> p t a", a=1),
                                            ALU.pow).then_inc(rstd_done, 1)

            skewed(pool, step)





def build(nc, ins, out):
    with ExitStack() as ctx:
        def sb(name, shape, dt=F32):
            return ctx.enter_context(nc.sbuf_tensor(name, shape, dt))

        g = {
            "ps": ctx.enter_context(nc.psum_tensor("ps", [P, 8, 512], F32)),
            "hres": sb("hres", [P, NT * B, D]),
            "ident": sb("ident", [P, P]),
            "mhalf": sb("mhalf", [P, 8]),
            "w1raw": sb("w1raw", [P, FC, NJ * 2 * HE]),
            "w2": sb("w2", [HE // 2, 2, NJ, D]),
            "ident_ready": ctx.enter_context(nc.semaphore("ident_ready")),
        }
        setup(nc, g)
        with ExitStack() as attn:
            def sba(name, shape, dt=F32):
                return attn.enter_context(nc.sbuf_tensor(name, shape, dt))

            g["wa_hi"] = sba("wa_hi", [P, FC, 4 * DA], F32R)
            g["wa_lo"] = sba("wa_lo", [P, FC, 4 * DA], F32R)
            g["gb"] = sba("gb", [64, DA], F32R)
            g["gbh"] = sba("gbh", [64, DA], F32R)
            g["ones64"] = sba("ones64", [64, P], F32R)
            g["wo"] = sba("wo", [P, DA // P, D])
            g["decay"] = sba("decay", [P, HA, T + P + 2 * TXT])
            token_mixer(nc, g, ins)
            linear_attention(nc, g)
        phase_cd(nc, g, ins, out)


def kernel(**inputs):
    import numpy as np
    import concourse.bacc as bacc
    from concourse.bass_utils import run_bass_kernel_spmd

    nc = bacc.Bacc("TRN2", target_bir_lowering=False, num_devices=1)
    i = {k: np.asarray(v) for k, v in inputs.items()}
    x = i["x"]
    arrays = {
        "x_t": x.transpose(0, 1, 3, 2),
        "x_flat": x.transpose(0, 2, 3, 1).reshape(B, L, H0 * F),
        "txt": i["txt"],
        "wq_t": i["L0_tok_Wq_w"].T, "wk_t": i["L0_tok_Wk_w"].T, "wv_t": i["L0_tok_Wv_w"].T,
        "bq": i["L0_tok_Wq_b"], "bk": i["L0_tok_Wk_b"], "bv": i["L0_tok_Wv_b"],
        "w_bias_t": i["L0_tok_w_bias"].T,
        "mask_t": i["L0_tok_local_mask"].T,
        "out_w": i["L0_tok_out_w"], "out_b": i["L0_tok_out_b"],
        "ln_g": i["L0_tok_ln_g"], "ln_b": i["L0_tok_ln_b"],
        "W_Q_t": i["L0_attn_W_Q"].T, "W_K_t": i["L0_attn_W_K"].T,
        "W_V_t": i["L0_attn_W_V"].T, "W_g_t": i["L0_attn_W_g_w"].T,
        "W_g_b": i["L0_attn_W_g_b"], "W_O_t": i["L0_attn_W_O"].T,
        "decay_log": i["L0_attn_decay_log"],
        "ffn_w": i["L0_ffn_weight"],
        "Wq1": i["L1_attn_w_qkv"][0:D], "Wk1_t": i["L1_attn_w_qkv"][D:2 * D].T,
        "Wv1": i["L1_attn_w_qkv"][2 * D:], "Wv1_t": i["L1_attn_w_qkv"][2 * D:].T,
        "w_conv1": i["L1_attn_w_conv1"],
        "gate_t": i["L1_ffn_gate_w"].T,
        "W1_t": i["L1_ffn_W1"].transpose(0, 2, 1), "W2_t": i["L1_ffn_W2"].transpose(0, 2, 1),
        "Ws1_t": i["L1_ffn_Ws1"].T, "Ws2_t": i["L1_ffn_Ws2"].T,
        "hadamard": hadamard(np),
    }
    arrays = {f"in_{n}": np.ascontiguousarray(a) for n, a in arrays.items()}
    ins = {n[3:]: nc.dram_tensor(n, a.shape, mybir.dt.from_np(a.dtype), kind="ExternalInput").ap()
           for n, a in arrays.items()}
    out = nc.dram_tensor("out", (B, T, D), F32, kind="ExternalOutput").ap()
    build(nc, ins, out)
    return run_bass_kernel_spmd(nc, [arrays], core_ids=[0]).results[0]["out"]


def hadamard(np):
    h = np.array([[1.0]])
    while h.shape[0] < D:
        h = np.block([[h, h], [h, -h]])
    return (h / np.sqrt(D)).astype(np.float32)
```

```python
from contextlib import ExitStack

import concourse.bass as bass
from concourse import mybir

F32 = mybir.dt.float32
F32R = mybir.dt.float32r
BF16 = mybir.dt.bfloat16
U8 = mybir.dt.uint8
U32 = mybir.dt.uint32
ALU = mybir.AluOpType
ACT = mybir.ActivationFunctionType
AX = mybir.AxisListType

P = 128
B, F, L, H0 = 8, 64, 256, 4
TXT = 32
D = 256
T = L + TXT
NT = 3
TP = NT * P
ROWS = (P, P, TXT)
HA, DK = 8, 64
DA = HA * DK
E, HE, HS = 8, 192, 384
NJ = E + HS // HE
LN_EPS = 1e-5
ATT_EPS = 1e-6
ACT_POS, ACT_NEG = 7.0, 8.0
ROUND = 12582912.0
FC = D // P
WIDTHS = (T, T - P, 2 * TXT)
SCORE_COLS = sum(WIDTHS)


def ge(eng, sem, value):
    if isinstance(value, int) and value <= 0:
        return
    eng.wait_ge(sem, value)


class Steps:

    def __init__(self, eng, sem, start):
        self.eng, self.sem, self.n = eng, sem, start

    def __call__(self, ins):
        self.n = self.n + 1
        ins.then_inc(self.sem, 1)
        self.eng.wait_ge(self.sem, self.n)


def skewed(eng, step):
    step(-2, True, False, False)
    step(-1, True, True, False)
    step(0, True, True, True)
    with eng.Fori(1, B - 2) as b:
        step(b, True, True, True)
    step(B - 2, False, True, True)
    step(B - 1, False, False, True)


def skewed4(eng, step):
    for b in range(-3, 1):
        step(b, True, b > -3, b > -2, b > -1)
    with eng.Fori(1, B - 3) as b:
        step(b, True, True, True, True)
    for b in range(B - 3, B):
        step(b, False, b < B - 2, b < B - 1, True)


def row_broadcast(ap, n):
    return ap.rearrange("(a n) -> a n", a=1).to_broadcast([P, n])


def token_mixer(nc, g, ins):
    with ExitStack() as ctx:
        def sb(name, shape, dt=F32):
            return ctx.enter_context(nc.sbuf_tensor(name, shape, dt))

        def sem(name):
            return ctx.enter_context(nc.semaphore(name))

        ps = g["ps"]
        hres = g["hres"]
        ident, gam = g["ident"], g["gam"]
        stage = sb("stage", [P, FC, 4 * DA])
        wqkv = sb("a_wqkv", [F + 1, 3 * F])
        ewt = sb("a_ewt", [P, 2, L])
        mask8 = sb("a_mask8", [P, 2, L], U8)
        maskf = sb("a_maskf", [P, 2, L])
        outw = sb("a_outw", [P, FC, D])
        outb = sb("a_outb", [P, D])
        lng = sb("a_lng", [P, D])
        lnb = sb("a_lnb", [P, D])
        xt = sb("a_xt", [F + 1, H0, L])
        xfl = sb("a_xfl", [P, 2, D])
        xb = sb("a_xb", [P, 2, D])
        nk = sb("a_nk", [P, 2, 2, 2 * D])
        eq = sb("a_eq", [P, 2, 2, D])
        den = sb("a_den", [P, 2, D])
        rden = sb("a_rden", [P, 2, D])
        y = sb("a_y", [P, 2, D])
        yt = sb("a_yt", [P, FC, L])
        hp = sb("a_hp", [P, 2, D])
        hn = sb("a_hn", [P, 2, D])
        stats = sb("a_stats", [P, 2, 6])
        mv = sb("a_mv", [P, 2, 2])
        ve = sb("a_ve", [P, 2, 1])
        tick = sb("a_tick", [P, 1])
        rstd = sb("a_rstd", [P, 2, 1])
        lgam = sb("a_lgam", [P, HA])
        age = sb("a_age", [P, T])
        agm = sb("a_agm", [P, T])
        draw = sb("a_draw", [P, HA])

        w_in = sem("a_w_in")
        ew_in = sem("a_ew_in")
        x_in = sem("a_x_in")
        xf_in = sem("a_xf_in")
        txt_in = sem("a_txt_in")
        attw_in = sem("a_attw_in")
        moew_in = sem("a_moew_in")
        ones_set = sem("a_ones_set")
        text_zeroed = sem("a_text_zeroed")
        mask_applied = sem("a_mask_applied")
        ew_ready = sem("a_ew_ready")
        qkv_done = sem("a_qkv_done")
        exps_done = sem("a_exps_done")
        ekv_done = sem("a_ekv_done")
        nd_done = sem("a_nd_done")
        y_done = sem("a_y_done")
        turned = sem("a_turned")
        yt_done = sem("a_yt_done")
        out_done = sem("a_out_done")
        hp_done = sem("a_hp_done")
        xb_done = sem("a_xb_done")
        var_done = sem("a_var_done")
        rstd_done = sem("a_rstd_done")
        y_steps = sem("a_y_steps")
        ln_steps = sem("a_ln_steps")
        hi_done = sem("a_hi_done")
        gam_in = sem("a_gam_in")
        gam_steps = sem("a_gam_steps")
        gam_ready = sem("a_gam_ready")
        age_steps = sem("a_age_steps")
        decay_set = sem("a_decay_set")
        pool_done = sem("a_pool_done")

        qkv = ps[:, 0:4, :].rearrange("p (l a) (c j) -> p l (a c) j", l=2, c=2)

        def part(i):
            return qkv[:, :, :, i * F:(i + 1) * F]

        def heads(ap):
            return ap.rearrange("p l (h d) -> p l h d", h=H0)

        def part_of(w, b):
            n = 4 * DA // B
            return w[:, :, b * n:(b + 1) * n] if isinstance(b, int) else w[:, :, bass.ds(b * n, n)]

        block = ctx.enter_context(nc.Block())

        @block.sync
        def _(sp):
            x_t, x_flat = ins["x_t"], ins["x_flat"]

            def load_x(b):
                if isinstance(b, int):
                    xs = x_t[b]
                else:
                    xs = x_t[bass.ds(b, 1)].rearrange("a c h l -> (a c) h l")
                ge(sp, qkv_done, b)
                sp.dma_start(xt[0:F], xs).then_inc(x_in, 16)

            def load_flat(b):
                fs = x_flat[b] if isinstance(b, int) else x_flat[bass.ds(b, 1)].rearrange("a l f -> (a l) f")
                ge(sp, xb_done, b)
                sp.dma_start(xfl[:], fs.rearrange("(t p) f -> p t f", p=P)).then_inc(xf_in, 16)

            load_x(0)
            sp.dma_start(draw[:], row_broadcast(ins["decay_log"], HA)).then_inc(gam_in, 16)
            for i, n in enumerate("qkv"):
                sp.dma_start(wqkv[0:F, i * F:(i + 1) * F], ins[f"w{n}_t"]).then_inc(w_in, 16)
                sp.dma_start(wqkv[F:F + 1, i * F:(i + 1) * F],
                             ins[f"b{n}"].rearrange("(a n) -> a n", a=1)).then_inc(w_in, 16)
            sp.dma_start(ewt[:], ins["w_bias_t"].rearrange("(s p) t -> p s t", p=P)).then_inc(ew_in, 16)
            sp.dma_start(mask8[:], ins["mask_t"].rearrange("(s p) t -> p s t", p=P)).then_inc(ew_in, 16)
            sp.dma_start(outb[:], row_broadcast(ins["out_b"], D)).then_inc(w_in, 16)
            sp.dma_start(outw[:], ins["out_w"].rearrange("(c p) n -> p c n", p=P)).then_inc(w_in, 16)
            sp.dma_start(lng[:], row_broadcast(ins["ln_g"], D)).then_inc(w_in, 16)
            sp.dma_start(lnb[:], row_broadcast(ins["ln_b"], D)).then_inc(w_in, 16)
            load_flat(0)
            load_x(1)
            for i, n in enumerate(("W_Q_t", "W_K_t", "W_V_t", "W_g_t")):
                sp.dma_start(stage[:, :, i * DA:(i + 1) * DA],
                             ins[n].rearrange("(c p) n -> p c n", p=P)).then_inc(attw_in, 16)
            load_x(2)
            with sp.Fori(3, B) as b:
                load_x(b)
                load_flat(b - 2)
            load_flat(B - 2)
            load_flat(B - 1)
            sp.dma_start(g["wo"][:], ins["W_O_t"].rearrange("(c p) n -> p c n", p=P)).then_inc(moew_in, 16)
            for e in range(E):
                sp.dma_start(g["w1raw"][:, :, e * 2 * HE:(e + 1) * 2 * HE],
                             ins["W1_t"][e].rearrange("(c p) n -> p c n", p=P)).then_inc(moew_in, 16)
                sp.dma_start(g["w2"][:, :, e, :],
                             ins["W2_t"][e].rearrange("(c p) n -> p c n", p=HE // 2)).then_inc(moew_in, 16)
            sp.dma_start(g["w1raw"][:, :, E * 2 * HE:],
                         ins["Ws1_t"].rearrange("(c p) n -> p c n", p=P)).then_inc(moew_in, 16)
            sp.dma_start(g["ws2"][:], ins["Ws2_t"].rearrange("(c p) n -> p c n", p=P)).then_inc(moew_in, 16)
            sp.wait_ge(moew_in, 16 * (3 + 2 * E))
            sp.wait_ge(txt_in, 16 * B)

        @block.tensor
        def _(pe):
            def qkv_products(b):
                ge(pe, x_in, 16 * b + 16)
                if isinstance(b, int) and b == 0:
                    pe.wait_ge(ones_set, 1)
                    pe.wait_ge(w_in, 16 * 10)
                ge(pe, ekv_done, b)
                ge(pe, exps_done, b)
                for lt in range(2):
                    for h in range(H0):
                        mm = nc.tensor.matmul(qkv[:, lt, h, 0:3 * F], xt[:, h, lt * P:(lt + 1) * P],
                                              wqkv[:, :], start=True, stop=True)
                mm.then_inc(qkv_done, 1)

            def turn(b):
                pe.wait_ge(y_done, b + 1)
                if isinstance(b, int) and b == 0:
                    pe.wait_ge(g["ident_ready"], 1)
                ge(pe, yt_done, b)
                for fc in range(FC):
                    for t in range(2):
                        mm = nc.tensor.transpose(ps[:, 6, fc * L + t * P:fc * L + (t + 1) * P],
                                                 y[:, t, fc * P:(fc + 1) * P], ident[:])
                mm.then_inc(turned, 1)

            def sums(b):
                if isinstance(b, int) and b == 0:
                    pe.wait_ge(ew_ready, 1)
                pe.wait_ge(ekv_done, b + 1)
                pe.wait_ge(exps_done, b + 1)
                ge(pe, y_done, b)
                for t in range(2):
                    for s in range(2):
                        mm = nc.tensor.matmul(ps[:, 4 + t, :], ewt[:, s, t * P:(t + 1) * P],
                                              nk[:, b % 2, s, :], start=s == 0, stop=s == 1)
                mm.then_inc(nd_done, 1)

            def project(b):
                pe.wait_ge(yt_done, b + 1)
                ge(pe, hp_done, b)
                for t in range(2):
                    for fc in range(FC):
                        mm = nc.tensor.matmul(ps[:, 7, t * D:(t + 1) * D], yt[:, fc, t * P:(t + 1) * P],
                                              outw[:, fc, :], start=fc == 0, stop=fc == FC - 1)
                mm.then_inc(out_done, 1)

            def step(b, s1, s2, s3):
                if s1:
                    qkv_products(b + 2)
                if s3:
                    turn(b)
                if s2:
                    sums(b + 1)
                if s3:
                    project(b)

            skewed(pe, step)

        @block.scalar
        def _(act):
            act.wait_ge(gam_in, 16)
            nc.scalar.activation(gam[:], draw[:], ACT.Exp, scale=-1.0).then_inc(gam_steps, 1)
            act.wait_ge(mask_applied, 1)
            nc.scalar.activation(ewt[:], maskf[:], ACT.Exp).then_inc(ew_ready, 1)
            act.wait_ge(gam_steps, 4)
            nc.scalar.activation(lgam[:], gam[:], ACT.Ln).then_inc(gam_ready, 1)
            act.wait_ge(gam_ready, 1)
            act.wait_ge(age_steps, 2)
            for h in range(HA):
                nc.scalar.activation(g["decay"][:, h, 0:T], agm[:], ACT.Exp,
                                     scale=lgam[:, h:h + 1]).then_inc(decay_set, 1)

            def exps(b):
                act.wait_ge(qkv_done, b + 1)
                ge(act, nd_done, b - 1)
                nc.scalar.activation(heads(nk[:, b % 2, :, D:2 * D]) if isinstance(b, int) else
                                     nk[:, b % 2, :, D:2 * D].rearrange("p l (h d) -> p l h d", h=H0),
                                     part(1), ACT.Exp)
                ge(act, y_done, b - 1)
                nc.scalar.activation(heads(eq[:, b % 2]), part(0), ACT.Exp, scale=-1.0).then_inc(exps_done, 1)

            def copy_yt(b):
                act.wait_ge(turned, b + 1)
                ge(act, out_done, b)
                nc.scalar.copy(yt[:].rearrange("p c l -> p (c l)"), ps[:, 6, :]).then_inc(yt_done, 1)

            def step(b, s1, s2, s3):
                if s3:
                    copy_yt(b)
                if s1:
                    exps(b + 2)
                if s3:
                    if isinstance(b, int) and b == 0:
                        act.wait_ge(attw_in, 16 * 4)
                    nc.scalar.copy(part_of(g["wa_hi"], b), part_of(stage, b)).then_inc(hi_done, 1)

            skewed(act, step)

        @block.vector
        def _(dve):
            nc.vector.memset(xt[F:F + 1], 1.0).then_inc(ones_set, 1)
            for b in range(B):
                ms = nc.vector.memset(hres[:, NT * b + 2, :], 0.0)
            ms.then_inc(text_zeroed, 1)
            dve.wait_ge(gam_steps, 1)
            step = Steps(dve, gam_steps, 1)
            step(nc.vector.tensor_scalar(gam[:], gam[:], 1.0, None, ALU.add))
            step(nc.vector.reciprocal(gam[:], gam[:]))
            step(nc.vector.tensor_scalar(gam[:], gam[:], 1e-18, None, ALU.max))
            dve.wait_ge(ew_in, 32)
            nc.vector.tensor_copy(maskf[:], mask8[:]).then_inc(y_steps, 1)
            dve.wait_ge(y_steps, 1)
            nc.vector.tensor_tensor(maskf[:], maskf[:], ewt[:], ALU.mult).then_inc(mask_applied, 1)

            def weigh(b):
                dve.wait_ge(exps_done, b + 1)
                ge(dve, nd_done, b - 1)
                nc.vector.tensor_tensor(heads(nk[:, b % 2, :, 0:D]), heads(nk[:, b % 2, :, D:2 * D]),
                                        part(2), ALU.mult).then_inc(ekv_done, 1)

            def divide(b):
                step = Steps(dve, y_steps, b * 2 + 1)
                dve.wait_ge(nd_done, b + 1)
                step(nc.vector.scalar_tensor_tensor(out=den[:], in0=eq[:, b % 2], scalar=1.0,
                                                    in1=ps[:, 4:6, D:2 * D], op0=ALU.add, op1=ALU.mult))
                step(nc.vector.reciprocal(rden[:], den[:]))
                ge(dve, turned, b)
                nc.vector.tensor_tensor(y[:], ps[:, 4:6, 0:D], rden[:], ALU.mult).then_inc(y_done, 1)

            def norm(b):
                step = Steps(dve, ln_steps, b * 6)
                dve.wait_ge(out_done, b + 1)
                dve.wait_ge(xb_done, b + 1)
                nc.vector.tensor_tensor(hp[:].rearrange("p t f -> p (t f)"), ps[:, 7, :],
                                        xb[:].rearrange("p t f -> p (t f)"), ALU.add).then_inc(hp_done, 1)
                dve.wait_ge(hp_done, b + 1)
                for t in range(2):
                    step(nc.vector.bn_stats(stats[:, t, :], hp[:, t, :]))
                nc.vector.memset(tick[:], 0.0)
                for t in range(2):
                    last = nc.vector.bn_aggr(mv[:, t, :], stats[:, t, :])
                step(last)
                nc.vector.tensor_scalar(ve[:], mv[:, :, 1:2], LN_EPS, None, ALU.add).then_inc(var_done, 1)
                dve.wait_ge(rstd_done, b + 1)
                for t in range(2):
                    step(nc.vector.tensor_scalar(hn[:, t, :], hp[:, t, :], mv[:, t, 0:1], rstd[:, t, :],
                                                 ALU.subtract, ALU.mult))
                gb = lng[:].rearrange("p (a f) -> p a f", a=1).to_broadcast([P, 2, D])
                bb = lnb[:].rearrange("p (a f) -> p a f", a=1).to_broadcast([P, 2, D])
                step(nc.vector.tensor_tensor(hn[:], hn[:], gb, ALU.mult))
                nc.vector.tensor_tensor(hres[:, bass.ds(b * NT, 2), :] if not isinstance(b, int) else
                                        hres[:, b * NT:b * NT + 2, :], hn[:], bb, ALU.add)

            def step(b, s1, s2, s3):
                if s1:
                    weigh(b + 2)
                if s2:
                    divide(b + 1)
                if s3:
                    norm(b)

            skewed(dve, step)

        @block.gpsimd
        def _(pool):
            nc.gpsimd.iota(age[:], [[1, T]], base=0, channel_multiplier=-1,
                           allow_small_or_imprecise_dtypes=True).then_inc(age_steps, 1)
            pool.wait_ge(age_steps, 1)
            nc.gpsimd.tensor_scalar(agm[:], age[:], 0.0, None, ALU.max).then_inc(age_steps, 1)
            pool.wait_ge(text_zeroed, 1)
            for b in range(B):
                pool.dma_start(hres[0:TXT, NT * b + 2, :], ins["txt"][b]).then_inc(txt_in, 16)

            def add_bias(b):
                pool.wait_ge(xf_in, 16 * b + 16)
                if isinstance(b, int) and b == 0:
                    pool.wait_ge(w_in, 16 * 10)
                ge(pool, hp_done, b)
                ob = outb[:].rearrange("p (a f) -> p a f", a=1).to_broadcast([P, 2, D])
                nc.gpsimd.tensor_tensor(xb[:], xfl[:], ob, ALU.add).then_inc(xb_done, 1)

            def root(b):
                pool.wait_ge(var_done, b + 1)
                nc.gpsimd.tensor_tensor(rstd[:], ve[:], g["mhalf"][:, 0:2].rearrange("p (t a) -> p t a", a=1),
                                        ALU.pow).then_inc(rstd_done, 1)

            def split(b):
                pool.wait_ge(hi_done, b + 1)
                nc.gpsimd.tensor_tensor(part_of(g["wa_lo"], b), part_of(stage, b),
                                        part_of(g["wa_hi"], b).bitcast(F32), ALU.subtract)

            add_bias(0)
            nc.gpsimd.memset(g["decay"][:, :, SCORE_COLS - 2 * TXT:SCORE_COLS - TXT], 0.0)
            for h in range(HA):
                pool.wait_ge(decay_set, h + 1)
                nc.gpsimd.affine_select(out=g["decay"][:, h, 0:T], in_=g["decay"][:, h, 0:T],
                                        compare_op=ALU.is_ge, fill=0.0, base=0, pattern=[[1, T]],
                                        channel_multiplier=-1).then_inc(pool_done, 1)
                pool.wait_ge(pool_done, 3 * h + 1)
                nc.gpsimd.tensor_copy(g["decay"][:, h, T:T + P + TXT],
                                      g["decay"][:, h, 0:P + TXT]).then_inc(pool_done, 1)
                nc.gpsimd.tensor_copy(g["decay"][:, h, SCORE_COLS - TXT:SCORE_COLS],
                                      g["decay"][:, h, 0:TXT]).then_inc(pool_done, 1)
            root(0)
            split(0)
            with pool.Fori(1, B) as b:
                add_bias(b)
                root(b)
                split(b)


def setup(nc, g):
    with ExitStack() as ctx:
        zeroed = ctx.enter_context(nc.semaphore("zeroed"))
        block = ctx.enter_context(nc.Block())

        @block.gpsimd
        def _(pool):
            nc.gpsimd.memset(g["mhalf"][:], -0.5)
            nc.gpsimd.memset(g["ident"][:], 0.0).then_inc(zeroed, 1)
            pool.wait_ge(zeroed, 1)
            nc.gpsimd.affine_select(out=g["ident"][:], in_=g["ident"][:], compare_op=ALU.not_equal,
                                    fill=1.0, base=0, pattern=[[-1, P]],
                                    channel_multiplier=1).then_inc(g["ident_ready"], 1)


def norm_stats(nc, dve, step, src, stats, mv, ve, tick, var_done):
    for t in range(NT):
        last = nc.vector.bn_stats(stats[:, t, :], src(t))
    step(last)
    nc.vector.memset(tick[:], 0.0)
    for t in range(NT):
        last = nc.vector.bn_aggr(mv[:, t, :], stats[:, t, :])
    step(last)
    nc.vector.tensor_scalar(ve[:], mv[:, :, 1:2], LN_EPS, None, ALU.add).then_inc(var_done, 1)


def res(g, b, t):
    if isinstance(b, int):
        return g["hres"][:, NT * b + t, :]
    return g["hres"][:, bass.ds(b * NT + t, 1), :].rearrange("p a f -> p (a f)")


def split_products(nc, out, x_hi, x_lo, w_hi, w_lo, start, stop):
    nc.tensor.matmul(out, x_hi, w_hi, start=start, stop=False)
    nc.tensor.matmul(out, x_hi, w_lo, start=False, stop=False)
    return nc.tensor.matmul(out, x_lo, w_hi, start=False, stop=stop)


def linear_attention(nc, g):
    with ExitStack() as ctx:
        def sb(name, shape, dt=F32):
            return ctx.enter_context(nc.sbuf_tensor(name, shape, dt))

        def sem(name):
            return ctx.enter_context(nc.semaphore(name))

        ps, hres, ident = g["ps"], g["hres"], g["ident"]
        wa_hi, wa_lo, wo = g["wa_hi"], g["wa_lo"], g["wo"]
        NP = HA // 2
        NG = 3 * NP // 2
        AW = SCORE_COLS
        stats = sb("b_stats", [P, NT, 6])
        mv = sb("b_mv", [P, NT, 2])
        ve = sb("b_ve", [P, NT, 1])
        rstd = sb("b_rstd", [P, NT, 1])
        tick = sb("b_tick", [P, 1])
        xn = sb("b_xn", [P, NT, D])
        x_hi = sb("b_x_hi", [P, FC, TP], F32R)
        x_lo = sb("b_x_lo", [P, FC, TP], F32R)
        qk = sb("b_qk", [P, 2 * NP, T])
        ex = sb("b_ex", [P, 2, 2, T])
        v = sb("b_v", [P, NT, DA])
        sg = sb("b_sg", [P, NP, T])
        z = sb("b_z", [P, NP, T])
        a = sb("b_a", [P, 2, AW])
        rd = sb("b_rd", [HA, T])
        yt = sb("b_yt", [P, NP, T])
        gpair = sb("b_gpair", [P, NP])
        bg = sb("b_bg", [P, NP])
        pick = sb("b_pick", [P, NP, HA])
        spread = sb("b_spread", [HA, NP, P])

        bias_in = sem("b_bias_in")
        pick_set = sem("b_pick_set")
        pick_turned = sem("b_pick_turned")
        ln_steps = sem("b_ln_steps")
        var_done = sem("b_var_done")
        rstd_done = sem("b_rstd_done")
        xn_done = sem("b_xn_done")
        x_turned = sem("b_x_turned")
        hi_done = sem("b_hi_done")
        lo_done = sem("b_lo_done")
        qk_done = sem("b_qk_done")
        exp_done = sem("b_exp_done")
        low_done = sem("b_low_done")
        phi_done = sem("b_phi_done")
        gate_done = sem("b_gate_done")
        gate_read = sem("b_gate_read")
        v_done = sem("b_v_done")
        v_read = sem("b_v_read")
        z_done = sem("b_z_done")
        qz_done = sem("b_qz_done")
        den_done = sem("b_den_done")
        den_steps = sem("b_den_steps")
        rd_done = sem("b_rd_done")
        spread_done = sem("b_spread_done")
        sg_done = sem("b_sg_done")
        score_done = sem("b_score_done")
        masked = sem("b_masked")
        num_done = sem("b_num_done")
        y_done = sem("b_y_done")
        wo_done = sem("b_wo_done")
        res_done = sem("b_res_done")

        def group(i):
            return 2 + 2 * (i % 2)

        block = ctx.enter_context(nc.Block())

        @block.sync
        def _(sp):
            for j in range(NP):
                sp.dma_start(bg[:, j:j + 1], g["W_g_b"].rearrange("(j p a) -> j p a", p=P, a=1)[j]
                             ).then_inc(bias_in, 16)

        @block.tensor
        def _(pe):
            pe.wait_ge(pick_set, 3)
            for j in range(NP):
                mm = nc.tensor.transpose(ps[0:HA, 7, j * P:(j + 1) * P], pick[:, j, :], ident[:])
            mm.then_inc(pick_turned, 1)

            def turn_x(b):
                pe.wait_ge(xn_done, b + 1)
                ge(pe, lo_done, b)
                for fc in range(FC):
                    for t in range(NT):
                        mm = nc.tensor.transpose(ps[:, fc, t * P:(t + 1) * P],
                                                 xn[:, t, fc * P:(fc + 1) * P], ident[:])
                mm.then_inc(x_turned, 1)

            def projections(b):
                pe.wait_ge(lo_done, b + 1)
                ge(pe, sg_done, 2 * b)
                ge(pe, masked, HA * b)
                for t in range(NT):
                    for fc in range(FC):
                        rows = slice(t * P, (t + 1) * P)
                        cols = slice(2 * DA, 3 * DA)
                        mm = split_products(nc, ps[:, 2 + t, :], x_hi[:, fc, rows], x_lo[:, fc, rows],
                                            wa_hi[:, fc, cols], wa_lo[:, fc, cols], fc == 0, fc == FC - 1)
                    if t:
                        mm.then_inc(v_done, 1)
                for i in range(NG):
                    if i < 2:
                        pe.wait_ge(v_read, 2 * b + i + 1)
                    else:
                        pe.wait_ge(phi_done, NP * b + i - 1)
                    for k in range(2):
                        cols = 2 * i + k
                        cols += 0 if i < NP else NP
                        cols = slice(cols * P, (cols + 1) * P)
                        for fc in range(FC):
                            mm = split_products(nc, ps[:, group(i) + k, 0:T], wa_hi[:, fc, cols],
                                                wa_lo[:, fc, cols], x_hi[:, fc, 0:T], x_lo[:, fc, 0:T],
                                                fc == 0, fc == FC - 1)
                    mm.then_inc(qk_done if i < NP else gate_done, 1)

            def denominators(b):
                pe.wait_ge(gate_read, 2 * (b + 1))
                pe.wait_ge(qz_done, NP * (b + 1))
                for j in range(NP):
                    mm = nc.tensor.matmul(ps[0:HA, 5, 0:T], pick[:, j, :], z[:, j, :],
                                          start=j == 0, stop=j == NP - 1)
                mm.then_inc(den_done, 1)

            def spread_out(b):
                pe.wait_ge(rd_done, b + 1)
                for j in range(NP):
                    mm = nc.tensor.matmul(ps[:, 2 + j, 0:T], spread[:, j, :], rd[:], start=True, stop=True)
                    if j % 2:
                        mm.then_inc(spread_done, 1)

            def scores(b, h):
                if h < 2:
                    pe.wait_ge(sg_done, 2 * (b + 1))
                else:
                    pe.wait_ge(masked, HA * b + h - 1)
                rows = slice(DK * (h % 2), DK * (h % 2) + DK)
                j, col = h // 2, 0
                for s in range(NT):
                    m, n = ROWS[s], WIDTHS[s]
                    mm = nc.tensor.matmul(ps[0:m, 4 + h % 2, col:col + n],
                                          qk[rows, NP + j, s * P:s * P + m],
                                          qk[rows, j, T - n:T], start=True, stop=True)
                    col += n
                mm.then_inc(score_done, 1)

            def values(b, h):
                pe.wait_ge(masked, HA * b + h + 1)
                j = h // 2
                if h % 2 == 0:
                    ge(pe, y_done, NP * b + j - 1)
                    if j < 2:
                        ge(pe, res_done, 2 * (b - 1) + j + 1)
                col = 0
                for s in range(NT):
                    n, kk = WIDTHS[s], ROWS[s]
                    mm = nc.tensor.matmul(ps[DK * (h % 2):DK * (h % 2) + DK, 6 + j % 2, T - n:T],
                                          v[0:kk, s, h * DK:(h + 1) * DK], a[0:kk, h % 2, col:col + n],
                                          start=s == 0, stop=s == NT - 1)
                    col += n
                mm.then_inc(num_done, 1)

            def attend(b):
                scores(b, 0)
                scores(b, 1)
                for h in range(HA):
                    values(b, h)
                    if h + 2 < HA:
                        scores(b, h + 2)

            def output(b, tiles):
                pe.wait_ge(y_done, NP * (b + 1))
                for t in tiles:
                    m = ROWS[t]
                    o = ps[0:m, 6 + t // 2, (t % 2) * D:(t % 2) * D + D]
                    for j in range(NP):
                        mm = nc.tensor.matmul(o, yt[:, j, t * P:t * P + m], wo[:, j, :],
                                              start=j == 0, stop=j == NP - 1)
                mm.then_inc(wo_done, 1)

            def step(b, s1, s2, s3):
                if s3:
                    attend(b)
                if s2:
                    projections(b + 1)
                if s3:
                    output(b, (0, 1))
                if s2:
                    if isinstance(b, int) and b == -1:
                        pe.wait_ge(pick_turned, 2)
                    denominators(b + 1)
                if s1:
                    turn_x(b + 2)
                if s2:
                    spread_out(b + 1)
                if s3:
                    output(b, (2,))

            skewed(pe, step)

        @block.scalar
        def _(act):
            act.wait_ge(pick_turned, 1)
            nc.scalar.copy(spread[:].rearrange("p j m -> p (j m)"), ps[0:HA, 7, :]).then_inc(pick_turned, 1)
            act.wait_ge(bias_in, 16 * NP)

            def evacuate(b):
                act.wait_ge(v_done, 2 * b + 1)
                ge(act, num_done, HA * b)
                nc.scalar.copy(v[:, 0:2, :], ps[:, 2:4, :]).then_inc(v_read, 1)
                act.wait_ge(v_done, 2 * b + 2)
                nc.scalar.copy(v[:, 2, :], ps[:, 4, :]).then_inc(v_read, 1)
                for i in range(NP):
                    act.wait_ge(qk_done, NP * b + i + 1)
                    ge(act, phi_done, NP * b + i - 1)
                    nc.scalar.activation(ex[:, i % 2], ps[:, group(i):group(i) + 2, 0:T], ACT.Exp
                                         ).then_inc(exp_done, 1)
                for i in range(NP, NG):
                    act.wait_ge(gate_done, 2 * b + i - NP + 1)
                    if i == NP:
                        ge(act, y_done, NP * b)
                    for k in range(2):
                        j = 2 * (i - NP) + k
                        last = nc.scalar.activation(sg[:, j, :], ps[:, group(i) + k, 0:T], ACT.Sigmoid,
                                                    bias=bg[:, j:j + 1])
                    last.then_inc(gate_read, 1)

            def split_x(b):
                act.wait_ge(x_turned, b + 1)
                ge(act, gate_done, 2 * b)
                nc.scalar.copy(x_hi[:], ps[:, 0:2, 0:TP]).then_inc(hi_done, 1)

            def step(b, s1, s2, s3):
                if s2:
                    evacuate(b + 1)
                if s1:
                    split_x(b + 2)

            skewed(act, step)

        @block.vector
        def _(dve):
            step = Steps(dve, pick_set, 0)
            for r in range(2):
                rows = slice(r * DK, (r + 1) * DK)
                last = nc.vector.tensor_copy(gpair[rows, :],
                                             g["gam"][rows, :].rearrange("p (j r) -> p j r", r=2)[:, :, r])
            step(last)
            step(nc.vector.memset(pick[:], 0.0))
            for j in range(NP):
                for r in range(2):
                    last = nc.vector.memset(pick[r * DK:(r + 1) * DK, j, 2 * j + r:2 * j + r + 1], 1.0)
            step(last)

            def norm(b):
                step = Steps(dve, ln_steps, 2 * b)
                norm_stats(nc, dve, step, lambda t: res(g, b, t), stats, mv, ve, tick, var_done)
                dve.wait_ge(rstd_done, b + 1)
                ge(dve, x_turned, b)
                for t in range(NT):
                    last = nc.vector.tensor_scalar(xn[:, t, :], res(g, b, t), mv[:, t, 0:1], rstd[:, t, :],
                                                   ALU.subtract, ALU.mult)
                last.then_inc(xn_done, 1)

            def take(b, j):
                dve.wait_ge(num_done, HA * b + 2 * j + 2)
                if j == 0:
                    ge(dve, wo_done, 2 * b)
                nc.vector.tensor_tensor(yt[:, j, :], ps[:, 6 + j % 2, 0:T], sg[:, j, :], ALU.mult
                                        ).then_inc(y_done, 1)

            def decay(b):
                for h in range(HA):
                    dve.wait_ge(score_done, HA * b + h + 1)
                    ge(dve, num_done, HA * b + h - 1)
                    nc.vector.tensor_tensor(a[:, h % 2, :], ps[:, 4 + h % 2, 0:AW], g["decay"][:, h, :],
                                            ALU.mult).then_inc(masked, 1)
                    if h % 2 and h > 1:
                        take(b, h // 2 - 1)
                take(b, NP - 1)

            def phi(b):
                for i in range(NP):
                    dve.wait_ge(exp_done, NP * b + i + 1)
                    nc.vector.tensor_scalar(ex[:, i % 2], ex[:, i % 2], 1.0, None, ALU.min).then_inc(low_done, 1)
                    dve.wait_ge(low_done, NP * b + i + 1)
                    if i == 0:
                        ge(dve, score_done, HA * b)
                    nc.vector.scalar_tensor_tensor(out=qk[:, 2 * i:2 * i + 2, 0:T],
                                                   in0=ps[:, group(i):group(i) + 2, 0:T], scalar=0.0,
                                                   in1=ex[:, i % 2], op0=ALU.max,
                                                   op1=ALU.add).then_inc(phi_done, 1)
                dve.wait_ge(phi_done, NP * (b + 1))
                ge(dve, den_done, b)
                for j in range(NP):
                    nc.vector.tensor_tensor_scan(z[:, j, :], gpair[:, j:j + 1].to_broadcast([P, T]),
                                                 qk[:, NP + j, 0:T], 0.0, ALU.mult, ALU.add
                                                 ).then_inc(z_done, 1)

            def split_x(b):
                dve.wait_ge(hi_done, b + 1)
                nc.vector.tensor_tensor(x_lo[:], ps[:, 0:2, 0:TP], x_hi[:].bitcast(F32),
                                        ALU.subtract).then_inc(lo_done, 1)

            def invert(b):
                step = Steps(dve, den_steps, b)
                dve.wait_ge(den_done, b + 1)
                ge(dve, spread_done, 2 * b)
                step(nc.vector.tensor_scalar(rd[:], ps[0:HA, 5, 0:T], ATT_EPS, None, ALU.add))
                nc.vector.reciprocal(rd[:], rd[:]).then_inc(rd_done, 1)

            def divide(b):
                dve.wait_ge(gate_read, 2 * (b + 1))
                for i in range(2):
                    dve.wait_ge(spread_done, 2 * b + i + 1)
                    s = sg[:, 2 * i:2 * i + 2, :]
                    nc.vector.tensor_tensor(s, ps[:, 2 + 2 * i:4 + 2 * i, 0:T], s, ALU.mult).then_inc(sg_done, 1)

            def residual(b, tiles):
                dve.wait_ge(wo_done, 2 * b + 1 + tiles[0] // 2)
                for t in tiles:
                    m = ROWS[t]
                    r = res(g, b, t)[0:m]
                    ins = nc.vector.tensor_tensor(r, ps[0:m, 6 + t // 2, (t % 2) * D:(t % 2) * D + D], r, ALU.add)
                ins.then_inc(res_done, 1)

            def step(b, s1, s2, s3):
                if s3:
                    decay(b)
                if s1:
                    norm(b + 2)
                if s2:
                    phi(b + 1)
                    invert(b + 1)
                if s1:
                    split_x(b + 2)
                if s3:
                    residual(b, (0, 1))
                if s2:
                    divide(b + 1)
                if s3:
                    residual(b, (2,))

            skewed(dve, step)

        @block.gpsimd
        def _(pool):
            def step(b, s1, s2, s3):
                if s1:
                    pool.wait_ge(var_done, b + 3)
                    nc.gpsimd.tensor_tensor(rstd[:], ve[:], g["mhalf"][:, 0:NT].rearrange("p (t a) -> p t a", a=1),
                                            ALU.pow).then_inc(rstd_done, 1)
                if s2:
                    for j in range(NP):
                        pool.wait_ge(z_done, NP * (b + 1) + j + 1)
                        nc.gpsimd.tensor_tensor(z[:, j, :], z[:, j, :], qk[:, j, 0:T], ALU.mult
                                                ).then_inc(qz_done, 1)

            skewed(pool, step)


def feed_forward(nc, g, ins):
    with ExitStack() as ctx:
        def sb(name, shape, dt=F32):
            return ctx.enter_context(nc.sbuf_tensor(name, shape, dt))

        def sem(name):
            return ctx.enter_context(nc.semaphore(name))

        ps, hres, ident = g["ps"], g["hres"], g["ident"]
        x3 = g["x3"]
        hraw = sb("c_hraw", [P, FC, D])
        had = sb("c_had", [P, FC, D], F32R)
        wf = sb("c_wf", [P, FC, D])
        wabs = sb("c_wabs", [P, FC])
        wsc = sb("c_wsc", [P, FC])
        wlim = sb("c_wlim", [P, FC, 2])
        tneg = sb("c_tneg", [P, FC, D])
        tern = sb("c_tern", [P, FC, D], BF16)
        tern_t = sb("c_tern_t", [P, FC, D], BF16)
        diag = sb("c_diag", [P, FC, P])
        ones = sb("c_ones", [P, P])
        identb = sb("c_identb", [P, P], BF16)
        wrow = sb("c_wrow", [P, D])
        wq1 = sb("c_wq1", [P, FC, D])
        w1c = sb("c_w1c", [P, FC])
        w1b = sb("c_w1b", [P, FC, P])
        ub = sb("c_ub", [P, D])
        roundc = sb("c_roundc", [P, 1])
        stats = sb("c_stats", [P, NT, 6])
        mv = sb("c_mv", [P, NT, 2])
        ve = sb("c_ve", [P, NT, 1])
        rstd = sb("c_rstd", [P, NT, 1])
        stats3 = sb("c_stats3", [P, NT, 6])
        mv3 = sb("c_mv3", [P, NT, 2])
        ve3 = sb("c_ve3", [P, NT, 1])
        rstd3 = sb("c_rstd3", [P, NT, 1])
        tick = sb("c_tick", [P, 1])
        xn = sb("c_xn", [P, NT, D])
        x_hi = sb("c_x_hi", [P, FC, TP], F32R)
        x_lo = sb("c_x_lo", [P, FC, TP], F32R)
        am = sb("c_am", [P, NT])
        xsc = sb("c_xsc", [P, NT])
        xinv = sb("c_xinv", [P, NT])
        qm = sb("c_qm", [P, NT, D])
        qi = sb("c_qi", [P, NT, D], BF16)
        q_t = sb("c_q_t", [P, FC, TP], BF16)
        fo = sb("c_fo", [P, NT, D])
        x3s = sb("c_x3s", [P, NT, D])
        junk = sb("c_junk", [P, NT, D])
        ags = sb("c_ags", [P, NT])

        w_in = sem("c_w_in")
        prep = sem("c_prep")
        pool_prep = sem("c_pool_prep")
        tern_ready = sem("c_tern_ready")
        tern_turned = sem("c_tern_turned")
        rows_done = sem("c_rows_done")
        rows_read = sem("c_rows_read")
        ternt_ready = sem("c_ternt_ready")
        ln_steps = sem("c_ln_steps")
        var_done = sem("c_var_done")
        rstd_done = sem("c_rstd_done")
        xn_done = sem("c_xn_done")
        x_turned = sem("c_x_turned")
        hi_done = sem("c_hi_done")
        lo_done = sem("c_lo_done")
        had_done = sem("c_had_done")
        q_steps = sem("c_q_steps")
        scaled = sem("c_scaled")
        inv_done = sem("c_inv_done")
        q_done = sem("c_q_done")
        q_turned = sem("c_q_turned")
        qt_done = sem("c_qt_done")
        ff_done = sem("c_ff_done")
        fo_done = sem("c_fo_done")
        fw_done = sem("c_fw_done")
        h2_done = sem("c_h2_done")
        ln3_steps = sem("c_ln3_steps")
        var3_done = sem("c_var3_done")
        rstd3_done = sem("c_rstd3_done")
        x3_done = sem("c_x3_done")
        ag_done = sem("c_ag_done")
        asum_done = sem("c_asum_done")
        acol_done = sem("c_acol_done")
        w_rounded = sem("c_w_rounded")

        def tiles(k):
            return ps[:, k:k + 2, :].rearrange("p k c -> p (k c)")[:, 0:NT * D].rearrange(
                "p (t f) -> p t f", t=NT)

        q_turn = ps[:, 4, :].bitcast(BF16)

        def part_of(w, b):
            n = NJ * 2 * HE // B
            return w[:, :, b * n:(b + 1) * n] if isinstance(b, int) else w[:, :, bass.ds(b * n, n)]

        block = ctx.enter_context(nc.Block())

        @block.sync
        def _(sp):
            for n, t in (("hadamard", hraw), ("ffn_w", wf), ("Wq1", wq1)):
                sp.dma_start(t[:], ins[n].rearrange("(c p) n -> p c n", p=P)).then_inc(w_in, 16)
            for c in range(FC):
                sp.dma_start(w1c[:, c:c + 1], ins["w_conv1"].rearrange("(c p a) -> c p a", p=P, a=1)[c]
                             ).then_inc(w_in, 16)
            for n, t in (("Wk1_t", g["wk_t"]), ("Wv1", g["wv"]), ("Wv1_t", g["wv_t"]), ("gate_t", g["gate"])):
                sp.dma_start(t[:], ins[n].rearrange("(c p) n -> p c n", p=P)).then_inc(w_in, 16)
            sp.wait_ge(w_in, 16 * (7 + FC))

        @block.tensor
        def _(pe):
            pe.wait_ge(tern_ready, 1)
            for ic in range(FC):
                for oc in range(FC):
                    mm = nc.tensor.transpose(q_turn[:, ic * D + oc * P:ic * D + oc * P + P],
                                             tern[:, oc, ic * P:(ic + 1) * P], identb[:])
            mm.then_inc(tern_turned, 1)
            pe.wait_ge(pool_prep, 3)
            for oc in range(FC):
                nc.tensor.matmul(ps[:, 7, oc * P:(oc + 1) * P], ones[:], diag[:, oc, :], start=True, stop=True)
            for c in range(FC):
                mm = nc.tensor.matmul(ps[:, 6, 0:D], w1b[:, c, :], wq1[:, c, :], start=c == 0, stop=c == FC - 1)
            mm.then_inc(rows_done, 1)
            pe.wait_ge(rows_read, 2)

            def turn_x(b):
                pe.wait_ge(xn_done, b + 1)
                ge(pe, hi_done, b)
                ge(pe, lo_done, b)
                for fc in range(FC):
                    for t in range(NT):
                        mm = nc.tensor.transpose(ps[:, fc, t * P:(t + 1) * P],
                                                 xn[:, t, fc * P:(fc + 1) * P], ident[:])
                mm.then_inc(x_turned, 1)

            def rotate(b):
                pe.wait_ge(hi_done, b + 1)
                pe.wait_ge(lo_done, b + 1)
                ge(pe, q_done, b)
                for t in range(NT):
                    for fc in range(FC):
                        for n, x in enumerate((x_hi, x_lo)):
                            mm = nc.tensor.matmul(tiles(2)[:, t, :], x[:, fc, t * P:(t + 1) * P], had[:, fc, :],
                                                  start=fc + n == 0, stop=fc + n == 2)
                mm.then_inc(had_done, 1)

            def turn_q(b):
                pe.wait_ge(q_done, b + 1)
                ge(pe, qt_done, b)
                for fc in range(FC):
                    for t in range(NT):
                        mm = nc.tensor.transpose(q_turn[:, fc * TP + t * P:fc * TP + (t + 1) * P],
                                                 qi[:, t, fc * P:(fc + 1) * P], identb[:])
                mm.then_inc(q_turned, 1)

            def ternary(b):
                pe.wait_ge(qt_done, b + 1)
                ge(pe, fo_done, b)
                for t in range(NT):
                    for fc in range(FC):
                        mm = nc.tensor.matmul(tiles(5)[:, t, :], q_t[:, fc, t * P:(t + 1) * P], tern_t[:, fc, :],
                                              start=fc == 0, stop=fc == FC - 1)
                mm.then_inc(ff_done, 1)

            def agent_sums(b):
                pe.wait_ge(ag_done, b + 1)
                ge(pe, acol_done, b)
                for ic in range(FC):
                    for t in range(NT):
                        m = ROWS[t]
                        mm = nc.tensor.matmul(ps[:, 7, ic:ic + 1], x3s[0:m, t, ic * P:(ic + 1) * P],
                                              ags[0:m, t:t + 1], start=t == 0, stop=t == NT - 1)
                mm.then_inc(asum_done, 1)

            def step(b, s1, s2, s3, s4):
                if s2:
                    if isinstance(b, int) and b == -2:
                        pe.wait_ge(ternt_ready, 1)
                    rotate(b + 2)
                if s4:
                    agent_sums(b)
                if s2:
                    turn_q(b + 2)
                if s1:
                    turn_x(b + 3)
                if s2:
                    ternary(b + 2)

            skewed4(pe, step)

        @block.scalar
        def _(act):
            act.wait_ge(tern_turned, 1)
            nc.scalar.copy(tern_t[:], q_turn[:, 0:FC * D].rearrange("p (c f) -> p c f", c=FC)).then_inc(ternt_ready, 1)
            act.wait_ge(rows_done, 1)
            nc.scalar.copy(wrow[:], ps[:, 7, 0:D]).then_inc(rows_read, 1)
            nc.scalar.copy(ub[:], ps[:, 6, 0:D]).then_inc(rows_read, 1)
            act.wait_ge(prep, 1)

            def step(b, s1, s2, s3, s4):
                if s2:
                    act.wait_ge(inv_done, b + 3)
                    for t in range(NT):
                        last = nc.scalar.activation(qm[:, t, :], tiles(2)[:, t, :], ACT.Identity,
                                                    bias=roundc[:], scale=xinv[:, t:t + 1])
                    last.then_inc(scaled, 1)
                    act.wait_ge(q_turned, b + 3)
                    ge(act, ff_done, b + 2)
                    nc.scalar.copy(q_t[:], q_turn[:, 0:FC * TP].rearrange("p (c f) -> p c f", c=FC)
                                   ).then_inc(qt_done, 1)
                if s1:
                    act.wait_ge(x_turned, b + 4)
                    ge(act, had_done, b + 3)
                    nc.scalar.copy(x_hi[:], ps[:, 0:2, 0:TP]).then_inc(hi_done, 1)
                if s2:
                    act.wait_ge(ff_done, b + 3)
                    ge(act, h2_done, b + 2)
                    for t in range(NT):
                        last = nc.scalar.mul(fo[:, t, :], tiles(5)[:, t, :], xsc[:, t:t + 1])
                    last.then_inc(fo_done, 1)
                if s4:
                    nc.scalar.copy(part_of(g["w1_hi"], b), part_of(g["w1raw"], b)).then_inc(w_rounded, 1)

            skewed4(act, step)

        @block.vector
        def _(dve):
            dve.wait_ge(w_in, 16 * (7 + FC))
            dve.wait_ge(pool_prep, 1)
            nc.vector.memset(roundc[:], ROUND).then_inc(prep, 1)
            step = Steps(dve, prep, 1)
            nc.vector.tensor_copy(had[:], hraw[:])
            nc.vector.tensor_copy(identb[:], ident[:])
            step(nc.vector.tensor_reduce(wabs[:], wf[:], AX.X, ALU.add, apply_absolute_value=True))
            step(nc.vector.tensor_scalar(wsc[:], wabs[:], 1.0 / D, 1e-5, ALU.mult, ALU.max))
            for s, f in enumerate((0.5, -0.5)):
                last = nc.vector.tensor_scalar(wlim[:, :, s], wsc[:], f, None, ALU.mult)
            step(last)
            for c in range(FC):
                last = nc.vector.tensor_scalar(tneg[:, c, :], wf[:, c, :], wlim[:, c, 1:2], None, ALU.is_lt)
            step(last)
            for c in range(FC):
                last = nc.vector.scalar_tensor_tensor(out=tern[:, c, :], in0=wf[:, c, :], scalar=wlim[:, c, 0:1],
                                                      in1=tneg[:, c, :], op0=ALU.is_gt, op1=ALU.subtract)
            last.then_inc(tern_ready, 1)
            for c in range(FC):
                nc.vector.tensor_scalar(diag[:, c, :], ident[:], wsc[:, c:c + 1], None, ALU.mult)
                last = nc.vector.tensor_scalar(w1b[:, c, :], ones[:], w1c[:, c:c + 1], None, ALU.mult)
                last.then_inc(pool_prep, 1)
            dve.wait_ge(rows_read, 2)

            def norm_sums(b):
                step = Steps(dve, ln_steps, 2 * b)
                norm_stats(nc, dve, step, lambda t: res(g, b, t), stats, mv, ve, tick, var_done)

            def norm(b):
                dve.wait_ge(rstd_done, b + 1)
                ge(dve, x_turned, b)
                for t in range(NT):
                    last = nc.vector.tensor_scalar(xn[:, t, :], res(g, b, t), mv[:, t, 0:1], rstd[:, t, :],
                                                   ALU.subtract, ALU.mult)
                last.then_inc(xn_done, 1)

            def split_x(b):
                dve.wait_ge(hi_done, b + 1)
                nc.vector.tensor_tensor(x_lo[:], ps[:, 0:2, 0:TP], x_hi[:].bitcast(F32),
                                        ALU.subtract).then_inc(lo_done, 1)

            def scale(b):
                step = Steps(dve, q_steps, 3 * b)
                dve.wait_ge(had_done, b + 1)
                step(nc.vector.tensor_reduce(am[:], tiles(2), AX.X, ALU.max, apply_absolute_value=True))
                ge(dve, fo_done, b)
                step(nc.vector.tensor_scalar(xsc[:], am[:], 1e-5, 1.0 / ACT_POS, ALU.max, ALU.mult))
                nc.vector.reciprocal(xinv[:], xsc[:]).then_inc(inv_done, 1)

            def quantise(b):
                step = Steps(dve, q_steps, 3 * b + 2)
                dve.wait_ge(scaled, b + 1)
                step(nc.vector.tensor_scalar(qm[:], qm[:], ROUND + ACT_POS, ROUND - ACT_NEG, ALU.min, ALU.max))
                nc.vector.tensor_scalar(qi[:], qm[:], ROUND, None, ALU.subtract).then_inc(q_done, 1)

            def add(b):
                dve.wait_ge(fw_done, b + 1)
                r = hres[:, NT * b:NT * b + NT, :] if isinstance(b, int) else hres[:, bass.ds(b * NT, NT), :]
                nc.vector.tensor_tensor(r, r, fo[:], ALU.add).then_inc(h2_done, 1)

            def agent_norm_sums(b):
                step = Steps(dve, ln3_steps, 2 * b)
                dve.wait_ge(h2_done, b + 1)
                norm_stats(nc, dve, step, lambda t: res(g, b, t), stats3, mv3, ve3, tick, var3_done)

            def agents(b):
                dve.wait_ge(rstd3_done, b + 1)
                ge(dve, asum_done, b)
                for t in range(NT):
                    last = nc.vector.tensor_scalar(x3s[:, t, :], res(g, b, t), mv3[:, t, 0:1], rstd3[:, t, :],
                                                   ALU.subtract, ALU.mult)
                last.then_inc(x3_done, 1)
                dve.wait_ge(x3_done, b + 1)
                for t in range(NT):
                    last = nc.vector.tensor_tensor_reduce(junk[:, t, :], x3s[:, t, :], ub[:], 1.0, 0.0, ALU.mult,
                                                          ALU.add, ags[:, t:t + 1])
                last.then_inc(ag_done, 1)
                all3 = x3[:, NT * b:NT * b + NT, :] if isinstance(b, int) else x3[:, bass.ds(b * NT, NT), :]
                nc.vector.tensor_copy(all3, x3s[:])
                dve.wait_ge(ag_done, b + 1)
                a3 = g["ag"][:, NT * b:NT * b + NT] if isinstance(b, int) else g["ag"][:, bass.ds(b * NT, NT)]
                nc.vector.tensor_copy(a3, ags[:])

            def take_sums(b):
                dve.wait_ge(asum_done, b + 1)
                ac = g["acol"][:, b, :] if isinstance(b, int) else g["acol"][:, bass.ds(b, 1), :].rearrange(
                    "p a c -> p (a c)")
                nc.vector.tensor_scalar(ac, ps[:, 7, 0:FC], float(D) ** -0.5, None,
                                        ALU.mult).then_inc(acol_done, 1)

            def step(b, s1, s2, s3, s4):
                if s2:
                    scale(b + 2)
                if s1:
                    norm_sums(b + 3)
                if s2:
                    quantise(b + 2)
                if s1:
                    norm(b + 3)
                if s3:
                    agent_norm_sums(b + 1)
                if s1:
                    split_x(b + 3)
                if s4:
                    take_sums(b)
                if s3:
                    agents(b + 1)
                if s2:
                    add(b + 2)

            skewed4(dve, step)

        @block.gpsimd
        def _(pool):
            nc.gpsimd.memset(ones[:], 1.0).then_inc(pool_prep, 1)

            def step(b, s1, s2, s3, s4):
                mh = g["mhalf"][:, 0:NT].rearrange("p (t a) -> p t a", a=1)
                if s1:
                    pool.wait_ge(var_done, b + 4)
                    nc.gpsimd.tensor_tensor(rstd[:], ve[:], mh, ALU.pow).then_inc(rstd_done, 1)
                if s3:
                    pool.wait_ge(var3_done, b + 2)
                    nc.gpsimd.tensor_tensor(rstd3[:], ve3[:], mh, ALU.pow).then_inc(rstd3_done, 1)
                if s2:
                    pool.wait_ge(fo_done, b + 3)
                    wr = wrow[:].rearrange("p (a f) -> p a f", a=1).to_broadcast([P, NT, D])
                    nc.gpsimd.tensor_tensor(fo[:], fo[:], wr, ALU.mult).then_inc(fw_done, 1)
                if s4:
                    pool.wait_ge(w_rounded, b + 1)
                    nc.gpsimd.tensor_tensor(part_of(g["w1_lo"], b), part_of(g["w1raw"], b),
                                            part_of(g["w1_hi"], b).bitcast(F32), ALU.subtract)

            skewed4(pool, step)


def agent_attention(nc, g):
    with ExitStack() as ctx:
        def sb(name, shape, dt=F32):
            return ctx.enter_context(nc.sbuf_tensor(name, shape, dt))

        def sem(name):
            return ctx.enter_context(nc.semaphore(name))

        ps, hres, ident, x3 = g["ps"], g["hres"], g["ident"], g["x3"]
        sel = sb("e_sel", [B, B, P])
        mx = sb("e_mx", [B, 2])
        ex = sb("e_ex", [B, D])
        su = sb("e_su", [B, 2])
        rs = sb("e_rs", [B, 2])
        attn_t = sb("e_attn_t", [P, FC, B])
        w8 = sb("e_w8", [B, D])
        junk = sb("e_junk", [P, 4, D])
        score = sb("e_score", [P, B, NT])
        pr = sb("e_pr", [B, T])
        pt = sb("e_pt", [P, NT, B])
        px = sb("e_px", [P, FC, B])
        av = sb("e_av", [B, D])
        zero = sb("e_zero", [P, NT * B])
        tok = sb("e_tok", [P, NT * B])
        rtok = sb("e_rtok", [P, NT * B])
        sel_ready = sem("e_sel_ready")
        pe_done = sem("e_pe_done")
        act_done = sem("e_act_done")
        dve_done = sem("e_dve_done")
        scored = sem("e_scored")
        block = ctx.enter_context(nc.Block())

        @block.gpsimd
        def _(pool):
            nc.gpsimd.memset(sel[:], 0.0).then_inc(sel_ready, 1)
            pool.wait_ge(sel_ready, 1)
            nc.gpsimd.affine_select(out=sel[:], in_=sel[:], compare_op=ALU.not_equal, fill=1.0, base=0,
                                    pattern=[[-1, B], [0, P]], channel_multiplier=1).then_inc(sel_ready, 1)

        def spread(row):
            for b in range(B):
                mm = nc.tensor.matmul(ps[:, b // 2, (b % 2) * D:(b % 2) * D + D], sel[:, b, :], row[:],
                                      start=True, stop=True)
            return mm

        @block.tensor
        def _(pe):
            for c in range(FC):
                mm = nc.tensor.matmul(ps[0:B, 4, 0:D], g["acol"][:, :, c], g["wk_t"][:, c, :],
                                      start=c == 0, stop=c == FC - 1)
            mm.then_inc(pe_done, 1)
            pe.wait_ge(act_done, 1)
            for c in range(FC):
                mm = nc.tensor.transpose(ps[:, 5, c * B:(c + 1) * B], ex[:, c * P:(c + 1) * P], ident[0:B, 0:B])
            mm.then_inc(pe_done, 1)
            pe.wait_ge(dve_done, 3)
            for c in range(FC):
                mm = nc.tensor.matmul(ps[0:B, 6, 0:D], attn_t[:, c, :], g["wv"][:, c, :],
                                      start=c == 0, stop=c == FC - 1)
            mm.then_inc(pe_done, 1)
            pe.wait_ge(dve_done, 4)
            pe.wait_ge(sel_ready, 2)
            spread(w8).then_inc(pe_done, 1)
            pe.wait_ge(scored, NT * B)
            for t in range(NT):
                m = ROWS[t]
                mm = nc.tensor.transpose(ps[0:B, 7, t * P:t * P + m], score[0:m, :, t], ident[0:m, 0:m])
            mm.then_inc(pe_done, 1)
            pe.wait_ge(act_done, 2)
            for t in range(NT):
                m = ROWS[t]
                mm = nc.tensor.transpose(ps[0:m, 4, t * B:(t + 1) * B], pr[:, t * P:t * P + m], ident[0:B, 0:B])
            mm.then_inc(pe_done, 1)
            pe.wait_ge(dve_done, 7)
            for b in range(B):
                for c in range(FC):
                    for t in range(NT):
                        m = ROWS[t]
                        mm = nc.tensor.matmul(ps[:, 5, c * B + b:c * B + b + 1],
                                              x3[0:m, NT * b + t, c * P:(c + 1) * P], pt[0:m, t, b:b + 1],
                                              start=t == 0, stop=t == NT - 1)
            mm.then_inc(pe_done, 1)
            pe.wait_ge(dve_done, 8)
            for c in range(FC):
                mm = nc.tensor.matmul(ps[0:B, 6, 0:D], px[:, c, :], g["wv_t"][:, c, :],
                                      start=c == 0, stop=c == FC - 1)
            mm.then_inc(pe_done, 1)
            pe.wait_ge(dve_done, 9)
            spread(av).then_inc(pe_done, 1)

        @block.scalar
        def _(act):
            act.wait_ge(dve_done, 1)
            nc.scalar.activation(ex[:], ps[0:B, 4, 0:D], ACT.Exp, bias=mx[:, 0:1],
                                 accum_out=su[:, 0:1]).then_inc(act_done, 1)
            act.wait_ge(dve_done, 5)
            nc.scalar.activation(pr[:], ps[0:B, 7, 0:T], ACT.Exp, bias=mx[:, 1:2],
                                 accum_out=su[:, 1:2]).then_inc(act_done, 1)
            act.wait_ge(scored, NT * B + 1)
            nc.scalar.activation(tok[:], zero[:], ACT.Exp).then_inc(act_done, 1)

        @block.vector
        def _(dve):
            dve.wait_ge(pe_done, 1)
            nc.vector.tensor_reduce(mx[:, 0:1], ps[0:B, 4, 0:D], AX.X, ALU.max, negate=True).then_inc(dve_done, 1)
            dve.wait_ge(act_done, 1)
            nc.vector.reciprocal(rs[:, 0:1], su[:, 0:1]).then_inc(dve_done, 1)
            dve.wait_ge(pe_done, 2)
            nc.vector.tensor_copy(attn_t[:].rearrange("p c b -> p (c b)"), ps[:, 5, 0:FC * B]).then_inc(dve_done, 1)
            dve.wait_ge(pe_done, 3)
            dve.wait_ge(dve_done, 2)
            nc.vector.tensor_scalar(w8[:], ps[0:B, 6, 0:D], rs[:, 0:1], None, ALU.mult).then_inc(dve_done, 1)
            dve.wait_ge(pe_done, 4)
            for b in range(B):
                for t in range(NT):
                    i = NT * b + t
                    if i >= 4:
                        dve.wait_ge(scored, i - 3)
                    nc.vector.tensor_tensor_reduce(junk[:, i % 4, :], x3[:, i, :],
                                                   ps[:, b // 2, (b % 2) * D:(b % 2) * D + D], 1.0, 0.0,
                                                   ALU.mult, ALU.add, score[:, b, t:t + 1]).then_inc(scored, 1)
            nc.vector.tensor_tensor(zero[:], g["ag"][:], g["ag"][:], ALU.subtract).then_inc(scored, 1)
            dve.wait_ge(pe_done, 5)
            nc.vector.tensor_reduce(mx[:, 1:2], ps[0:B, 7, 0:T], AX.X, ALU.max, negate=True).then_inc(dve_done, 1)
            dve.wait_ge(act_done, 2)
            nc.vector.reciprocal(rs[:, 1:2], su[:, 1:2]).then_inc(dve_done, 1)
            dve.wait_ge(pe_done, 6)
            for t in range(NT):
                m = ROWS[t]
                last = nc.vector.tensor_copy(pt[0:m, t, :], ps[0:m, 4, t * B:(t + 1) * B])
            last.then_inc(dve_done, 1)
            dve.wait_ge(pe_done, 7)
            nc.vector.tensor_copy(px[:].rearrange("p c b -> p (c b)"), ps[:, 5, 0:FC * B]).then_inc(dve_done, 1)
            dve.wait_ge(pe_done, 8)
            dve.wait_ge(dve_done, 6)
            nc.vector.tensor_scalar(av[:], ps[0:B, 6, 0:D], rs[:, 1:2], None, ALU.mult).then_inc(dve_done, 1)
            dve.wait_ge(act_done, 3)
            nc.vector.reciprocal(rtok[:], tok[:]).then_inc(dve_done, 1)
            dve.wait_ge(dve_done, 10)
            nc.vector.tensor_tensor(tok[:], tok[:], rtok[:], ALU.mult).then_inc(dve_done, 1)
            dve.wait_ge(dve_done, 11)
            dve.wait_ge(pe_done, 9)
            for b in range(B):
                for t in range(NT):
                    i = NT * b + t
                    m = ROWS[t]
                    nc.vector.scalar_tensor_tensor(out=hres[0:m, i, :],
                                                   in0=ps[0:m, b // 2, (b % 2) * D:(b % 2) * D + D],
                                                   scalar=tok[0:m, i:i + 1], in1=hres[0:m, i, :],
                                                   op0=ALU.mult, op1=ALU.add)


def phase_cd(nc, g, ins, out):
    with ExitStack() as ctx:
        def sb(name, shape, dt=F32):
            return ctx.enter_context(nc.sbuf_tensor(name, shape, dt))

        g["w1_hi"] = sb("w1_hi", [P, FC, NJ * 2 * HE], F32R)
        g["w1_lo"] = sb("w1_lo", [P, FC, NJ * 2 * HE], F32R)
        g["gate"] = sb("gate", [P, FC, E])
        with ExitStack() as agent:
            def sba(name, shape, dt=F32):
                return agent.enter_context(nc.sbuf_tensor(name, shape, dt))

            g["x3"] = sba("x3", [P, NT * B, D])
            g["ag"] = sba("ag", [P, NT * B])
            g["acol"] = sba("acol", [P, B, FC])
            g["wk_t"] = sba("wk_t", [P, FC, D])
            g["wv"] = sba("wv", [P, FC, D])
            g["wv_t"] = sba("wv_t", [P, FC, D])
            feed_forward(nc, g, ins)
            agent_attention(nc, g)
        experts(nc, g, out)


NB = (2 * B * T + E * (P - 1)) // P
NB += NB % 2
NI = NT * B


def top_two(nc, step, score, bufs):
    n = score.shape[1]
    mx, ex, p, c, one, two, rank = bufs

    def over(t):
        return t[:].to_broadcast([P, n, E])

    step(nc.vector.tensor_reduce(mx[:, :, 0], score, AX.X, ALU.max))
    step(nc.vector.tensor_tensor(ex[:], score, over(mx), ALU.subtract))
    yield
    step(nc.vector.tensor_reduce(mx[:, :, 0], p[:], AX.X, ALU.add))
    step(nc.vector.reciprocal(mx[:, :, 0], mx[:, :, 0]))
    step(nc.vector.tensor_tensor(p[:], p[:], over(mx), ALU.mult))
    for k, pick in enumerate((one, two)):
        step(nc.vector.tensor_reduce(mx[:, :, 0], p[:] if k == 0 else ex[:], AX.X, ALU.max))
        step(nc.vector.tensor_tensor(c[:], p[:] if k == 0 else ex[:], over(mx), ALU.is_equal))
        step(nc.vector.tensor_tensor(c[:], c[:], rank[:], ALU.mult))
        step(nc.vector.tensor_reduce(mx[:, :, 0], c[:], AX.X, ALU.max))
        step(nc.vector.tensor_tensor(pick[:], c[:], over(mx), ALU.is_equal))
        if k == 0:
            step(nc.vector.scalar_tensor_tensor(out=ex[:], in0=one[:], scalar=-2.0, in1=p[:],
                                                op0=ALU.mult, op1=ALU.add))


def shared_expert(nc, g):
    with ExitStack() as ctx:
        def sb(name, shape, dt=F32):
            return ctx.enter_context(nc.sbuf_tensor(name, shape, dt))

        def sem(name):
            return ctx.enter_context(nc.semaphore(name))

        ps, ident = g["ps"], g["ident"]
        w1_hi, w1_lo, ws2 = g["w1_hi"], g["w1_lo"], g["ws2"]
        NC = HS // P
        stats = sb("d_stats", [P, NT, 6])
        mv = sb("d_mv", [P, NT, 2])
        ve = sb("d_ve", [P, NT, 1])
        rstd = sb("d_rstd", [P, NT, 1])
        tick = sb("d_tick", [P, 1])
        xn = sb("d_xn", [P, NT, D])
        x_hi = sb("d_x_hi", [P, FC, TP], F32R)
        x_lo = sb("d_x_lo", [P, FC, TP], F32R)
        g_hi = sb("d_g_hi", [P, FC, E], F32R)
        g_lo = sb("d_g_lo", [P, FC, E], F32R)
        si = sb("d_si", [P, NC, T])
        ht = sb("d_ht", [P, NC, T])
        sct = sb("d_sct", [E, TP])

        g_steps = sem("d_g_steps")
        padded = sem("d_padded")
        ln_steps = sem("d_ln_steps")
        var_done = sem("d_var_done")
        rstd_done = sem("d_rstd_done")
        xn_done = sem("d_xn_done")
        x_turned = sem("d_x_turned")
        hi_done = sem("d_hi_done")
        lo_done = sem("d_lo_done")
        h_done = sem("d_h_done")
        silu_done = sem("d_silu_done")
        ht_done = sem("d_ht_done")
        score_done = sem("d_score_done")
        sct_done = sem("d_sct_done")
        z_done = sem("d_z_done")
        z_read = sem("d_z_read")
        stored = sem("d_stored")

        block = ctx.enter_context(nc.Block())

        @block.sync
        def _(sp):
            def store(b):
                sp.wait_ge(xn_done, b + 1)
                rows = g["x_rows"][bass.ds(b * TP, TP)] if not isinstance(b, int) else g["x_rows"][b * TP:(b + 1) * TP]
                sp.dma_start(rows.rearrange("(t p) f -> p t f", p=P), xn[:]).then_inc(stored, 16)

            store(0)
            with sp.Fori(1, B) as b:
                store(b)
            sp.wait_ge(stored, 16 * B)

        @block.tensor
        def _(pe):
            pe.wait_ge(g_steps, 2)
            pe.wait_ge(padded, 1)

            def turn_x(b):
                pe.wait_ge(xn_done, b + 1)
                ge(pe, lo_done, b)
                for fc in range(FC):
                    for t in range(NT):
                        mm = nc.tensor.transpose(ps[:, fc, t * P:(t + 1) * P],
                                                 xn[:, t, fc * P:(fc + 1) * P], ident[:])
                mm.then_inc(x_turned, 1)

            def hidden(b, i):
                if i == 0:
                    pe.wait_ge(lo_done, b + 1)
                    ge(pe, ht_done, NC * b)
                elif i == 1:
                    ge(pe, sct_done, b)
                else:
                    pe.wait_ge(ht_done, NC * b + i - 1)
                for gate in range(2):
                    col = E * 2 * HE + gate * HS + i * P
                    for fc in range(FC):
                        mm = split_products(nc, ps[:, 2 + 2 * (i % 2) + gate, 0:T], w1_hi[:, fc, col:col + P],
                                            w1_lo[:, fc, col:col + P], x_hi[:, fc, 0:T], x_lo[:, fc, 0:T],
                                            fc == 0, fc == FC - 1)
                mm.then_inc(h_done, 1)

            def scores(b):
                pe.wait_ge(ht_done, NC * b + 2)
                for fc in range(FC):
                    mm = split_products(nc, ps[0:E, 5, 0:T], g_hi[:, fc, :], g_lo[:, fc, :],
                                        x_hi[:, fc, 0:T], x_lo[:, fc, 0:T], fc == 0, fc == FC - 1)
                mm.then_inc(score_done, 1)

            def output(b):
                for t in range(NT):
                    if t != 1:
                        ge(pe, z_read, 2 * b - 1 + t // 2)
                    if t == 2:
                        pe.wait_ge(sct_done, b + 1)
                    m = ROWS[t]
                    for i in range(NC):
                        if t == 0:
                            pe.wait_ge(ht_done, NC * b + i + 1)
                        mm = nc.tensor.matmul(ps[0:m, 6 + t // 2, (t % 2) * D:(t % 2) * D + D],
                                              ht[:, i, t * P:t * P + m], ws2[:, i, :],
                                              start=i == 0, stop=i == NC - 1)
                    if t == 1:
                        mm.then_inc(z_done, 1)
                for t in range(NT):
                    mm = nc.tensor.transpose(ps[:, 7, D + t * E:D + (t + 1) * E], sct[:, t * P:(t + 1) * P],
                                             ident[0:E, 0:E])
                mm.then_inc(z_done, 1)

            def step(b, s1, s2, s3):
                if s3:
                    for i in range(NC):
                        hidden(b, i)
                    scores(b)
                if s2:
                    turn_x(b + 1)
                if s3:
                    output(b)

            skewed(pe, step)

        @block.scalar
        def _(act):
            def step(b, s1, s2, s3):
                if s3:
                    for i in range(NC):
                        act.wait_ge(h_done, NC * b + i + 1)
                        nc.scalar.activation(si[:, i, :], ps[:, 3 + 2 * (i % 2), 0:T],
                                             ACT.Silu).then_inc(silu_done, 1)
                if s3:
                    act.wait_ge(score_done, b + 1)
                    nc.scalar.copy(sct[:, 0:T], ps[0:E, 5, 0:T]).then_inc(sct_done, 1)
                if s2:
                    act.wait_ge(x_turned, b + 2)
                    nc.scalar.copy(x_hi[:], ps[:, 0:2, 0:TP]).then_inc(hi_done, 1)

            skewed(act, step)

        @block.vector
        def _(dve):
            nc.vector.memset(sct[:, T:TP], 0.0).then_inc(padded, 1)
            nc.vector.tensor_copy(g_hi[:], g["gate"][:]).then_inc(g_steps, 1)
            dve.wait_ge(g_steps, 1)
            nc.vector.tensor_tensor(g_lo[:], g["gate"][:], g_hi[:].bitcast(F32), ALU.subtract).then_inc(g_steps, 1)

            def norm(b):
                step = Steps(dve, ln_steps, 2 * b)
                norm_stats(nc, dve, step, lambda t: res(g, b, t), stats, mv, ve, tick, var_done)
                dve.wait_ge(rstd_done, b + 1)
                ge(dve, stored, 16 * b)
                ge(dve, x_turned, b)
                for t in range(NT):
                    last = nc.vector.tensor_scalar(xn[:, t, :], res(g, b, t), mv[:, t, 0:1], rstd[:, t, :],
                                                   ALU.subtract, ALU.mult)
                last.then_inc(xn_done, 1)

            def split_x(b):
                dve.wait_ge(hi_done, b + 1)
                nc.vector.tensor_tensor(x_lo[:], ps[:, 0:2, 0:TP], x_hi[:].bitcast(F32),
                                        ALU.subtract).then_inc(lo_done, 1)

            def gated(b):
                for i in range(NC):
                    dve.wait_ge(silu_done, NC * b + i + 1)
                    nc.vector.tensor_tensor(ht[:, i, :], ps[:, 2 + 2 * (i % 2), 0:T], si[:, i, :],
                                            ALU.mult).then_inc(ht_done, 1)

            def take(b):
                for t in range(NT):
                    if t != 1:
                        dve.wait_ge(z_done, 2 * b + 1 + t // 2)
                    r = res(g, b, t)[0:ROWS[t]]
                    add = nc.vector.tensor_tensor(r, ps[0:ROWS[t], 6 + t // 2, (t % 2) * D:(t % 2) * D + D],
                                                  r, ALU.add)
                    if t == 1:
                        add.then_inc(z_read, 1)
                sc = g["score"][:, NT * b:NT * b + NT, :] if isinstance(b, int) else (
                    g["score"][:, bass.ds(b * NT, NT), :])
                nc.vector.tensor_copy(sc, ps[:, 7, D:D + NT * E].rearrange("p (t e) -> p t e", t=NT)
                                      ).then_inc(z_read, 1)

            def step(b, s1, s2, s3):
                if s3:
                    gated(b)
                if s2:
                    split_x(b + 1)
                if s1:
                    norm(b + 2)
                if s3:
                    take(b)

            skewed(dve, step)

        @block.gpsimd
        def _(pool):
            def step(b, s1, s2, s3):
                if s1:
                    pool.wait_ge(var_done, b + 3)
                    nc.gpsimd.tensor_tensor(rstd[:], ve[:], g["mhalf"][:, 0:NT].rearrange("p (t a) -> p t a", a=1),
                                            ALU.pow).then_inc(rstd_done, 1)

            skewed(pool, step)


def route(nc, g):
    with ExitStack() as ctx:
        def sb(name, shape, dt=F32):
            return ctx.enter_context(nc.sbuf_tensor(name, shape, dt))

        def sem(name):
            return ctx.enter_context(nc.semaphore(name))

        ps = g["ps"]
        mx = sb("r_mx", [P, NI, 1])
        ex = sb("r_ex", [P, NI, E])
        pr = sb("r_pr", [P, NI, E])
        cc = sb("r_cc", [P, NI, E])
        pick = [sb("r_one", [P, NI, E]), sb("r_two", [P, NI, E])]
        rank = sb("r_rank", [P, NI, E])
        valid = sb("r_valid", [P, NI, 1])
        both = sb("r_both", [P, NI, E])
        upper = sb("r_upper", [P, P])
        ones = sb("r_ones", [P, P])
        cnt = sb("r_cnt", [P, E, NI])
        cum = sb("r_cum", [P, E, NI])
        keep = sb("r_keep", [P, E, NI])
        nblk = sb("r_nblk", [P, E])
        bend = sb("r_bend", [P, E])
        base = sb("r_base", [P, E])
        slot = sb("r_slot", [P, NI, E])
        sk = sb("r_sk", [P, 2, NI])
        blk = sb("r_blk", [P, 2, NI])
        row = sb("r_row", [P, 2, NI])
        wk = sb("r_wk", [P, 2, NI])
        src = sb("r_src", [P, NI])
        dst = sb("r_dst", [P, 2, NI])
        cols = sb("r_cols", [P, P])
        pads = sb("r_pads", [P, 1])
        hot = sb("r_hot", [P, 2 * NI, P])
        one = sb("r_isblk", [P, 2 * NI, NB])
        val = sb("r_val", [P, 2 * NI, 3, NB])
        found = sb("r_found", [P, 3 * NB])
        isp = sb("r_isp", [P, NB])
        bex = sb("r_bex", [P, NB])

        const = sem("r_const")
        steps = sem("r_steps")
        exp_done = sem("r_exp_done")
        both_done = sem("r_both_done")
        pre_done = sem("r_pre_done")
        hot_done = sem("r_hot_done")
        placed = sem("r_placed")
        one_done = sem("r_one_done")
        val_done = sem("r_val_done")
        PART = 2 * NI // 6
        block = ctx.enter_context(nc.Block())

        @block.gpsimd
        def _(pool):
            for e in range(E):
                nc.gpsimd.memset(rank[:, :, e:e + 1], float(E - e))
            nc.gpsimd.memset(ones[:], 1.0)
            nc.gpsimd.iota(cols[:], [[1, P]], base=0, channel_multiplier=0, allow_small_or_imprecise_dtypes=True)
            nc.gpsimd.iota(src[:], [[P, NI]], base=0, channel_multiplier=1, allow_small_or_imprecise_dtypes=True)
            for k in range(2):
                nc.gpsimd.iota(dst[:, k, :], [[2 * P, NI]], base=k + 1, channel_multiplier=2,
                               allow_small_or_imprecise_dtypes=True)
            nc.gpsimd.iota(pads[:], [[0, 1]], base=2 * P * NI + 1, channel_multiplier=1,
                           allow_small_or_imprecise_dtypes=True)
            nc.gpsimd.memset(valid[:], 1.0)
            nc.gpsimd.memset(keep[:], 1.0)
            nc.gpsimd.memset(upper[:], 1.0).then_inc(const, 1)
            pool.wait_ge(const, 1)
            nc.gpsimd.affine_select(out=upper[:], in_=upper[:], compare_op=ALU.is_gt, fill=0.0, base=0,
                                    pattern=[[1, P]], channel_multiplier=-1).then_inc(const, 1)
            vt = valid[:].rearrange("p (b t) a -> p b (t a)", t=NT)[:, :, NT - 1:NT]
            nc.gpsimd.affine_select(out=vt, in_=vt, compare_op=ALU.is_gt, fill=0.0, base=TXT,
                                    pattern=[[0, B], [0, 1]], channel_multiplier=-1).then_inc(const, 1)
            for e in range(E):
                ms = nc.gpsimd.memset(keep[:, e, 0:1], 0.0)
            ms.then_inc(const, 1)
            pool.wait_ge(one_done, 1)
            nc.gpsimd.tensor_tensor(val[:, :, 2, :], one[:],
                                    wk[:].rearrange("p k (i a) -> p (k i) a", a=1).to_broadcast([P, 2 * NI, NB]),
                                    ALU.mult).then_inc(val_done, 1)

        @block.scalar
        def _(act):
            act.wait_ge(steps, 2)
            nc.scalar.activation(pr[:], ex[:], ACT.Exp).then_inc(exp_done, 1)

        @block.tensor
        def _(pe):
            pe.wait_ge(both_done, 1)
            m = both[:].rearrange("p i e -> p (i e)")
            nc.tensor.matmul(ps[:, 0, 0:NI * E], upper[:], m, start=True, stop=True)
            nc.tensor.matmul(ps[:, 1, 0:NI * E], ones[:], m, start=True, stop=True).then_inc(pre_done, 1)
            pe.wait_ge(val_done, 3)
            for n in range(2 * NI):
                if n % PART == 0:
                    pe.wait_ge(hot_done, n // PART + 1)
                mm = nc.tensor.matmul(ps[:, 2, 0:3 * NB], hot[:, n, :], val[:, n].rearrange("p c j -> p (c j)"),
                                      start=n == 0, stop=n == 2 * NI - 1)
            mm.then_inc(placed, 1)

        @block.vector
        def _(dve):
            dve.wait_ge(const, 4)
            step = Steps(dve, steps, 0)
            V = nc.vector

            def whole(out_, in_):
                step(V.tensor_scalar(out_, in_, 1.0 / P, 0.5 / P - 0.5, ALU.mult, ALU.add))
                step(V.tensor_scalar(out_, out_, ROUND, None, ALU.add))
                step(V.tensor_scalar(out_, out_, ROUND, None, ALU.subtract))

            choose = top_two(nc, step, g["score"][:], (mx, ex, pr, cc, *pick, rank))
            next(choose)
            dve.wait_ge(exp_done, 1)
            for _ in choose:
                pass
            over = valid[:].to_broadcast([P, NI, E])
            for k in range(2):
                step(V.tensor_tensor(pick[k][:], pick[k][:], over, ALU.mult))
            V.tensor_tensor(both[:], pick[0][:], pick[1][:], ALU.add).then_inc(both_done, 1)
            for k in range(2):
                step(V.tensor_tensor(cc[:], pick[k][:], pr[:], ALU.mult))
                step(V.tensor_reduce(wk[:, k, :], cc[:], AX.X, ALU.add))
            dve.wait_ge(pre_done, 1)
            step(V.tensor_copy(cnt[:], ps[:, 1, 0:NI * E].rearrange("p (i e) -> p e i", e=E)))
            step(V.tensor_tensor_scan(cum[:].rearrange("p e i -> p (e i)"), keep[:].rearrange("p e i -> p (e i)"),
                                      cnt[:].rearrange("p e i -> p (e i)"), 0.0, ALU.mult, ALU.add))
            step(V.tensor_scalar(nblk[:], cum[:, :, NI - 1], float(P - 1), None, ALU.add))
            whole(nblk[:], nblk[:])
            step(V.tensor_tensor_scan(bend[:], ones[:, 0:E], nblk[:], 0.0, ALU.mult, ALU.add))
            step(V.tensor_tensor(base[:], bend[:], nblk[:], ALU.subtract))
            step(V.tensor_scalar(base[:], base[:], float(P), None, ALU.mult))
            step(V.tensor_tensor(cum[:], cum[:], cnt[:], ALU.subtract))
            step(V.tensor_tensor(cum[:], cum[:], base[:].rearrange("p (e a) -> p e a", a=1).to_broadcast([P, E, NI]),
                                 ALU.add))
            step(V.tensor_tensor(slot[:], ps[:, 0, 0:NI * E].rearrange("p (i e) -> p i e", e=E),
                                 cum[:].rearrange("p e i -> p i e"), ALU.add))
            for k in range(2):
                step(V.tensor_tensor(cc[:], pick[k][:], slot[:], ALU.mult))
                step(V.tensor_reduce(sk[:, k, :], cc[:], AX.X, ALU.add))
            whole(blk[:], sk[:])
            step(V.scalar_tensor_tensor(out=row[:], in0=blk[:], scalar=-float(P), in1=sk[:],
                                        op0=ALU.mult, op1=ALU.add))
            for k in range(2):
                step(V.scalar_tensor_tensor(out=blk[:, k, :], in0=blk[:, k, :], scalar=1.0, in1=valid[:, :, 0],
                                            op0=ALU.add, op1=ALU.mult))
            step(V.tensor_scalar(blk[:], blk[:], -1.0, None, ALU.add))
            def over(t, n):
                return t.rearrange("p k (i a) -> p (k i) a", a=1).to_broadcast([P, 2 * NI, n])

            blocks = cols[:, 0:NB].rearrange("p (a j) -> p a j", a=1).to_broadcast([P, 2 * NI, NB])
            rows = cols[:].rearrange("p (a j) -> p a j", a=1).to_broadcast([P, PART, P])
            V.tensor_tensor(one[:], blocks, over(blk[:], NB), ALU.is_equal).then_inc(one_done, 1)
            dve.wait_ge(one_done, 1)
            for k in range(2):
                last = V.tensor_tensor(val[:, k * NI:(k + 1) * NI, 0, :], one[:, k * NI:(k + 1) * NI, :],
                                       src[:].rearrange("p (i a) -> p i a", a=1).to_broadcast([P, NI, NB]),
                                       ALU.mult)
            last.then_inc(val_done, 1)
            V.tensor_tensor(val[:, :, 1, :], one[:], over(dst[:], NB), ALU.mult).then_inc(val_done, 1)
            for n in range(0, 2 * NI, PART):
                V.tensor_tensor(hot[:, n:n + PART, :], rows,
                                row[:].rearrange("p k (i a) -> p (k i) a", a=1)[:, n:n + PART].to_broadcast(
                                    [P, PART, P]), ALU.is_equal).then_inc(hot_done, 1)
            step(V.tensor_scalar(bex[:], cols[:, 0:NB], bend[:, 0:1], None, ALU.is_ge))
            for e in range(1, E - 1):
                step(V.scalar_tensor_tensor(out=bex[:], in0=cols[:, 0:NB], scalar=bend[:, e:e + 1], in1=bex[:],
                                            op0=ALU.is_ge, op1=ALU.add))
            step(V.tensor_copy(g["bex_i"][:], bex[:]))
            dve.wait_ge(placed, 1)
            step(V.tensor_copy(found[:], ps[:, 2, 0:3 * NB]))
            step(V.tensor_copy(g["src_i"][:], found[:, 0:NB]))
            step(V.tensor_copy(g["w_slot"][:], found[:, 2 * NB:3 * NB]))
            step(V.tensor_scalar(isp[:], found[:, NB:2 * NB], 0.0, pads[:], ALU.is_equal, ALU.mult))
            step(V.scalar_tensor_tensor(out=isp[:], in0=found[:, NB:2 * NB], scalar=-1.0, in1=isp[:],
                                        op0=ALU.add, op1=ALU.add))
            step(V.tensor_copy(g["dst_i"][:], isp[:]))


def paired(eng, step, depth):
    total = NB + depth - 1
    first = depth + (depth % 2)

    def run(j, u):
        on = [True] * depth if not isinstance(j, int) else [0 <= j - s < NB for s in range(depth)]
        step(j, u, on)

    for j in range(first):
        run(j, j % 2)
    with eng.Fori(first // 2, NB // 2) as i:
        for u in range(2):
            run(2 * i + u, u)
    for j in range(NB, total):
        run(j, j % 2)


def expert_blocks(nc, g):
    with ExitStack() as ctx:
        def sb(name, shape, dt=F32):
            return ctx.enter_context(nc.sbuf_tensor(name, shape, dt))

        def sem(name):
            return ctx.enter_context(nc.semaphore(name))

        ps, ident = g["ps"], g["ident"]
        w1_hi, w1_lo, w2 = g["w1_hi"], g["w1_lo"], g["w2"]
        idx = [sb(f"f_idx{u}", [P, 1], U32) for u in range(2)]
        odx = [sb(f"f_odx{u}", [P, 1], U32) for u in range(2)]
        xg = [sb(f"f_xg{u}", [P, D]) for u in range(2)]
        yo = [sb(f"f_yo{u}", [P, D]) for u in range(2)]
        x_hi = sb("f_x_hi", [P, 2, D], F32R)
        x_lo = sb("f_x_lo", [P, 2, D], F32R)
        si = sb("f_si", [P, 2, HE])
        hg = sb("f_hg", [P, 2, 2 * P])
        ht = sb("f_ht", [HE // 2, 2, 2, P])
        tick = sb("f_tick", [P, 2])

        idx_set = sem("f_idx_set")
        odx_set = sem("f_odx_set")
        gathered = [sem(f"f_gathered{u}") for u in range(2)]
        scattered = [sem(f"f_scattered{u}") for u in range(2)]
        x_turned = sem("f_x_turned")
        hi_done = sem("f_hi_done")
        lo_done = sem("f_lo_done")
        h_done = sem("f_h_done")
        silu_done = sem("f_silu_done")
        hg_done = sem("f_hg_done")
        h_turned = sem("f_h_turned")
        ht_done = sem("f_ht_done")
        z_done = sem("f_z_done")
        yo_done = sem("f_yo_done")
        tick_set = sem("f_tick_set")

        DEPTH = 6
        block = ctx.enter_context(nc.Block())

        def half(j, u):
            return j // 2 if isinstance(j, int) else (j - u) // 2

        @block.tensor
        def _(pe):
            def turn_x(j, u):
                pe.wait_ge(gathered[u], 8 * (j - u) + 16)
                ge(pe, lo_done, j - 1)
                for fc in range(FC):
                    mm = nc.tensor.transpose(ps[:, u, fc * P:(fc + 1) * P], xg[u][:, fc * P:(fc + 1) * P], ident[:])
                mm.then_inc(x_turned, 1)

            def hidden(j, u, e):
                pe.wait_ge(lo_done, j + 1)
                ge(pe, hg_done, j - 1)
                for fc in range(FC):
                    cols = bass.ds(e * (2 * HE), 2 * HE)
                    rows = slice(fc * P, (fc + 1) * P)
                    mm = split_products(nc, ps[:, 2 + u, 0:2 * HE], x_hi[:, u, rows], x_lo[:, u, rows],
                                        w1_hi[:, fc, cols], w1_lo[:, fc, cols], fc == 0, fc == FC - 1)
                mm.then_inc(h_done, 1)

            def turn(j, u):
                pe.wait_ge(hg_done, j + 1)
                ge(pe, ht_done, j - 1)
                for k in range(2):
                    mm = nc.tensor.transpose(ps[0:HE // 2, 4 + u, k * P:(k + 1) * P],
                                             hg[:, u, k * P:k * P + HE // 2], ident[:])
                mm.then_inc(h_turned, 1)

            def second(j, u, e):
                pe.wait_ge(ht_done, j + 1)
                ge(pe, yo_done, j - 1)
                for k in range(2):
                    mm = nc.tensor.matmul(ps[:, 6 + u, 0:D], ht[:, u, k, :],
                                          w2[:, k, bass.ds(e, 1), :].rearrange("p a f -> p (a f)"),
                                          start=k == 0, stop=k == 1)
                mm.then_inc(z_done, 1)

            def expert(j):
                at = g["bex_i"][0:1, j:j + 1] if isinstance(j, int) else g["bex_i"][0:1, bass.ds(j, 1)]
                return pe.value_load(at, min_val=0, max_val=E - 1)

            def step(j, u, on):
                v = 1 - u
                hidden_of = expert(j - 2) if on[2] else None
                output_of = expert(j - 4) if on[4] else None
                if on[2]:
                    hidden(j - 2, u, hidden_of)
                if on[1]:
                    turn_x(j - 1, v)
                if on[4]:
                    second(j - 4, u, output_of)
                if on[3]:
                    turn(j - 3, v)

            paired(pe, step, DEPTH)

        @block.scalar
        def _(act):
            def step(j, u, on):
                v = 1 - u
                if on[2]:
                    act.wait_ge(h_done, j - 1)
                    ge(act, hg_done, j - 3)
                    nc.scalar.activation(si[:, u, :], ps[:, 2 + u, HE:2 * HE], ACT.Silu).then_inc(silu_done, 1)
                if on[1]:
                    act.wait_ge(x_turned, j)
                    ge(act, h_done, j - 2)
                    nc.scalar.copy(x_hi[:, v, :], ps[:, v, 0:D]).then_inc(hi_done, 1)
                if on[4]:
                    act.wait_ge(z_done, j - 3)
                    ge(act, scattered[u], 8 * (j - 4 - u))
                    nc.scalar.copy(yo[u][:], ps[:, 6 + u, 0:D]).then_inc(yo_done, 1)
                if on[3]:
                    act.wait_ge(h_turned, j - 2)
                    ge(act, z_done, j - 4)
                    nc.scalar.copy(ht[:, v].rearrange("p k m -> p (k m)"), ps[0:HE // 2, 4 + v, 0:2 * P]
                                   ).then_inc(ht_done, 1)

            paired(act, step, DEPTH)

        @block.vector
        def _(dve):
            def column(t, j):
                return t[:, j:j + 1] if isinstance(j, int) else t[:, bass.ds(j, 1)]

            def step(j, u, on):
                v = 1 - u
                if on[0]:
                    ge(dve, gathered[u], 8 * (j - u))
                    nc.vector.tensor_copy(idx[u][:], column(g["src_i"], j)).then_inc(idx_set, 1)
                if on[2]:
                    dve.wait_ge(silu_done, j - 1)
                    ge(dve, h_turned, j - 3)
                    nc.vector.scalar_tensor_tensor(
                        out=hg[:, u, :].rearrange("p (k m) -> p k m", k=2)[:, :, 0:HE // 2],
                        in0=ps[:, 2 + u, 0:HE].rearrange("p (k m) -> p k m", k=2),
                        scalar=column(g["w_slot"], j - 2),
                        in1=si[:, u, :].rearrange("p (k m) -> p k m", k=2),
                        op0=ALU.mult, op1=ALU.mult).then_inc(hg_done, 1)
                if on[1]:
                    dve.wait_ge(hi_done, j)
                    nc.vector.tensor_tensor(x_lo[:, v, :], ps[:, v, 0:D], x_hi[:, v, :].bitcast(F32),
                                            ALU.subtract).then_inc(lo_done, 1)
                if on[4]:
                    ge(dve, scattered[u], 8 * (j - 4 - u))
                    nc.vector.tensor_copy(odx[u][:], column(g["dst_i"], j - 4)).then_inc(odx_set, 1)

            paired(dve, step, DEPTH)

        @block.gpsimd
        def _(pool):
            nc.gpsimd.memset(tick[:], 0.0).then_inc(tick_set, 1)

            def ticks(j):
                return 1 + (min(j, NB) + max(0, j - 5) if isinstance(j, int) else 2 * j - 5)

            def hold(n):
                pool.wait_ge(tick_set, n)
                nc.gpsimd.tensor_tensor(tick[:, 1:2], tick[:, 0:1], tick[:, 0:1], ALU.add).then_inc(tick_set, 1)

            def step(j, u, on):
                v = 1 - u
                if on[0]:
                    pool.wait_ge(idx_set, j + 1)
                    ge(pool, x_turned, j - 1)
                    hold(ticks(j))
                    pool.indirect_dma_start(xg[u][:], None, g["x_rows"],
                                            bass.IndirectOffsetOnAxis(ap=idx[u][:], axis=0)
                                            ).then_inc(gathered[u], 16)
                if on[5]:
                    pool.wait_ge(yo_done, j - 4)
                    pool.wait_ge(odx_set, j - 4)
                    if not isinstance(j, int) or j > 5:
                        pool.wait_ge(scattered[u], 8 * (j - 6 - u) + 16)
                    hold(ticks(j) + (1 if on[0] else 0))
                    pool.indirect_dma_start(g["y_rows"], bass.IndirectOffsetOnAxis(ap=odx[v][:], axis=0),
                                            yo[v][:], None).then_inc(scattered[v], 16)

            paired(pool, step, DEPTH)
            for u in range(2):
                pool.wait_ge(scattered[u], 8 * NB)


def combine(nc, g, out):
    with ExitStack() as ctx:
        ps, hres = g["ps"], g["hres"]
        RING = 6
        yin = ctx.enter_context(nc.sbuf_tensor("z_yin", [P, RING, 2, D], F32))
        loaded = [ctx.enter_context(nc.semaphore(f"z_loaded{u}")) for u in range(RING)]
        half_done = ctx.enter_context(nc.semaphore("z_half_done"))
        added = ctx.enter_context(nc.semaphore("z_added"))
        stored = ctx.enter_context(nc.semaphore("z_stored"))
        block = ctx.enter_context(nc.Block())

        @block.sync
        def _(sp):
            for i in range(NI):
                if i >= RING:
                    sp.wait_ge(added, i - RING + 1)
                m = ROWS[i % NT]
                sp.dma_start(yin[0:m, i % RING].rearrange("p k f -> p (k f)"),
                             g["y_rows"][2 * P * i:2 * P * i + 2 * m, :].rearrange("(p k) f -> p (k f)", k=2)
                             ).then_inc(loaded[i % RING], 16)

        @block.scalar
        def _(act):
            for i in range(NI):
                b, t = i // NT, i % NT
                act.wait_ge(added, i + 1)
                act.dma_start(out[b, t * P:t * P + ROWS[t], :], hres[0:ROWS[t], i, :]).then_inc(stored, 16)
            act.wait_ge(stored, 16 * NI)

        @block.vector
        def _(dve):
            for i in range(NI + 1):
                if i < NI:
                    m = ROWS[i % NT]
                    dve.wait_ge(loaded[i % RING], 16 * (i // RING + 1))
                    nc.vector.tensor_tensor(yin[0:m, i % RING, 0, :], yin[0:m, i % RING, 0, :],
                                            yin[0:m, i % RING, 1, :], ALU.add).then_inc(half_done, 1)
                if i >= 1:
                    m = ROWS[(i - 1) % NT]
                    dve.wait_ge(half_done, i)
                    nc.vector.tensor_tensor(hres[0:m, i - 1, :], hres[0:m, i - 1, :],
                                            yin[0:m, (i - 1) % RING, 0, :], ALU.add).then_inc(added, 1)


def experts(nc, g, out):
    with ExitStack() as ctx:
        def sb(name, shape, dt=F32):
            return ctx.enter_context(nc.sbuf_tensor(name, shape, dt))

        g["score"] = sb("score", [P, NI, E])
        g["src_i"] = sb("src_i", [P, NB], U32)
        g["dst_i"] = sb("dst_i", [P, NB], U32)
        g["w_slot"] = sb("w_slot", [P, NB])
        g["bex_i"] = sb("bex_i", [P, NB], U32)
        g["x_rows"] = nc.dram_tensor("x_rows", (P * NI, D), F32, kind="Internal").ap()
        g["y_rows"] = nc.dram_tensor("y_rows", (2 * P * NI + P, D), F32, kind="Internal").ap()
        shared_expert(nc, g)
        route(nc, g)
        expert_blocks(nc, g)
        combine(nc, g, out)





def build(nc, ins, out):
    with ExitStack() as ctx:
        def sb(name, shape, dt=F32):
            return ctx.enter_context(nc.sbuf_tensor(name, shape, dt))

        g = {
            "ps": ctx.enter_context(nc.psum_tensor("ps", [P, 8, 512], F32)),
            "hres": sb("hres", [P, NT * B, D]),
            "ident": sb("ident", [P, P]),
            "mhalf": sb("mhalf", [P, 8]),
            "w1raw": sb("w1raw", [P, FC, NJ * 2 * HE]),
            "w2": sb("w2", [HE // 2, 2, E, D]),
            "ws2": sb("ws2", [P, HS // P, D]),
            "ident_ready": ctx.enter_context(nc.semaphore("ident_ready")),
        }
        setup(nc, g)
        with ExitStack() as attn:
            def sba(name, shape, dt=F32):
                return attn.enter_context(nc.sbuf_tensor(name, shape, dt))

            g["wa_hi"] = sba("wa_hi", [P, FC, 4 * DA], F32R)
            g["wa_lo"] = sba("wa_lo", [P, FC, 4 * DA], F32R)
            g["gam"] = sba("gam", [P, HA])
            g["W_g_b"] = ins["W_g_b"]
            g["wo"] = sba("wo", [P, DA // P, D])
            g["decay"] = sba("decay", [P, HA, SCORE_COLS])
            token_mixer(nc, g, ins)
            linear_attention(nc, g)
        phase_cd(nc, g, ins, out)


def kernel(**inputs):
    import numpy as np
    import concourse.bacc as bacc
    from concourse.bass_utils import run_bass_kernel_spmd

    nc = bacc.Bacc("TRN2", target_bir_lowering=False, num_devices=1)
    i = {k: np.asarray(v) for k, v in inputs.items()}
    x = i["x"]
    arrays = {
        "x_t": x.transpose(0, 1, 3, 2),
        "x_flat": x.transpose(0, 2, 3, 1).reshape(B, L, H0 * F),
        "txt": i["txt"],
        "wq_t": i["L0_tok_Wq_w"].T, "wk_t": i["L0_tok_Wk_w"].T, "wv_t": i["L0_tok_Wv_w"].T,
        "bq": i["L0_tok_Wq_b"], "bk": i["L0_tok_Wk_b"], "bv": i["L0_tok_Wv_b"],
        "w_bias_t": i["L0_tok_w_bias"].T,
        "mask_t": i["L0_tok_local_mask"].T,
        "out_w": i["L0_tok_out_w"], "out_b": i["L0_tok_out_b"],
        "ln_g": i["L0_tok_ln_g"], "ln_b": i["L0_tok_ln_b"],
        "W_Q_t": i["L0_attn_W_Q"].T, "W_K_t": i["L0_attn_W_K"].T,
        "W_V_t": i["L0_attn_W_V"].T, "W_g_t": i["L0_attn_W_g_w"].T,
        "W_g_b": i["L0_attn_W_g_b"], "W_O_t": i["L0_attn_W_O"].T,
        "decay_log": i["L0_attn_decay_log"],
        "ffn_w": i["L0_ffn_weight"],
        "Wq1": i["L1_attn_w_qkv"][0:D], "Wk1_t": i["L1_attn_w_qkv"][D:2 * D].T,
        "Wv1": i["L1_attn_w_qkv"][2 * D:], "Wv1_t": i["L1_attn_w_qkv"][2 * D:].T,
        "w_conv1": i["L1_attn_w_conv1"],
        "gate_t": i["L1_ffn_gate_w"].T,
        "W1_t": i["L1_ffn_W1"].transpose(0, 2, 1), "W2_t": i["L1_ffn_W2"].transpose(0, 2, 1),
        "Ws1_t": i["L1_ffn_Ws1"].T, "Ws2_t": i["L1_ffn_Ws2"].T,
        "hadamard": hadamard(np),
    }
    arrays = {f"in_{n}": np.ascontiguousarray(a) for n, a in arrays.items()}
    ins = {n[3:]: nc.dram_tensor(n, a.shape, mybir.dt.from_np(a.dtype), kind="ExternalInput").ap()
           for n, a in arrays.items()}
    out = nc.dram_tensor("out", (B, T, D), F32, kind="ExternalOutput").ap()
    build(nc, ins, out)
    return run_bass_kernel_spmd(nc, [arrays], core_ids=[0]).results[0]["out"]


def hadamard(np):
    h = np.array([[1.0]])
    while h.shape[0] < D:
        h = np.block([[h, h], [h, -h]])
    return (h / np.sqrt(D)).astype(np.float32)
```

```python
from contextlib import ExitStack

import concourse.bass as bass
from concourse import mybir

F32 = mybir.dt.float32
F32R = mybir.dt.float32r
BF16 = mybir.dt.bfloat16
U8 = mybir.dt.uint8
U32 = mybir.dt.uint32
ALU = mybir.AluOpType
ACT = mybir.ActivationFunctionType
AX = mybir.AxisListType

P = 128
B, F, L, H0 = 8, 64, 256, 4
TXT = 32
D = 256
T = L + TXT
NT = 3
TP = NT * P
ROWS = (P, P, TXT)
NI = NT * B
HA, DK = 8, 64
DA = HA * DK
E, HE, HS = 8, 192, 384
NJ = E + HS // HE
LN_EPS = 1e-5
ATT_EPS = 1e-6
ACT_POS, ACT_NEG = 7.0, 8.0
ROUND = 12582912.0
FC = D // P
WIDTHS = (T, T - P, 2 * TXT)
SCORE_COLS = sum(WIDTHS)


def ge(eng, sem, value):
    if isinstance(value, int) and value <= 0:
        return
    eng.wait_ge(sem, value)


class Steps:

    def __init__(self, eng, sem, start):
        self.eng, self.sem, self.n = eng, sem, start

    def __call__(self, ins):
        self.n = self.n + 1
        ins.then_inc(self.sem, 1)
        self.eng.wait_ge(self.sem, self.n)


def skewed(eng, step):
    step(-2, True, False, False)
    step(-1, True, True, False)
    step(0, True, True, True)
    with eng.Fori(1, B - 2) as b:
        step(b, True, True, True)
    step(B - 2, False, True, True)
    step(B - 1, False, False, True)


def skewed4(eng, step):
    for b in range(-3, 1):
        step(b, True, b > -3, b > -2, b > -1)
    with eng.Fori(1, B - 3) as b:
        step(b, True, True, True, True)
    for b in range(B - 3, B):
        step(b, False, b < B - 2, b < B - 1, True)


def row_broadcast(ap, n):
    return ap.rearrange("(a n) -> a n", a=1).to_broadcast([P, n])


def token_mixer(nc, g, ins):
    with ExitStack() as ctx:
        def sb(name, shape, dt=F32):
            return ctx.enter_context(nc.sbuf_tensor(name, shape, dt))

        def sem(name):
            return ctx.enter_context(nc.semaphore(name))

        ps = g["ps"]
        hres = g["hres"]
        ident, gam = g["ident"], g["gam"]
        stage = sb("stage", [P, FC, 4 * DA])
        wqkv = sb("a_wqkv", [F + 1, 3 * F])
        ewt = sb("a_ewt", [P, 2, L])
        mask8 = sb("a_mask8", [P, 2, L], U8)
        maskf = sb("a_maskf", [P, 2, L])
        outw = sb("a_outw", [P, FC, D])
        outb = sb("a_outb", [P, D])
        lng = sb("a_lng", [P, D])
        lnb = sb("a_lnb", [P, D])
        xt = sb("a_xt", [F + 1, H0, L])
        xfl = sb("a_xfl", [P, 2, D])
        xb = sb("a_xb", [P, 2, D])
        nk = sb("a_nk", [P, 2, 2, 2 * D])
        eq = sb("a_eq", [P, 2, 2, D])
        den = sb("a_den", [P, 2, D])
        rden = sb("a_rden", [P, 2, D])
        y = sb("a_y", [P, 2, D])
        yt = sb("a_yt", [P, FC, L])
        hp = sb("a_hp", [P, 2, D])
        hn = sb("a_hn", [P, 2, D])
        stats = sb("a_stats", [P, 2, 6])
        mv = sb("a_mv", [P, 2, 2])
        ve = sb("a_ve", [P, 2, 1])
        tick = sb("a_tick", [P, 1])
        rstd = sb("a_rstd", [P, 2, 1])
        lgam = sb("a_lgam", [P, HA])
        age = sb("a_age", [P, T])
        agm = sb("a_agm", [P, T])
        draw = sb("a_draw", [P, HA])

        w_in = sem("a_w_in")
        ln_in = sem("a_ln_in")
        ew_in = sem("a_ew_in")
        x_in = sem("a_x_in")
        xf_in = sem("a_xf_in")
        attw_in = sem("a_attw_in")
        txt_in = sem("a_txt_in")
        later_in = sem("a_later_in")
        filled = sem("a_filled")
        ew_ready = sem("a_ew_ready")
        qkv_done = sem("a_qkv_done")
        exps_done = sem("a_exps_done")
        ekv_done = sem("a_ekv_done")
        nd_done = sem("a_nd_done")
        y_done = sem("a_y_done")
        turned = sem("a_turned")
        yt_done = sem("a_yt_done")
        out_done = sem("a_out_done")
        hp_done = sem("a_hp_done")
        xb_done = sem("a_xb_done")
        var_done = sem("a_var_done")
        rstd_done = sem("a_rstd_done")
        y_steps = sem("a_y_steps")
        ln_steps = sem("a_ln_steps")
        hn_done = sem("a_hn_done")
        gain_steps = sem("a_gain_steps")
        hi_done = sem("a_hi_done")
        gam_in = sem("a_gam_in")
        gam_steps = sem("a_gam_steps")
        decay_set = sem("a_decay_set")
        pool_done = sem("a_pool_done")

        qkv = ps[:, 0:4, :].rearrange("p (l a) (c j) -> p l (a c) j", l=2, c=2)

        def part(i):
            return qkv[:, :, :, i * F:(i + 1) * F]

        def heads(ap):
            return ap.rearrange("p l (h d) -> p l h d", h=H0)

        def twice(row):
            return row[:].rearrange("p (a f) -> p a f", a=1).to_broadcast([P, 2, D])

        def part_of(w, b):
            n = 4 * DA // B
            return w[:, :, b * n:(b + 1) * n] if isinstance(b, int) else w[:, :, bass.ds(b * n, n)]

        block = ctx.enter_context(nc.Block())

        @block.sync
        def _(sp):
            x_t, x_flat = ins["x_t"], ins["x_flat"]

            def load_x(b):
                if isinstance(b, int):
                    xs = x_t[b]
                else:
                    xs = x_t[bass.ds(b, 1)].rearrange("a c h l -> (a c) h l")
                ge(sp, qkv_done, b)
                sp.dma_start(xt[0:F], xs).then_inc(x_in, 16)

            def load_flat(b):
                fs = x_flat[b] if isinstance(b, int) else x_flat[bass.ds(b, 1)].rearrange("a l f -> (a l) f")
                ge(sp, xb_done, b)
                sp.dma_start(xfl[:], fs.rearrange("(t p) f -> p t f", p=P)).then_inc(xf_in, 16)

            load_x(0)
            sp.dma_start(draw[:], row_broadcast(ins["decay_log"], HA)).then_inc(gam_in, 16)
            for i, n in enumerate("qkv"):
                sp.dma_start(wqkv[0:F, i * F:(i + 1) * F], ins[f"w{n}_t"]).then_inc(w_in, 16)
                sp.dma_start(wqkv[F:F + 1, i * F:(i + 1) * F],
                             ins[f"b{n}"].rearrange("(a n) -> a n", a=1)).then_inc(w_in, 16)
            sp.dma_start(ewt[:], ins["w_bias_t"].rearrange("(s p) t -> p s t", p=P)).then_inc(ew_in, 16)
            sp.dma_start(mask8[:], ins["mask_t"].rearrange("(s p) t -> p s t", p=P)).then_inc(ew_in, 16)
            sp.dma_start(outb[:], row_broadcast(ins["out_b"], D)).then_inc(ln_in, 16)
            sp.dma_start(outw[:], ins["out_w"].rearrange("(c p) n -> p c n", p=P)).then_inc(ln_in, 16)
            sp.dma_start(lng[:], row_broadcast(ins["ln_g"], D)).then_inc(ln_in, 16)
            sp.dma_start(lnb[:], row_broadcast(ins["ln_b"], D)).then_inc(ln_in, 16)
            load_flat(0)
            load_x(1)
            for i, n in enumerate(("W_Q_t", "W_K_t", "W_V_t", "W_g_t")):
                sp.dma_start(stage[:, :, i * DA:(i + 1) * DA],
                             ins[n].rearrange("(c p) n -> p c n", p=P)).then_inc(attw_in, 16)
            load_x(2)
            with sp.Fori(3, B) as b:
                load_x(b)
                load_flat(b - 2)
            load_flat(B - 2)
            load_flat(B - 1)
            sp.dma_start(g["wo"][:], ins["W_O_t"].rearrange("(c p) n -> p c n", p=P)).then_inc(later_in, 16)
            for e in range(E):
                sp.dma_start(g["w1raw"][:, :, e * 2 * HE:(e + 1) * 2 * HE],
                             ins["W1_t"][e].rearrange("(c p) n -> p c n", p=P)).then_inc(later_in, 16)
                sp.dma_start(g["w2"][:, :, e, :],
                             ins["W2_t"][e].rearrange("(c p) n -> p c n", p=HE // 2)).then_inc(later_in, 16)
            sp.dma_start(g["w1raw"][:, :, E * 2 * HE:],
                         ins["Ws1_t"].rearrange("(c p) n -> p c n", p=P)).then_inc(later_in, 16)
            sp.dma_start(g["ws2"][:], ins["Ws2_t"].rearrange("(c p) n -> p c n", p=P)).then_inc(later_in, 16)
            sp.wait_ge(later_in, 16 * (3 + 2 * E))
            sp.wait_ge(txt_in, 16 * B)

        @block.tensor
        def _(pe):
            def qkv_products(b):
                ge(pe, x_in, 16 * b + 16)
                if isinstance(b, int) and b == 0:
                    pe.wait_ge(filled, 1)
                    pe.wait_ge(w_in, 16 * 6)
                ge(pe, ekv_done, b)
                ge(pe, exps_done, b)
                for lt in range(2):
                    for h in range(H0):
                        mm = nc.tensor.matmul(qkv[:, lt, h, 0:3 * F], xt[:, h, lt * P:(lt + 1) * P],
                                              wqkv[:, :], start=True, stop=True)
                mm.then_inc(qkv_done, 1)

            def turn(b):
                pe.wait_ge(y_done, b + 1)
                if isinstance(b, int) and b == 0:
                    pe.wait_ge(g["ident_ready"], 1)
                ge(pe, yt_done, b)
                for fc in range(FC):
                    for t in range(2):
                        mm = nc.tensor.transpose(ps[:, 6, fc * L + t * P:fc * L + (t + 1) * P],
                                                 y[:, t, fc * P:(fc + 1) * P], ident[:])
                mm.then_inc(turned, 1)

            def sums(b):
                if isinstance(b, int) and b == 0:
                    pe.wait_ge(ew_ready, 1)
                pe.wait_ge(ekv_done, b + 1)
                pe.wait_ge(exps_done, b + 1)
                ge(pe, y_done, b)
                for t in range(2):
                    for s in range(2):
                        mm = nc.tensor.matmul(ps[:, 4 + t, :], ewt[:, s, t * P:(t + 1) * P],
                                              nk[:, b % 2, s, :], start=s == 0, stop=s == 1)
                mm.then_inc(nd_done, 1)

            def project(b):
                if isinstance(b, int) and b == 0:
                    pe.wait_ge(ln_in, 16 * 4)
                pe.wait_ge(yt_done, b + 1)
                ge(pe, hp_done, b)
                for t in range(2):
                    for fc in range(FC):
                        mm = nc.tensor.matmul(ps[:, 7, t * D:(t + 1) * D], yt[:, fc, t * P:(t + 1) * P],
                                              outw[:, fc, :], start=fc == 0, stop=fc == FC - 1)
                mm.then_inc(out_done, 1)

            def step(b, s1, s2, s3):
                if s1:
                    qkv_products(b + 2)
                if s3:
                    turn(b)
                if s2:
                    sums(b + 1)
                if s3:
                    project(b)

            skewed(pe, step)

        @block.scalar
        def _(act):
            act.wait_ge(gam_in, 16)
            nc.scalar.activation(gam[:], draw[:], ACT.Exp, scale=-1.0).then_inc(gam_steps, 1)
            act.wait_ge(y_steps, 2)
            nc.scalar.activation(ewt[:], maskf[:], ACT.Exp).then_inc(ew_ready, 1)
            act.wait_ge(gam_steps, 4)
            nc.scalar.activation(lgam[:], gam[:], ACT.Ln).then_inc(gam_steps, 1)
            act.wait_ge(gam_steps, 5)
            act.wait_ge(pool_done, 2)
            for h in range(HA):
                nc.scalar.activation(g["decay"][:, h, 0:T], agm[:], ACT.Exp,
                                     scale=lgam[:, h:h + 1]).then_inc(decay_set, 1)

            def exps(b):
                act.wait_ge(qkv_done, b + 1)
                ge(act, nd_done, b - 1)
                nc.scalar.activation(heads(nk[:, b % 2, :, D:2 * D]) if isinstance(b, int) else
                                     nk[:, b % 2, :, D:2 * D].rearrange("p l (h d) -> p l h d", h=H0),
                                     part(1), ACT.Exp)
                ge(act, y_done, b - 1)
                nc.scalar.activation(heads(eq[:, b % 2]), part(0), ACT.Exp, scale=-1.0).then_inc(exps_done, 1)

            def copy_yt(b):
                act.wait_ge(turned, b + 1)
                ge(act, out_done, b)
                nc.scalar.copy(yt[:].rearrange("p c l -> p (c l)"), ps[:, 6, :]).then_inc(yt_done, 1)

            def step(b, s1, s2, s3):
                if s3:
                    copy_yt(b)
                if s1:
                    exps(b + 2)
                if s3:
                    if isinstance(b, int) and b == 0:
                        act.wait_ge(attw_in, 16 * 4)
                    nc.scalar.copy(part_of(g["wa_hi"], b), part_of(stage, b)).then_inc(hi_done, 1)

            skewed(act, step)

        @block.vector
        def _(dve):
            nc.vector.memset(xt[F:F + 1], 1.0).then_inc(filled, 1)
            for b in range(B):
                ms = nc.vector.memset(hres[:, NT * b + 2, :], 0.0)
            ms.then_inc(filled, 1)
            dve.wait_ge(gam_steps, 1)
            step = Steps(dve, gam_steps, 1)
            step(nc.vector.tensor_scalar(gam[:], gam[:], 1.0, None, ALU.add))
            step(nc.vector.reciprocal(gam[:], gam[:]))
            step(nc.vector.tensor_scalar(gam[:], gam[:], 1e-18, None, ALU.max))
            dve.wait_ge(ew_in, 32)
            nc.vector.tensor_copy(maskf[:], mask8[:]).then_inc(y_steps, 1)
            dve.wait_ge(y_steps, 1)
            nc.vector.tensor_tensor(maskf[:], maskf[:], ewt[:], ALU.mult).then_inc(y_steps, 1)

            def weigh(b):
                dve.wait_ge(exps_done, b + 1)
                ge(dve, nd_done, b - 1)
                nc.vector.tensor_tensor(heads(nk[:, b % 2, :, 0:D]), heads(nk[:, b % 2, :, D:2 * D]),
                                        part(2), ALU.mult).then_inc(ekv_done, 1)

            def divide(b):
                step = Steps(dve, y_steps, b * 2 + 2)
                dve.wait_ge(nd_done, b + 1)
                step(nc.vector.scalar_tensor_tensor(out=den[:], in0=eq[:, b % 2], scalar=1.0,
                                                    in1=ps[:, 4:6, D:2 * D], op0=ALU.add, op1=ALU.mult))
                step(nc.vector.reciprocal(rden[:], den[:]))
                ge(dve, turned, b)
                nc.vector.tensor_tensor(y[:], ps[:, 4:6, 0:D], rden[:], ALU.mult).then_inc(y_done, 1)

            def norm(b):
                step = Steps(dve, ln_steps, b * 2)
                dve.wait_ge(out_done, b + 1)
                dve.wait_ge(xb_done, b + 1)
                ge(dve, hn_done, b)
                nc.vector.tensor_tensor(hp[:].rearrange("p t f -> p (t f)"), ps[:, 7, :],
                                        xb[:].rearrange("p t f -> p (t f)"), ALU.add).then_inc(hp_done, 1)
                dve.wait_ge(hp_done, b + 1)
                for t in range(2):
                    last = nc.vector.bn_stats(stats[:, t, :], hp[:, t, :])
                step(last)
                nc.vector.memset(tick[:], 0.0)
                for t in range(2):
                    last = nc.vector.bn_aggr(mv[:, t, :], stats[:, t, :])
                step(last)
                nc.vector.tensor_scalar(ve[:], mv[:, :, 1:2], LN_EPS, None, ALU.add).then_inc(var_done, 1)
                dve.wait_ge(rstd_done, b + 1)
                ge(dve, gain_steps, 2 * b)
                for t in range(2):
                    last = nc.vector.tensor_scalar(hn[:, t, :], hp[:, t, :], mv[:, t, 0:1], rstd[:, t, :],
                                                   ALU.subtract, ALU.mult)
                last.then_inc(hn_done, 1)

            def step(b, s1, s2, s3):
                if s1:
                    weigh(b + 2)
                if s2:
                    divide(b + 1)
                if s3:
                    norm(b)

            skewed(dve, step)

        @block.gpsimd
        def _(pool):
            nc.gpsimd.iota(age[:], [[1, T]], base=0, channel_multiplier=-1,
                           allow_small_or_imprecise_dtypes=True).then_inc(pool_done, 1)
            pool.wait_ge(pool_done, 1)
            nc.gpsimd.tensor_scalar(agm[:], age[:], 0.0, None, ALU.max).then_inc(pool_done, 1)
            pool.wait_ge(filled, 2)
            for b in range(B):
                pool.dma_start(hres[0:TXT, NT * b + 2, :], ins["txt"][b]).then_inc(txt_in, 16)

            def add_bias(b):
                pool.wait_ge(xf_in, 16 * b + 16)
                if isinstance(b, int) and b == 0:
                    pool.wait_ge(ln_in, 16 * 4)
                ge(pool, hp_done, b)
                nc.gpsimd.tensor_tensor(xb[:], xfl[:], twice(outb), ALU.add).then_inc(xb_done, 1)

            def root(b):
                pool.wait_ge(var_done, b + 1)
                nc.gpsimd.tensor_tensor(rstd[:], ve[:], g["mhalf"][:, 0:2].rearrange("p (t a) -> p t a", a=1),
                                        ALU.pow).then_inc(rstd_done, 1)

            def gain(b):
                pool.wait_ge(hn_done, b + 1)
                nc.gpsimd.tensor_tensor(hn[:], hn[:], twice(lng), ALU.mult).then_inc(gain_steps, 1)
                pool.wait_ge(gain_steps, 2 * b + 1)
                nc.gpsimd.tensor_tensor(hres[:, bass.ds(b * NT, 2), :] if not isinstance(b, int) else
                                        hres[:, b * NT:b * NT + 2, :], hn[:], twice(lnb),
                                        ALU.add).then_inc(gain_steps, 1)

            def split(b):
                pool.wait_ge(hi_done, b + 1)
                nc.gpsimd.tensor_tensor(part_of(g["wa_lo"], b), part_of(stage, b),
                                        part_of(g["wa_hi"], b).bitcast(F32), ALU.subtract)

            add_bias(0)
            nc.gpsimd.memset(g["decay"][:, :, SCORE_COLS - 2 * TXT:SCORE_COLS - TXT], 0.0)
            for h in range(HA):
                pool.wait_ge(decay_set, h + 1)
                nc.gpsimd.affine_select(out=g["decay"][:, h, 0:T], in_=g["decay"][:, h, 0:T],
                                        compare_op=ALU.is_ge, fill=0.0, base=0, pattern=[[1, T]],
                                        channel_multiplier=-1).then_inc(pool_done, 1)
                pool.wait_ge(pool_done, 2 + 3 * h + 1)
                nc.gpsimd.tensor_copy(g["decay"][:, h, T:T + P + TXT],
                                      g["decay"][:, h, 0:P + TXT]).then_inc(pool_done, 1)
                nc.gpsimd.tensor_copy(g["decay"][:, h, SCORE_COLS - TXT:SCORE_COLS],
                                      g["decay"][:, h, 0:TXT]).then_inc(pool_done, 1)
            root(0)
            add_bias(1)
            gain(0)
            split(0)
            with pool.Fori(1, B - 1) as b:
                root(b)
                add_bias(b + 1)
                gain(b)
                split(b)
            split(B - 1)
            root(B - 1)
            gain(B - 1)


def setup(nc, g):
    with ExitStack() as ctx:
        zeroed = ctx.enter_context(nc.semaphore("zeroed"))
        block = ctx.enter_context(nc.Block())

        @block.gpsimd
        def _(pool):
            nc.gpsimd.memset(g["mhalf"][:], -0.5)
            nc.gpsimd.memset(g["ident"][:], 0.0).then_inc(zeroed, 1)
            pool.wait_ge(zeroed, 1)
            nc.gpsimd.affine_select(out=g["ident"][:], in_=g["ident"][:], compare_op=ALU.not_equal,
                                    fill=1.0, base=0, pattern=[[-1, P]],
                                    channel_multiplier=1).then_inc(g["ident_ready"], 1)


def norm_stats(nc, dve, step, src, stats, mv, ve, tick, var_done):
    for t in range(NT):
        last = nc.vector.bn_stats(stats[:, t, :], src(t))
    step(last)
    nc.vector.memset(tick[:], 0.0)
    for t in range(NT):
        last = nc.vector.bn_aggr(mv[:, t, :], stats[:, t, :])
    step(last)
    nc.vector.tensor_scalar(ve[:], mv[:, :, 1:2], LN_EPS, None, ALU.add).then_inc(var_done, 1)


def res(g, b, t):
    if isinstance(b, int):
        return g["hres"][:, NT * b + t, :]
    return g["hres"][:, bass.ds(b * NT + t, 1), :].rearrange("p a f -> p (a f)")


def split_products(nc, out, x_hi, x_lo, w_hi, w_lo, start, stop):
    nc.tensor.matmul(out, x_hi, w_hi, start=start, stop=False)
    nc.tensor.matmul(out, x_hi, w_lo, start=False, stop=False)
    return nc.tensor.matmul(out, x_lo, w_hi, start=False, stop=stop)


def linear_attention(nc, g):
    with ExitStack() as ctx:
        def sb(name, shape, dt=F32):
            return ctx.enter_context(nc.sbuf_tensor(name, shape, dt))

        def sem(name):
            return ctx.enter_context(nc.semaphore(name))

        ps, hres, ident = g["ps"], g["hres"], g["ident"]
        wa_hi, wa_lo = g["wa_hi"], g["wa_lo"]
        NP = HA // 2
        NG = 3 * NP // 2
        AW = SCORE_COLS
        stats = sb("b_stats", [P, NT, 6])
        mv = sb("b_mv", [P, NT, 2])
        ve = sb("b_ve", [P, NT, 1])
        rstd = sb("b_rstd", [P, NT, 1])
        tick = sb("b_tick", [P, 1])
        warm = sb("b_warm", [P, 1])
        xn = sb("b_xn", [P, NT, D])
        x_hi = sb("b_x_hi", [P, FC, TP], F32R)
        x_lo = sb("b_x_lo", [P, FC, TP], F32R)
        qk = sb("b_qk", [P, 2 * NP, T])
        ex = sb("b_ex", [P, 2, 2, T])
        v = sb("b_v", [P, NT, DA])
        sg = sb("b_sg", [P, NP, T])
        z = sb("b_z", [P, NP, T])
        a = sb("b_a", [P, 2, AW])
        rd = sb("b_rd", [HA, T])
        yt = sb("b_yt", [P, 2, T])
        y_hi = sb("b_y_hi", [P, NP, T], F32R)
        y_lo = sb("b_y_lo", [P, NP, T], F32R)
        wo_hi = sb("b_wo_hi", [P, NP, D], F32R)
        wo_lo = sb("b_wo_lo", [P, NP, D], F32R)
        gpair = sb("b_gpair", [P, NP])
        bg = sb("b_bg", [P, NP])
        pick = sb("b_pick", [P, NP, HA])
        spread = sb("b_spread", [HA, NP, P])

        bias_in = sem("b_bias_in")
        pick_set = sem("b_pick_set")
        tables_done = sem("b_tables_done")
        ln_steps = sem("b_ln_steps")
        var_done = sem("b_var_done")
        rstd_done = sem("b_rstd_done")
        xn_done = sem("b_xn_done")
        x_turned = sem("b_x_turned")
        hi_done = sem("b_hi_done")
        lo_done = sem("b_lo_done")
        qk_done = sem("b_qk_done")
        exp_done = sem("b_exp_done")
        low_done = sem("b_low_done")
        phi_done = sem("b_phi_done")
        gate_done = sem("b_gate_done")
        gate_read = sem("b_gate_read")
        v_done = sem("b_v_done")
        v_read = sem("b_v_read")
        z_done = sem("b_z_done")
        qz_done = sem("b_qz_done")
        den_done = sem("b_den_done")
        den_steps = sem("b_den_steps")
        rd_done = sem("b_rd_done")
        spread_done = sem("b_spread_done")
        sg_done = sem("b_sg_done")
        score_done = sem("b_score_done")
        masked = sem("b_masked")
        num_done = sem("b_num_done")
        y_done = sem("b_y_done")
        y_hi_done = sem("b_y_hi_done")
        y_lo_done = sem("b_y_lo_done")
        wo_done = sem("b_wo_done")
        res_done = sem("b_res_done")

        def group(i):
            return (2, 4, 6, 2, 4, 2)[i]

        block = ctx.enter_context(nc.Block())

        @block.sync
        def _(sp):
            for j in range(NP):
                sp.dma_start(bg[:, j:j + 1], g["W_g_b"].rearrange("(j p a) -> j p a", p=P, a=1)[j]
                             ).then_inc(bias_in, 16)

        @block.tensor
        def _(pe):
            pe.wait_ge(pick_set, 3)
            for j in range(NP):
                mm = nc.tensor.transpose(ps[0:HA, 7, j * P:(j + 1) * P], pick[:, j, :], ident[:])
            mm.then_inc(tables_done, 1)

            def turn_x(b):
                pe.wait_ge(xn_done, b + 1)
                ge(pe, lo_done, b)
                for fc in range(FC):
                    for t in range(NT):
                        mm = nc.tensor.transpose(ps[:, fc, t * P:(t + 1) * P],
                                                 xn[:, t, fc * P:(fc + 1) * P], ident[:])
                mm.then_inc(x_turned, 1)

            def projections(b):
                pe.wait_ge(lo_done, b + 1)
                ge(pe, sg_done, 2 * b)
                ge(pe, masked, HA * b)
                for t in range(NT):
                    for fc in range(FC):
                        rows = slice(t * P, (t + 1) * P)
                        cols = slice(2 * DA, 3 * DA)
                        mm = split_products(nc, ps[:, 2 + t, :], x_hi[:, fc, rows], x_lo[:, fc, rows],
                                            wa_hi[:, fc, cols], wa_lo[:, fc, cols], fc == 0, fc == FC - 1)
                    if t:
                        mm.then_inc(v_done, 1)
                for i in range(NG):
                    if i < 2:
                        pe.wait_ge(v_read, 2 * b + i + 1)
                    elif i == 2:
                        ge(pe, y_done, NP * b)
                    else:
                        pe.wait_ge(phi_done, NP * b + (1, 2, 4)[i - 3])
                    for k in range(2):
                        cols = 2 * i + k
                        cols += 0 if i < NP else NP
                        cols = slice(cols * P, (cols + 1) * P)
                        for fc in range(FC):
                            mm = split_products(nc, ps[:, group(i) + k, 0:T], wa_hi[:, fc, cols],
                                                wa_lo[:, fc, cols], x_hi[:, fc, 0:T], x_lo[:, fc, 0:T],
                                                fc == 0, fc == FC - 1)
                    mm.then_inc(qk_done if i < NP else gate_done, 1)

            def denominators(b):
                pe.wait_ge(gate_read, 2 * (b + 1))
                pe.wait_ge(qz_done, NP * (b + 1))
                for j in range(NP):
                    mm = nc.tensor.matmul(ps[0:HA, 5, 0:T], pick[:, j, :], z[:, j, :],
                                          start=j == 0, stop=j == NP - 1)
                mm.then_inc(den_done, 1)

            def spread_out(b):
                for half in range(2):
                    pe.wait_ge(rd_done, 2 * b + half + 1)
                    cols = slice(half * T // 2, (half + 1) * T // 2)
                    for j in range(NP):
                        mm = nc.tensor.matmul(ps[:, 2 + j, cols], spread[:, j, :], rd[:, cols],
                                              start=True, stop=True)
                        if half and j % 2:
                            mm.then_inc(spread_done, 1)

            def scores(b, h):
                if h < 2:
                    pe.wait_ge(sg_done, 2 * (b + 1))
                else:
                    pe.wait_ge(masked, HA * b + h - 1)
                rows = slice(DK * (h % 2), DK * (h % 2) + DK)
                j, col = h // 2, 0
                for s in range(NT):
                    m, n = ROWS[s], WIDTHS[s]
                    mm = nc.tensor.matmul(ps[0:m, 4 + h % 2, col:col + n],
                                          qk[rows, NP + j, s * P:s * P + m],
                                          qk[rows, j, T - n:T], start=True, stop=True)
                    col += n
                mm.then_inc(score_done, 1)

            def values(b, h):
                pe.wait_ge(masked, HA * b + h + 1)
                j = h // 2
                if h % 2 == 0:
                    ge(pe, y_done, NP * b + j - 1)
                    if j < 2:
                        ge(pe, res_done, 2 * (b - 1) + j + 1)
                col = 0
                for s in range(NT):
                    n, kk = WIDTHS[s], ROWS[s]
                    mm = nc.tensor.matmul(ps[DK * (h % 2):DK * (h % 2) + DK, 6 + j % 2, T - n:T],
                                          v[0:kk, s, h * DK:(h + 1) * DK], a[0:kk, h % 2, col:col + n],
                                          start=s == 0, stop=s == NT - 1)
                    col += n
                mm.then_inc(num_done, 1)

            def attend(b):
                scores(b, 0)
                scores(b, 1)
                for h in range(HA):
                    values(b, h)
                    if h + 2 < HA:
                        scores(b, h + 2)

            def output(b, t):
                if isinstance(b, int) and b == 0 and t == 0:
                    pe.wait_ge(tables_done, 4)
                pe.wait_ge(y_lo_done, NP * (b + 1))
                m = ROWS[t]
                rows = slice(t * P, t * P + m)
                for j in range(NP):
                    mm = split_products(nc, ps[0:m, 6 + t // 2, (t % 2) * D:(t % 2) * D + D], y_hi[:, j, rows],
                                        y_lo[:, j, rows], wo_hi[:, j, :], wo_lo[:, j, :], j == 0, j == NP - 1)
                mm.then_inc(wo_done, 1)

            def step(b, s1, s2, s3):
                if s3:
                    attend(b)
                if s2:
                    projections(b + 1)
                if s3:
                    output(b, 0)
                if s2:
                    if isinstance(b, int) and b == -1:
                        pe.wait_ge(tables_done, 2)
                    denominators(b + 1)
                if s1:
                    turn_x(b + 2)
                if s3:
                    output(b, 1)
                if s2:
                    spread_out(b + 1)
                if s3:
                    output(b, 2)

            skewed(pe, step)

        @block.scalar
        def _(act):
            act.wait_ge(tables_done, 1)
            nc.scalar.copy(spread[:].rearrange("p j m -> p (j m)"), ps[0:HA, 7, :]).then_inc(tables_done, 1)
            act.wait_ge(bias_in, 16 * NP)

            def evacuate(b):
                nc.scalar.activation(warm[:], g["gam"][:, 0:1], ACT.Exp)
                act.wait_ge(v_done, 2 * b + 1)
                ge(act, num_done, HA * b)
                nc.scalar.copy(v[:, 0:2, :], ps[:, 2:4, :]).then_inc(v_read, 1)
                act.wait_ge(v_done, 2 * b + 2)
                nc.scalar.copy(v[:, 2, :], ps[:, 4, :]).then_inc(v_read, 1)
                for i in range(NP):
                    act.wait_ge(qk_done, NP * b + i + 1)
                    ge(act, phi_done, NP * b + i - 1)
                    nc.scalar.activation(ex[:, i % 2], ps[:, group(i):group(i) + 2, 0:T], ACT.Exp
                                         ).then_inc(exp_done, 1)
                for i in range(NP, NG):
                    act.wait_ge(gate_done, 2 * b + i - NP + 1)
                    if i == NP:
                        ge(act, y_done, NP * b)
                    for k in range(2):
                        j = 2 * (i - NP) + k
                        last = nc.scalar.activation(sg[:, j, :], ps[:, group(i) + k, 0:T], ACT.Sigmoid,
                                                    bias=bg[:, j:j + 1])
                    last.then_inc(gate_read, 1)

            def split_x(b):
                act.wait_ge(x_turned, b + 1)
                ge(act, gate_done, 2 * b)
                nc.scalar.copy(x_hi[:], ps[:, 0:2, 0:TP]).then_inc(hi_done, 1)

            def round_y(b):
                for j in range(NP):
                    act.wait_ge(y_done, NP * b + j + 1)
                    if j == 0:
                        ge(act, wo_done, 3 * b)
                    nc.scalar.copy(y_hi[:, j, :], yt[:, j % 2, :]).then_inc(y_hi_done, 1)

            def step(b, s1, s2, s3):
                if s3:
                    round_y(b)
                if s2:
                    evacuate(b + 1)
                if s1:
                    split_x(b + 2)

            skewed(act, step)

        @block.vector
        def _(dve):
            step = Steps(dve, pick_set, 0)
            for r in range(2):
                rows = slice(r * DK, (r + 1) * DK)
                last = nc.vector.tensor_copy(gpair[rows, :],
                                             g["gam"][rows, :].rearrange("p (j r) -> p j r", r=2)[:, :, r])
            step(last)
            step(nc.vector.memset(pick[:], 0.0))
            for j in range(NP):
                for r in range(2):
                    last = nc.vector.memset(pick[r * DK:(r + 1) * DK, j, 2 * j + r:2 * j + r + 1], 1.0)
            step(last)

            def norm(b):
                step = Steps(dve, ln_steps, 2 * b)
                norm_stats(nc, dve, step, lambda t: res(g, b, t), stats, mv, ve, tick, var_done)
                dve.wait_ge(rstd_done, b + 1)
                ge(dve, x_turned, b)
                for t in range(NT):
                    last = nc.vector.tensor_scalar(xn[:, t, :], res(g, b, t), mv[:, t, 0:1], rstd[:, t, :],
                                                   ALU.subtract, ALU.mult)
                last.then_inc(xn_done, 1)

            def take(b, j):
                dve.wait_ge(num_done, HA * b + 2 * j + 2)
                ge(dve, y_lo_done, NP * b + j - 1)
                nc.vector.tensor_tensor(yt[:, j % 2, :], ps[:, 6 + j % 2, 0:T], sg[:, j, :], ALU.mult
                                        ).then_inc(y_done, 1)

            def split_y(b, j):
                dve.wait_ge(y_hi_done, NP * b + j + 1)
                nc.vector.tensor_tensor(y_lo[:, j, :], yt[:, j % 2, :], y_hi[:, j, :].bitcast(F32), ALU.subtract
                                        ).then_inc(y_lo_done, 1)

            def decay(b):
                for h in range(HA):
                    dve.wait_ge(score_done, HA * b + h + 1)
                    ge(dve, num_done, HA * b + h - 1)
                    nc.vector.tensor_tensor(a[:, h % 2, :], ps[:, 4 + h % 2, 0:AW], g["decay"][:, h, :],
                                            ALU.mult).then_inc(masked, 1)
                    if h % 2 and h > 1:
                        take(b, h // 2 - 1)
                    if h % 2 == 0 and h > 3:
                        split_y(b, h // 2 - 2)
                take(b, NP - 1)
                split_y(b, NP - 2)

            def phi(b):
                for i in range(NP):
                    dve.wait_ge(exp_done, NP * b + i + 1)
                    nc.vector.tensor_scalar(ex[:, i % 2], ex[:, i % 2], 1.0, None, ALU.min).then_inc(low_done, 1)
                    dve.wait_ge(low_done, NP * b + i + 1)
                    if i == 0:
                        ge(dve, score_done, HA * b)
                    nc.vector.scalar_tensor_tensor(out=qk[:, 2 * i:2 * i + 2, 0:T],
                                                   in0=ps[:, group(i):group(i) + 2, 0:T], scalar=0.0,
                                                   in1=ex[:, i % 2], op0=ALU.max,
                                                   op1=ALU.add).then_inc(phi_done, 1)
                dve.wait_ge(phi_done, NP * (b + 1))
                ge(dve, den_done, b)
                for j in range(NP):
                    nc.vector.tensor_tensor_scan(z[:, j, :], gpair[:, j:j + 1].to_broadcast([P, T]),
                                                 qk[:, NP + j, 0:T], 0.0, ALU.mult, ALU.add
                                                 ).then_inc(z_done, 1)
                for j in range(NP // 2, NP):
                    dve.wait_ge(z_done, NP * b + j + 1)
                    nc.vector.tensor_tensor(z[:, j, :], z[:, j, :], qk[:, j, 0:T], ALU.mult
                                            ).then_inc(qz_done, 1)

            def split_x(b):
                dve.wait_ge(hi_done, b + 1)
                nc.vector.tensor_tensor(x_lo[:], ps[:, 0:2, 0:TP], x_hi[:].bitcast(F32),
                                        ALU.subtract).then_inc(lo_done, 1)

            def invert(b):
                step = Steps(dve, den_steps, b)
                dve.wait_ge(den_done, b + 1)
                ge(dve, spread_done, 2 * b)
                step(nc.vector.tensor_scalar(rd[:], ps[0:HA, 5, 0:T], ATT_EPS, None, ALU.add))
                for half in range(2):
                    cols = slice(half * T // 2, (half + 1) * T // 2)
                    nc.vector.reciprocal(rd[:, cols], rd[:, cols]).then_inc(rd_done, 1)

            def divide(b):
                dve.wait_ge(gate_read, 2 * (b + 1))
                for i in range(2):
                    dve.wait_ge(spread_done, 2 * b + i + 1)
                    s = sg[:, 2 * i:2 * i + 2, :]
                    nc.vector.tensor_tensor(s, ps[:, 2 + 2 * i:4 + 2 * i, 0:T], s, ALU.mult).then_inc(sg_done, 1)

            def residual(b, tiles):
                dve.wait_ge(wo_done, 3 * b + 2 + tiles[0] // 2)
                for t in tiles:
                    m = ROWS[t]
                    r = res(g, b, t)[0:m]
                    ins = nc.vector.tensor_tensor(r, ps[0:m, 6 + t // 2, (t % 2) * D:(t % 2) * D + D], r, ALU.add)
                ins.then_inc(res_done, 1)

            def step(b, s1, s2, s3):
                if s3:
                    decay(b)
                if s1:
                    norm(b + 2)
                if s3:
                    split_y(b, NP - 1)
                if s2:
                    phi(b + 1)
                    invert(b + 1)
                if s1:
                    split_x(b + 2)
                if s3:
                    residual(b, (0, 1))
                if s2:
                    divide(b + 1)
                if s3:
                    residual(b, (2,))

            skewed(dve, step)

        @block.gpsimd
        def _(pool):
            def step(b, s1, s2, s3):
                if s1:
                    pool.wait_ge(var_done, b + 3)
                    nc.gpsimd.tensor_tensor(rstd[:], ve[:], g["mhalf"][:, 0:NT].rearrange("p (t a) -> p t a", a=1),
                                            ALU.pow).then_inc(rstd_done, 1)
                if s2:
                    for j in range(NP // 2):
                        pool.wait_ge(z_done, NP * (b + 1) + j + 1)
                        nc.gpsimd.tensor_tensor(z[:, j, :], z[:, j, :], qk[:, j, 0:T], ALU.mult
                                                ).then_inc(qz_done, 1)
                if isinstance(b, int) and b == -1:
                    pool.wait_ge(tables_done, 2)
                    nc.gpsimd.tensor_copy(wo_hi[:], g["wo"][:]).then_inc(tables_done, 1)
                    pool.wait_ge(tables_done, 3)
                    nc.gpsimd.tensor_tensor(wo_lo[:], g["wo"][:], wo_hi[:].bitcast(F32), ALU.subtract
                                            ).then_inc(tables_done, 1)

            skewed(pool, step)


def feed_forward(nc, g, ins):
    with ExitStack() as ctx:
        def sb(name, shape, dt=F32):
            return ctx.enter_context(nc.sbuf_tensor(name, shape, dt))

        def sem(name):
            return ctx.enter_context(nc.semaphore(name))

        ps, hres, ident = g["ps"], g["hres"], g["ident"]
        x3 = g["x3"]
        hraw = sb("c_hraw", [P, FC, D])
        had = sb("c_had", [P, FC, D], F32R)
        wf = sb("c_wf", [P, FC, D])
        wabs = sb("c_wabs", [P, FC])
        wsc = sb("c_wsc", [P, FC])
        wlim = sb("c_wlim", [P, FC, 2])
        tneg = sb("c_tneg", [P, FC, D])
        tern = sb("c_tern", [P, FC, D], BF16)
        tern_t = sb("c_tern_t", [P, FC, D], BF16)
        diag = sb("c_diag", [P, FC, P])
        ones = sb("c_ones", [P, P])
        identb = sb("c_identb", [P, P], BF16)
        wrow = sb("c_wrow", [P, D])
        wq1 = sb("c_wq1", [P, FC, D])
        w1c = sb("c_w1c", [P, FC])
        w1b = sb("c_w1b", [P, FC, P])
        ub = sb("c_ub", [P, D])
        roundc = sb("c_roundc", [P, 1])
        stats = sb("c_stats", [P, NT, 6])
        mv = sb("c_mv", [P, NT, 2])
        ve = sb("c_ve", [P, NT, 1])
        rstd = sb("c_rstd", [P, NT, 1])
        stats3 = sb("c_stats3", [P, NT, 6])
        mv3 = sb("c_mv3", [P, NT, 2])
        ve3 = sb("c_ve3", [P, NT, 1])
        rstd3 = sb("c_rstd3", [P, NT, 1])
        tick = sb("c_tick", [P, 1])
        xn = sb("c_xn", [P, NT, D])
        x_hi = sb("c_x_hi", [P, FC, TP], F32R)
        x_lo = sb("c_x_lo", [P, FC, TP], F32R)
        am = sb("c_am", [P, NT])
        xsc = sb("c_xsc", [P, NT])
        xinv = sb("c_xinv", [P, NT])
        qm = sb("c_qm", [P, NT, D])
        qi = sb("c_qi", [P, NT, D], BF16)
        q_t = sb("c_q_t", [P, FC, TP], BF16)
        fo = sb("c_fo", [P, NT, D])
        x3s = sb("c_x3s", [P, NT, D])
        junk = sb("c_junk", [P, NT, D])
        ags = sb("c_ags", [P, NT])

        w_in = sem("c_w_in")
        later_in = sem("c_later_in")
        prep = sem("c_prep")
        pool_prep = sem("c_pool_prep")
        tern_ready = sem("c_tern_ready")
        tern_turned = sem("c_tern_turned")
        rows_done = sem("c_rows_done")
        rows_read = sem("c_rows_read")
        ternt_ready = sem("c_ternt_ready")
        ln_steps = sem("c_ln_steps")
        var_done = sem("c_var_done")
        rstd_done = sem("c_rstd_done")
        xn_done = sem("c_xn_done")
        x_turned = sem("c_x_turned")
        hi_done = sem("c_hi_done")
        lo_done = sem("c_lo_done")
        had_done = sem("c_had_done")
        q_steps = sem("c_q_steps")
        scaled = sem("c_scaled")
        inv_done = sem("c_inv_done")
        q_done = sem("c_q_done")
        q_turned = sem("c_q_turned")
        qt_done = sem("c_qt_done")
        ff_done = sem("c_ff_done")
        fo_done = sem("c_fo_done")
        fw_done = sem("c_fw_done")
        h2_done = sem("c_h2_done")
        ln3_steps = sem("c_ln3_steps")
        var3_done = sem("c_var3_done")
        rstd3_done = sem("c_rstd3_done")
        x3_done = sem("c_x3_done")
        ag_done = sem("c_ag_done")
        asum_done = sem("c_asum_done")
        acol_done = sem("c_acol_done")
        w_rounded = sem("c_w_rounded")

        def tiles(k):
            return ps[:, k:k + 2, :].rearrange("p k c -> p (k c)")[:, 0:NT * D].rearrange(
                "p (t f) -> p t f", t=NT)

        q_turn = ps[:, 4, :].bitcast(BF16)

        def part_of(w, b):
            n = NJ * 2 * HE // B
            return w[:, :, b * n:(b + 1) * n] if isinstance(b, int) else w[:, :, bass.ds(b * n, n)]

        block = ctx.enter_context(nc.Block())

        @block.sync
        def _(sp):
            for n, t in (("hadamard", hraw), ("ffn_w", wf), ("Wq1", wq1)):
                sp.dma_start(t[:], ins[n].rearrange("(c p) n -> p c n", p=P)).then_inc(w_in, 16)
            for c in range(FC):
                sp.dma_start(w1c[:, c:c + 1], ins["w_conv1"].rearrange("(c p a) -> c p a", p=P, a=1)[c]
                             ).then_inc(w_in, 16)
            for n, t in (("Wk1_t", g["wk_t"]), ("Wv1", g["wv"]), ("Wv1_t", g["wv_t"]), ("gate_t", g["gate"])):
                sp.dma_start(t[:], ins[n].rearrange("(c p) n -> p c n", p=P)).then_inc(later_in, 16)
            sp.wait_ge(later_in, 16 * 4)

        @block.tensor
        def _(pe):
            def weights():
                pe.wait_ge(tern_ready, 1)
                for ic in range(FC):
                    for oc in range(FC):
                        mm = nc.tensor.transpose(q_turn[:, ic * D + oc * P:ic * D + oc * P + P],
                                                 tern[:, oc, ic * P:(ic + 1) * P], identb[:])
                mm.then_inc(tern_turned, 1)
                pe.wait_ge(pool_prep, 3)
                for oc in range(FC):
                    nc.tensor.matmul(ps[:, 7, oc * P:(oc + 1) * P], ones[:], diag[:, oc, :], start=True, stop=True)
                for c in range(FC):
                    mm = nc.tensor.matmul(ps[:, 6, 0:D], w1b[:, c, :], wq1[:, c, :], start=c == 0, stop=c == FC - 1)
                mm.then_inc(rows_done, 1)
                pe.wait_ge(rows_read, 2)

            def turn_x(b):
                pe.wait_ge(xn_done, b + 1)
                ge(pe, hi_done, b)
                ge(pe, lo_done, b)
                for fc in range(FC):
                    for t in range(NT):
                        mm = nc.tensor.transpose(ps[:, fc, t * P:(t + 1) * P],
                                                 xn[:, t, fc * P:(fc + 1) * P], ident[:])
                mm.then_inc(x_turned, 1)

            def rotate(b):
                pe.wait_ge(hi_done, b + 1)
                pe.wait_ge(lo_done, b + 1)
                ge(pe, q_done, b)
                for t in range(NT):
                    for fc in range(FC):
                        for n, x in enumerate((x_hi, x_lo)):
                            mm = nc.tensor.matmul(tiles(2)[:, t, :], x[:, fc, t * P:(t + 1) * P], had[:, fc, :],
                                                  start=fc + n == 0, stop=fc + n == 2)
                mm.then_inc(had_done, 1)

            def turn_q(b):
                pe.wait_ge(q_done, b + 1)
                ge(pe, qt_done, b)
                for fc in range(FC):
                    for t in range(NT):
                        mm = nc.tensor.transpose(q_turn[:, fc * TP + t * P:fc * TP + (t + 1) * P],
                                                 qi[:, t, fc * P:(fc + 1) * P], identb[:])
                mm.then_inc(q_turned, 1)

            def ternary(b):
                pe.wait_ge(qt_done, b + 1)
                ge(pe, fo_done, b)
                for t in range(NT):
                    for fc in range(FC):
                        mm = nc.tensor.matmul(tiles(5)[:, t, :], q_t[:, fc, t * P:(t + 1) * P], tern_t[:, fc, :],
                                              start=fc == 0, stop=fc == FC - 1)
                mm.then_inc(ff_done, 1)

            def agent_sums(b):
                pe.wait_ge(ag_done, b + 1)
                ge(pe, acol_done, b)
                for ic in range(FC):
                    for t in range(NT):
                        m = ROWS[t]
                        mm = nc.tensor.matmul(ps[:, 7, ic:ic + 1], x3s[0:m, t, ic * P:(ic + 1) * P],
                                              ags[0:m, t:t + 1], start=t == 0, stop=t == NT - 1)
                mm.then_inc(asum_done, 1)

            def step(b, s1, s2, s3, s4):
                if s2:
                    if isinstance(b, int) and b == -2:
                        weights()
                        pe.wait_ge(ternt_ready, 1)
                    rotate(b + 2)
                if s4:
                    agent_sums(b)
                if s2:
                    turn_q(b + 2)
                if s1:
                    turn_x(b + 3)
                if s2:
                    ternary(b + 2)

            skewed4(pe, step)

        @block.scalar
        def _(act):
            def weights():
                act.wait_ge(tern_turned, 1)
                nc.scalar.copy(tern_t[:], q_turn[:, 0:FC * D].rearrange("p (c f) -> p c f", c=FC)
                               ).then_inc(ternt_ready, 1)
                act.wait_ge(rows_done, 1)
                nc.scalar.copy(wrow[:], ps[:, 7, 0:D]).then_inc(rows_read, 1)
                nc.scalar.copy(ub[:], ps[:, 6, 0:D]).then_inc(rows_read, 1)
                act.wait_ge(prep, 1)

            def step(b, s1, s2, s3, s4):
                if isinstance(b, int) and b == -2:
                    weights()
                if s2:
                    act.wait_ge(inv_done, b + 3)
                    for t in range(NT):
                        last = nc.scalar.activation(qm[:, t, :], tiles(2)[:, t, :], ACT.Identity,
                                                    bias=roundc[:], scale=xinv[:, t:t + 1])
                    last.then_inc(scaled, 1)
                    act.wait_ge(q_turned, b + 3)
                    ge(act, ff_done, b + 2)
                    nc.scalar.copy(q_t[:], q_turn[:, 0:FC * TP].rearrange("p (c f) -> p c f", c=FC)
                                   ).then_inc(qt_done, 1)
                if s1:
                    act.wait_ge(x_turned, b + 4)
                    ge(act, had_done, b + 3)
                    nc.scalar.copy(x_hi[:], ps[:, 0:2, 0:TP]).then_inc(hi_done, 1)
                if s2:
                    act.wait_ge(ff_done, b + 3)
                    ge(act, h2_done, b + 2)
                    for t in range(NT):
                        last = nc.scalar.mul(fo[:, t, :], tiles(5)[:, t, :], xsc[:, t:t + 1])
                    last.then_inc(fo_done, 1)
                if s4:
                    nc.scalar.copy(part_of(g["w1_hi"], b), part_of(g["w1raw"], b)).then_inc(w_rounded, 1)

            skewed4(act, step)

        @block.vector
        def _(dve):
            def weights():
                dve.wait_ge(w_in, 16 * (3 + FC))
                dve.wait_ge(pool_prep, 1)
                nc.vector.memset(roundc[:], ROUND).then_inc(prep, 1)
                step = Steps(dve, prep, 1)
                nc.vector.tensor_copy(had[:], hraw[:])
                nc.vector.tensor_copy(identb[:], ident[:])
                step(nc.vector.tensor_reduce(wabs[:], wf[:], AX.X, ALU.add, apply_absolute_value=True))
                step(nc.vector.tensor_scalar(wsc[:], wabs[:], 1.0 / D, 1e-5, ALU.mult, ALU.max))
                for s, f in enumerate((0.5, -0.5)):
                    last = nc.vector.tensor_scalar(wlim[:, :, s], wsc[:], f, None, ALU.mult)
                step(last)
                for c in range(FC):
                    last = nc.vector.tensor_scalar(tneg[:, c, :], wf[:, c, :], wlim[:, c, 1:2], None, ALU.is_lt)
                step(last)
                for c in range(FC):
                    last = nc.vector.scalar_tensor_tensor(out=tern[:, c, :], in0=wf[:, c, :], scalar=wlim[:, c, 0:1],
                                                          in1=tneg[:, c, :], op0=ALU.is_gt, op1=ALU.subtract)
                last.then_inc(tern_ready, 1)
                for c in range(FC):
                    nc.vector.tensor_scalar(diag[:, c, :], ident[:], wsc[:, c:c + 1], None, ALU.mult)
                    last = nc.vector.tensor_scalar(w1b[:, c, :], ones[:], w1c[:, c:c + 1], None, ALU.mult)
                    last.then_inc(pool_prep, 1)
                dve.wait_ge(rows_read, 2)

            def norm_sums(b):
                step = Steps(dve, ln_steps, 2 * b)
                norm_stats(nc, dve, step, lambda t: res(g, b, t), stats, mv, ve, tick, var_done)

            def norm(b):
                dve.wait_ge(rstd_done, b + 1)
                ge(dve, x_turned, b)
                for t in range(NT):
                    last = nc.vector.tensor_scalar(xn[:, t, :], res(g, b, t), mv[:, t, 0:1], rstd[:, t, :],
                                                   ALU.subtract, ALU.mult)
                last.then_inc(xn_done, 1)

            def split_x(b):
                dve.wait_ge(hi_done, b + 1)
                nc.vector.tensor_tensor(x_lo[:], ps[:, 0:2, 0:TP], x_hi[:].bitcast(F32),
                                        ALU.subtract).then_inc(lo_done, 1)

            def scale(b):
                step = Steps(dve, q_steps, 3 * b)
                dve.wait_ge(had_done, b + 1)
                step(nc.vector.tensor_reduce(am[:], tiles(2), AX.X, ALU.max, apply_absolute_value=True))
                ge(dve, fo_done, b)
                step(nc.vector.tensor_scalar(xsc[:], am[:], 1e-5, 1.0 / ACT_POS, ALU.max, ALU.mult))
                nc.vector.reciprocal(xinv[:], xsc[:]).then_inc(inv_done, 1)

            def quantise(b):
                step = Steps(dve, q_steps, 3 * b + 2)
                dve.wait_ge(scaled, b + 1)
                step(nc.vector.tensor_scalar(qm[:], qm[:], ROUND + ACT_POS, ROUND - ACT_NEG, ALU.min, ALU.max))
                nc.vector.tensor_scalar(qi[:], qm[:], ROUND, None, ALU.subtract).then_inc(q_done, 1)

            def add(b):
                dve.wait_ge(fw_done, b + 1)
                r = hres[:, NT * b:NT * b + NT, :] if isinstance(b, int) else hres[:, bass.ds(b * NT, NT), :]
                nc.vector.tensor_tensor(r, r, fo[:], ALU.add).then_inc(h2_done, 1)

            def agent_norm_sums(b):
                step = Steps(dve, ln3_steps, 2 * b)
                dve.wait_ge(h2_done, b + 1)
                norm_stats(nc, dve, step, lambda t: res(g, b, t), stats3, mv3, ve3, tick, var3_done)

            def agents(b):
                dve.wait_ge(rstd3_done, b + 1)
                ge(dve, asum_done, b)
                for t in range(NT):
                    last = nc.vector.tensor_scalar(x3s[:, t, :], res(g, b, t), mv3[:, t, 0:1], rstd3[:, t, :],
                                                   ALU.subtract, ALU.mult)
                last.then_inc(x3_done, 1)
                dve.wait_ge(x3_done, b + 1)
                for t in range(NT):
                    last = nc.vector.tensor_tensor_reduce(junk[:, t, :], x3s[:, t, :], ub[:], 1.0, 0.0, ALU.mult,
                                                          ALU.add, ags[:, t:t + 1])
                last.then_inc(ag_done, 1)
                all3 = x3[:, NT * b:NT * b + NT, :] if isinstance(b, int) else x3[:, bass.ds(b * NT, NT), :]
                nc.vector.tensor_copy(all3, x3s[:])
                dve.wait_ge(ag_done, b + 1)
                a3 = g["ag"][:, NT * b:NT * b + NT] if isinstance(b, int) else g["ag"][:, bass.ds(b * NT, NT)]
                nc.vector.tensor_copy(a3, ags[:])

            def take_sums(b):
                dve.wait_ge(asum_done, b + 1)
                ac = g["acol"][:, b, :] if isinstance(b, int) else g["acol"][:, bass.ds(b, 1), :].rearrange(
                    "p a c -> p (a c)")
                nc.vector.tensor_scalar(ac, ps[:, 7, 0:FC], float(D) ** -0.5, None,
                                        ALU.mult).then_inc(acol_done, 1)

            def step(b, s1, s2, s3, s4):
                if isinstance(b, int) and b == -2:
                    weights()
                if s2:
                    scale(b + 2)
                if s1:
                    norm_sums(b + 3)
                if s2:
                    quantise(b + 2)
                if s1:
                    norm(b + 3)
                if s3:
                    agent_norm_sums(b + 1)
                if s1:
                    split_x(b + 3)
                if s4:
                    take_sums(b)
                if s3:
                    agents(b + 1)
                if s2:
                    add(b + 2)

            skewed4(dve, step)

        @block.gpsimd
        def _(pool):
            nc.gpsimd.memset(ones[:], 1.0).then_inc(pool_prep, 1)

            def step(b, s1, s2, s3, s4):
                mh = g["mhalf"][:, 0:NT].rearrange("p (t a) -> p t a", a=1)
                if s1:
                    pool.wait_ge(var_done, b + 4)
                    nc.gpsimd.tensor_tensor(rstd[:], ve[:], mh, ALU.pow).then_inc(rstd_done, 1)
                if s3:
                    pool.wait_ge(var3_done, b + 2)
                    nc.gpsimd.tensor_tensor(rstd3[:], ve3[:], mh, ALU.pow).then_inc(rstd3_done, 1)
                if s2:
                    pool.wait_ge(fo_done, b + 3)
                    wr = wrow[:].rearrange("p (a f) -> p a f", a=1).to_broadcast([P, NT, D])
                    nc.gpsimd.tensor_tensor(fo[:], fo[:], wr, ALU.mult).then_inc(fw_done, 1)
                if s4:
                    pool.wait_ge(w_rounded, b + 1)
                    nc.gpsimd.tensor_tensor(part_of(g["w1_lo"], b), part_of(g["w1raw"], b),
                                            part_of(g["w1_hi"], b).bitcast(F32), ALU.subtract)

            skewed4(pool, step)


def agent_attention(nc, g):
    with ExitStack() as ctx:
        def sb(name, shape, dt=F32):
            return ctx.enter_context(nc.sbuf_tensor(name, shape, dt))

        def sem(name):
            return ctx.enter_context(nc.semaphore(name))

        ps, hres, ident, x3 = g["ps"], g["hres"], g["ident"], g["x3"]
        sel = sb("e_sel", [B, B, P])
        mx = sb("e_mx", [B, 2])
        ex = sb("e_ex", [B, D])
        su = sb("e_su", [B, 2])
        rs = sb("e_rs", [B, 2])
        attn_t = sb("e_attn_t", [P, FC, B])
        w8 = sb("e_w8", [B, D])
        junk = sb("e_junk", [P, 4, D])
        score = sb("e_score", [P, B, NT])
        pr = sb("e_pr", [B, T])
        pt = sb("e_pt", [P, NT, B, B])
        pxs = sb("e_pxs", [B, D])
        px = sb("e_px", [P, FC, B])
        av = sb("e_av", [B, D])
        zero = sb("e_zero", [P, NT * B])
        tok = sb("e_tok", [P, NT * B])
        rtok = sb("e_rtok", [P, NT * B])
        sel_ready = sem("e_sel_ready")
        pe_done = sem("e_pe_done")
        act_done = sem("e_act_done")
        dve_done = sem("e_dve_done")
        scored = sem("e_scored")
        spread_done = sem("e_spread_done")
        block = ctx.enter_context(nc.Block())

        @block.gpsimd
        def _(pool):
            nc.gpsimd.memset(sel[:], 0.0).then_inc(sel_ready, 1)
            nc.gpsimd.memset(pt[:], 0.0).then_inc(sel_ready, 1)
            pool.wait_ge(sel_ready, 2)
            nc.gpsimd.affine_select(out=sel[:], in_=sel[:], compare_op=ALU.not_equal, fill=1.0, base=0,
                                    pattern=[[-1, B], [0, P]], channel_multiplier=1).then_inc(sel_ready, 1)

        def spread(row):
            for b in range(B):
                mm = nc.tensor.matmul(ps[:, b // 2, (b % 2) * D:(b % 2) * D + D], sel[:, b, :], row[:],
                                      start=True, stop=True)
                if b % 2:
                    mm.then_inc(spread_done, 1)

        @block.tensor
        def _(pe):
            for c in range(FC):
                mm = nc.tensor.matmul(ps[0:B, 4, 0:D], g["acol"][:, :, c], g["wk_t"][:, c, :],
                                      start=c == 0, stop=c == FC - 1)
            mm.then_inc(pe_done, 1)
            pe.wait_ge(act_done, 1)
            for c in range(FC):
                mm = nc.tensor.transpose(ps[:, 5, c * B:(c + 1) * B], ex[:, c * P:(c + 1) * P], ident[0:B, 0:B])
            mm.then_inc(pe_done, 1)
            pe.wait_ge(dve_done, 3)
            for c in range(FC):
                mm = nc.tensor.matmul(ps[0:B, 6, 0:D], attn_t[:, c, :], g["wv"][:, c, :],
                                      start=c == 0, stop=c == FC - 1)
            mm.then_inc(pe_done, 1)
            pe.wait_ge(dve_done, 4)
            pe.wait_ge(sel_ready, 3)
            spread(w8)
            pe.wait_ge(scored, NT * B)
            for t in range(NT):
                m = ROWS[t]
                mm = nc.tensor.transpose(ps[0:B, 7, t * P:t * P + m], score[0:m, :, t], ident[0:m, 0:m])
            mm.then_inc(pe_done, 1)
            pe.wait_ge(act_done, 2)
            for t in range(NT):
                m = ROWS[t]
                mm = nc.tensor.transpose(ps[0:m, 4, t * B:(t + 1) * B], pr[:, t * P:t * P + m], ident[0:B, 0:B])
            mm.then_inc(pe_done, 1)
            pe.wait_ge(dve_done, 7)
            for i in range(NI):
                b, t = i // NT, i % NT
                m = ROWS[t]
                mm = nc.tensor.matmul(ps[0:B, 5, 0:D], pt[0:m, t, b, :], x3[0:m, i, :],
                                      start=i == 0, stop=i == NI - 1)
            mm.then_inc(pe_done, 1)
            pe.wait_ge(dve_done, 8)
            for c in range(FC):
                mm = nc.tensor.transpose(ps[:, 6, c * B:(c + 1) * B], pxs[:, c * P:(c + 1) * P], ident[0:B, 0:B])
            mm.then_inc(pe_done, 1)
            pe.wait_ge(dve_done, 9)
            for c in range(FC):
                mm = nc.tensor.matmul(ps[0:B, 7, 0:D], px[:, c, :], g["wv_t"][:, c, :],
                                      start=c == 0, stop=c == FC - 1)
            mm.then_inc(pe_done, 1)
            pe.wait_ge(dve_done, 10)
            spread(av)

        @block.scalar
        def _(act):
            act.wait_ge(dve_done, 1)
            nc.scalar.activation(ex[:], ps[0:B, 4, 0:D], ACT.Exp, bias=mx[:, 0:1],
                                 accum_out=su[:, 0:1]).then_inc(act_done, 1)
            act.wait_ge(dve_done, 5)
            nc.scalar.activation(pr[:], ps[0:B, 7, 0:T], ACT.Exp, bias=mx[:, 1:2],
                                 accum_out=su[:, 1:2]).then_inc(act_done, 1)
            act.wait_ge(scored, NT * B + 1)
            nc.scalar.activation(tok[:], zero[:], ACT.Exp).then_inc(act_done, 1)

        @block.vector
        def _(dve):
            dve.wait_ge(pe_done, 1)
            nc.vector.tensor_reduce(mx[:, 0:1], ps[0:B, 4, 0:D], AX.X, ALU.max, negate=True).then_inc(dve_done, 1)
            dve.wait_ge(act_done, 1)
            nc.vector.reciprocal(rs[:, 0:1], su[:, 0:1]).then_inc(dve_done, 1)
            dve.wait_ge(pe_done, 2)
            nc.vector.tensor_copy(attn_t[:].rearrange("p c b -> p (c b)"), ps[:, 5, 0:FC * B]).then_inc(dve_done, 1)
            dve.wait_ge(pe_done, 3)
            dve.wait_ge(dve_done, 2)
            nc.vector.tensor_scalar(w8[:], ps[0:B, 6, 0:D], rs[:, 0:1], None, ALU.mult).then_inc(dve_done, 1)
            for b in range(B):
                dve.wait_ge(spread_done, b // 2 + 1)
                for t in range(NT):
                    i = NT * b + t
                    if i >= 4:
                        dve.wait_ge(scored, i - 3)
                    nc.vector.tensor_tensor_reduce(junk[:, i % 4, :], x3[:, i, :],
                                                   ps[:, b // 2, (b % 2) * D:(b % 2) * D + D], 1.0, 0.0,
                                                   ALU.mult, ALU.add, score[:, b, t:t + 1]).then_inc(scored, 1)
            nc.vector.tensor_tensor(zero[:], g["ag"][:], g["ag"][:], ALU.subtract).then_inc(scored, 1)
            dve.wait_ge(pe_done, 4)
            nc.vector.tensor_reduce(mx[:, 1:2], ps[0:B, 7, 0:T], AX.X, ALU.max, negate=True).then_inc(dve_done, 1)
            dve.wait_ge(act_done, 2)
            nc.vector.reciprocal(rs[:, 1:2], su[:, 1:2]).then_inc(dve_done, 1)
            dve.wait_ge(pe_done, 5)
            dve.wait_ge(sel_ready, 2)
            for t in range(NT):
                m = ROWS[t]
                diag = pt[0:m, t].rearrange("p b k -> p (b k)")[:, 0:B * B:B + 1]
                last = nc.vector.tensor_copy(diag, ps[0:m, 4, t * B:(t + 1) * B])
            last.then_inc(dve_done, 1)
            dve.wait_ge(pe_done, 6)
            nc.vector.tensor_copy(pxs[:], ps[0:B, 5, 0:D]).then_inc(dve_done, 1)
            dve.wait_ge(pe_done, 7)
            nc.vector.tensor_copy(px[:].rearrange("p c b -> p (c b)"), ps[:, 6, 0:FC * B]).then_inc(dve_done, 1)
            dve.wait_ge(pe_done, 8)
            dve.wait_ge(dve_done, 6)
            nc.vector.tensor_scalar(av[:], ps[0:B, 7, 0:D], rs[:, 1:2], None, ALU.mult).then_inc(dve_done, 1)
            dve.wait_ge(act_done, 3)
            nc.vector.reciprocal(rtok[:], tok[:]).then_inc(dve_done, 1)
            dve.wait_ge(dve_done, 11)
            nc.vector.tensor_tensor(tok[:], tok[:], rtok[:], ALU.mult).then_inc(dve_done, 1)
            dve.wait_ge(dve_done, 12)
            for b in range(B):
                dve.wait_ge(spread_done, B // 2 + b // 2 + 1)
                for t in range(NT):
                    i = NT * b + t
                    m = ROWS[t]
                    nc.vector.scalar_tensor_tensor(out=hres[0:m, i, :],
                                                   in0=ps[0:m, b // 2, (b % 2) * D:(b % 2) * D + D],
                                                   scalar=tok[0:m, i:i + 1], in1=hres[0:m, i, :],
                                                   op0=ALU.mult, op1=ALU.add)


def phase_cd(nc, g, ins, out):
    with ExitStack() as ctx:
        def sb(name, shape, dt=F32):
            return ctx.enter_context(nc.sbuf_tensor(name, shape, dt))

        g["w1_hi"] = sb("w1_hi", [P, FC, NJ * 2 * HE], F32R)
        g["w1_lo"] = sb("w1_lo", [P, FC, NJ * 2 * HE], F32R)
        g["gate"] = sb("gate", [P, FC, E])
        with ExitStack() as agent:
            def sba(name, shape, dt=F32):
                return agent.enter_context(nc.sbuf_tensor(name, shape, dt))

            g["x3"] = sba("x3", [P, NT * B, D])
            g["ag"] = sba("ag", [P, NT * B])
            g["acol"] = sba("acol", [P, B, FC])
            g["wk_t"] = sba("wk_t", [P, FC, D])
            g["wv"] = sba("wv", [P, FC, D])
            g["wv_t"] = sba("wv_t", [P, FC, D])
            feed_forward(nc, g, ins)
            agent_attention(nc, g)
        experts(nc, g, out)


NB = (2 * B * T + E * (P - 1)) // P
NB += NB % 2


def top_two(nc, step, score, bufs):
    n = score.shape[1]
    mx, ex, p, c, one, two, rank = bufs

    def over(t):
        return t[:].to_broadcast([P, n, E])

    step(nc.vector.tensor_reduce(mx[:, :, 0], score, AX.X, ALU.max))
    step(nc.vector.tensor_tensor(ex[:], score, over(mx), ALU.subtract))
    yield
    step(nc.vector.tensor_reduce(mx[:, :, 0], p[:], AX.X, ALU.add))
    step(nc.vector.reciprocal(mx[:, :, 0], mx[:, :, 0]))
    step(nc.vector.tensor_tensor(p[:], p[:], over(mx), ALU.mult))
    for k, pick in enumerate((one, two)):
        step(nc.vector.tensor_reduce(mx[:, :, 0], p[:] if k == 0 else ex[:], AX.X, ALU.max))
        step(nc.vector.tensor_tensor(c[:], p[:] if k == 0 else ex[:], over(mx), ALU.is_equal))
        step(nc.vector.tensor_tensor(c[:], c[:], rank[:], ALU.mult))
        step(nc.vector.tensor_reduce(mx[:, :, 0], c[:], AX.X, ALU.max))
        step(nc.vector.tensor_tensor(pick[:], c[:], over(mx), ALU.is_equal))
        if k == 0:
            step(nc.vector.scalar_tensor_tensor(out=ex[:], in0=one[:], scalar=-2.0, in1=p[:],
                                                op0=ALU.mult, op1=ALU.add))


def shared_expert(nc, g):
    with ExitStack() as ctx:
        def sb(name, shape, dt=F32):
            return ctx.enter_context(nc.sbuf_tensor(name, shape, dt))

        def sem(name):
            return ctx.enter_context(nc.semaphore(name))

        ps, ident = g["ps"], g["ident"]
        w1_hi, w1_lo, ws2 = g["w1_hi"], g["w1_lo"], g["ws2"]
        NC = HS // P
        stats = sb("d_stats", [P, NT, 6])
        mv = sb("d_mv", [P, NT, 2])
        ve = sb("d_ve", [P, NT, 1])
        rstd = sb("d_rstd", [P, NT, 1])
        tick = sb("d_tick", [P, 1])
        xn = sb("d_xn", [P, NT, D])
        x_hi = sb("d_x_hi", [P, FC, TP], F32R)
        x_lo = sb("d_x_lo", [P, FC, TP], F32R)
        g_hi = sb("d_g_hi", [P, FC, E], F32R)
        g_lo = sb("d_g_lo", [P, FC, E], F32R)
        si = sb("d_si", [P, NC, T])
        ht = sb("d_ht", [P, NC, T])
        sct = sb("d_sct", [E, TP])

        g_steps = sem("d_g_steps")
        ln_steps = sem("d_ln_steps")
        var_done = sem("d_var_done")
        rstd_done = sem("d_rstd_done")
        xn_done = sem("d_xn_done")
        x_turned = sem("d_x_turned")
        hi_done = sem("d_hi_done")
        lo_done = sem("d_lo_done")
        h_done = sem("d_h_done")
        silu_done = sem("d_silu_done")
        ht_done = sem("d_ht_done")
        sct_done = sem("d_sct_done")
        z_done = sem("d_z_done")
        z_read = sem("d_z_read")
        stored = sem("d_stored")

        block = ctx.enter_context(nc.Block())

        @block.sync
        def _(sp):
            def store(b):
                sp.wait_ge(xn_done, b + 1)
                rows = g["x_rows"][bass.ds(b * TP, TP)] if not isinstance(b, int) else g["x_rows"][b * TP:(b + 1) * TP]
                sp.dma_start(rows.rearrange("(t p) f -> p t f", p=P), xn[:]).then_inc(stored, 16)

            store(0)
            with sp.Fori(1, B) as b:
                store(b)
            sp.wait_ge(stored, 16 * B)

        @block.tensor
        def _(pe):
            pe.wait_ge(g_steps, 3)

            def turn_x(b):
                pe.wait_ge(xn_done, b + 1)
                ge(pe, lo_done, b)
                for fc in range(FC):
                    for t in range(NT):
                        mm = nc.tensor.transpose(ps[:, fc, t * P:(t + 1) * P],
                                                 xn[:, t, fc * P:(fc + 1) * P], ident[:])
                mm.then_inc(x_turned, 1)

            def hidden(b, i):
                if i == 0:
                    pe.wait_ge(lo_done, b + 1)
                    ge(pe, ht_done, NC * b)
                elif i == 1:
                    ge(pe, sct_done, b)
                else:
                    pe.wait_ge(ht_done, NC * b + i - 1)
                for gate in range(2):
                    col = E * 2 * HE + gate * HS + i * P
                    for fc in range(FC):
                        mm = split_products(nc, ps[:, 2 + 2 * (i % 2) + gate, 0:T], w1_hi[:, fc, col:col + P],
                                            w1_lo[:, fc, col:col + P], x_hi[:, fc, 0:T], x_lo[:, fc, 0:T],
                                            fc == 0, fc == FC - 1)
                mm.then_inc(h_done, 1)

            def scores(b):
                pe.wait_ge(ht_done, NC * b + 2)
                for fc in range(FC):
                    mm = split_products(nc, ps[0:E, 5, 0:T], g_hi[:, fc, :], g_lo[:, fc, :],
                                        x_hi[:, fc, 0:T], x_lo[:, fc, 0:T], fc == 0, fc == FC - 1)
                mm.then_inc(h_done, 1)

            def output(b):
                for t in range(NT):
                    if t != 1:
                        ge(pe, z_read, 2 * b - 1 + t // 2)
                    if t == 2:
                        pe.wait_ge(sct_done, b + 1)
                    m = ROWS[t]
                    for i in range(NC):
                        if t == 0:
                            pe.wait_ge(ht_done, NC * b + i + 1)
                        mm = nc.tensor.matmul(ps[0:m, 6 + t // 2, (t % 2) * D:(t % 2) * D + D],
                                              ht[:, i, t * P:t * P + m], ws2[:, i, :],
                                              start=i == 0, stop=i == NC - 1)
                    if t == 1:
                        mm.then_inc(z_done, 1)
                for t in range(NT):
                    mm = nc.tensor.transpose(ps[:, 7, D + t * E:D + (t + 1) * E], sct[:, t * P:(t + 1) * P],
                                             ident[0:E, 0:E])
                mm.then_inc(z_done, 1)

            def step(b, s1, s2, s3):
                if s3:
                    for i in range(NC):
                        hidden(b, i)
                    scores(b)
                if s2:
                    turn_x(b + 1)
                if s3:
                    output(b)

            skewed(pe, step)

        @block.scalar
        def _(act):
            def step(b, s1, s2, s3):
                if s3:
                    for i in range(NC):
                        act.wait_ge(h_done, (NC + 1) * b + i + 1)
                        nc.scalar.activation(si[:, i, :], ps[:, 3 + 2 * (i % 2), 0:T],
                                             ACT.Silu).then_inc(silu_done, 1)
                if s3:
                    act.wait_ge(h_done, (NC + 1) * (b + 1))
                    nc.scalar.copy(sct[:, 0:T], ps[0:E, 5, 0:T]).then_inc(sct_done, 1)
                if s2:
                    act.wait_ge(x_turned, b + 2)
                    nc.scalar.copy(x_hi[:], ps[:, 0:2, 0:TP]).then_inc(hi_done, 1)

            skewed(act, step)

        @block.vector
        def _(dve):
            nc.vector.memset(sct[:, T:TP], 0.0).then_inc(g_steps, 1)
            nc.vector.tensor_copy(g_hi[:], g["gate"][:]).then_inc(g_steps, 1)
            dve.wait_ge(g_steps, 2)
            nc.vector.tensor_tensor(g_lo[:], g["gate"][:], g_hi[:].bitcast(F32), ALU.subtract).then_inc(g_steps, 1)

            def norm_sums(b):
                step = Steps(dve, ln_steps, 2 * b)
                norm_stats(nc, dve, step, lambda t: res(g, b, t), stats, mv, ve, tick, var_done)

            def norm(b):
                dve.wait_ge(rstd_done, b + 1)
                ge(dve, stored, 16 * b)
                ge(dve, x_turned, b)
                for t in range(NT):
                    last = nc.vector.tensor_scalar(xn[:, t, :], res(g, b, t), mv[:, t, 0:1], rstd[:, t, :],
                                                   ALU.subtract, ALU.mult)
                last.then_inc(xn_done, 1)

            def split_x(b):
                dve.wait_ge(hi_done, b + 1)
                nc.vector.tensor_tensor(x_lo[:], ps[:, 0:2, 0:TP], x_hi[:].bitcast(F32),
                                        ALU.subtract).then_inc(lo_done, 1)

            def gated(b):
                for i in range(NC):
                    dve.wait_ge(silu_done, NC * b + i + 1)
                    nc.vector.tensor_tensor(ht[:, i, :], ps[:, 2 + 2 * (i % 2), 0:T], si[:, i, :],
                                            ALU.mult).then_inc(ht_done, 1)

            def take(b, tiles):
                dve.wait_ge(z_done, 2 * b + 1 + tiles[0] // 2)
                for t in tiles:
                    r = res(g, b, t)[0:ROWS[t]]
                    add = nc.vector.tensor_tensor(r, ps[0:ROWS[t], 6 + t // 2, (t % 2) * D:(t % 2) * D + D],
                                                  r, ALU.add)
                if t == 1:
                    add.then_inc(z_read, 1)
                else:
                    sc = g["score"][:, NT * b:NT * b + NT, :] if isinstance(b, int) else (
                        g["score"][:, bass.ds(b * NT, NT), :])
                    nc.vector.tensor_copy(sc, ps[:, 7, D:D + NT * E].rearrange("p (t e) -> p t e", t=NT)
                                          ).then_inc(z_read, 1)

            def step(b, s1, s2, s3):
                if s3:
                    gated(b)
                if s2:
                    split_x(b + 1)
                if s1:
                    norm_sums(b + 2)
                if s3:
                    take(b, (0, 1))
                if s1:
                    norm(b + 2)
                if s3:
                    take(b, (2,))

            skewed(dve, step)

        @block.gpsimd
        def _(pool):
            def step(b, s1, s2, s3):
                if s1:
                    pool.wait_ge(var_done, b + 3)
                    nc.gpsimd.tensor_tensor(rstd[:], ve[:], g["mhalf"][:, 0:NT].rearrange("p (t a) -> p t a", a=1),
                                            ALU.pow).then_inc(rstd_done, 1)

            skewed(pool, step)


def route(nc, g):
    with ExitStack() as ctx:
        def sb(name, shape, dt=F32):
            return ctx.enter_context(nc.sbuf_tensor(name, shape, dt))

        def sem(name):
            return ctx.enter_context(nc.semaphore(name))

        ps = g["ps"]
        mx = sb("r_mx", [P, NI, 1])
        ex = sb("r_ex", [P, NI, E])
        pr = sb("r_pr", [P, NI, E])
        cc = sb("r_cc", [P, NI, E])
        pick = [sb("r_one", [P, NI, E]), sb("r_two", [P, NI, E])]
        rank = sb("r_rank", [P, NI, E])
        valid = sb("r_valid", [P, NI, 1])
        both = sb("r_both", [P, NI, E])
        upper = sb("r_upper", [P, P])
        ones = sb("r_ones", [P, P])
        cnt = sb("r_cnt", [P, E, NI])
        cum = sb("r_cum", [P, E, NI])
        keep = sb("r_keep", [P, E, NI])
        nblk = sb("r_nblk", [P, E])
        bend = sb("r_bend", [P, E])
        base = sb("r_base", [P, E])
        slot = sb("r_slot", [P, NI, E])
        sk = sb("r_sk", [P, 2, NI])
        blk = sb("r_blk", [P, 2, NI])
        row = sb("r_row", [P, 2, NI])
        wk = sb("r_wk", [P, 2, NI])
        dst = sb("r_dst", [P, 2, NI])
        cols = sb("r_cols", [P, P])
        pads = sb("r_pads", [P, 1])
        hot = sb("r_hot", [P, 2 * NI, P])
        one = sb("r_isblk", [P, 2 * NI, NB])
        val = sb("r_val", [P, 2 * NI, 2, NB])
        found_t = sb("r_found_t", [2 * NB, P])
        found = sb("r_found", [P, 2 * NB])
        tok = sb("r_tok", [P, NB])
        isp = sb("r_isp", [P, NB])
        bex = sb("r_bex", [P, NB])

        const = sem("r_const")
        steps = sem("r_steps")
        exp_done = sem("r_exp_done")
        both_done = sem("r_both_done")
        hot_done = sem("r_hot_done")
        pe_done = sem("r_pe_done")
        one_done = sem("r_one_done")
        found_done = sem("r_found_done")
        val_done = sem("r_val_done")
        PART = 2 * NI // 6
        block = ctx.enter_context(nc.Block())

        @block.gpsimd
        def _(pool):
            for e in range(E):
                nc.gpsimd.memset(rank[:, :, e:e + 1], float(E - e))
            nc.gpsimd.memset(ones[:], 1.0)
            nc.gpsimd.iota(cols[:], [[1, P]], base=0, channel_multiplier=0, allow_small_or_imprecise_dtypes=True)
            for k in range(2):
                nc.gpsimd.iota(dst[:, k, :], [[2 * P, NI]], base=k + 1, channel_multiplier=2,
                               allow_small_or_imprecise_dtypes=True)
            nc.gpsimd.iota(pads[:], [[0, 1]], base=2 * P * NI + 1, channel_multiplier=1,
                           allow_small_or_imprecise_dtypes=True)
            nc.gpsimd.memset(valid[:], 1.0)
            nc.gpsimd.memset(keep[:], 1.0)
            nc.gpsimd.memset(upper[:], 1.0).then_inc(const, 1)
            pool.wait_ge(const, 1)
            nc.gpsimd.affine_select(out=upper[:], in_=upper[:], compare_op=ALU.is_gt, fill=0.0, base=0,
                                    pattern=[[1, P]], channel_multiplier=-1).then_inc(const, 1)
            vt = valid[:].rearrange("p (b t) a -> p b (t a)", t=NT)[:, :, NT - 1:NT]
            nc.gpsimd.affine_select(out=vt, in_=vt, compare_op=ALU.is_gt, fill=0.0, base=TXT,
                                    pattern=[[0, B], [0, 1]], channel_multiplier=-1).then_inc(const, 1)
            for e in range(E):
                ms = nc.gpsimd.memset(keep[:, e, 0:1], 0.0)
            ms.then_inc(const, 1)
            pool.wait_ge(one_done, 1)
            nc.gpsimd.tensor_tensor(val[:, :, 1, :], one[:],
                                    wk[:].rearrange("p k (i a) -> p (k i) a", a=1).to_broadcast([P, 2 * NI, NB]),
                                    ALU.mult).then_inc(val_done, 1)

        @block.scalar
        def _(act):
            act.wait_ge(steps, 2)
            nc.scalar.activation(pr[:], ex[:], ACT.Exp).then_inc(exp_done, 1)

        @block.tensor
        def _(pe):
            pe.wait_ge(both_done, 1)
            m = both[:].rearrange("p i e -> p (i e)")
            nc.tensor.matmul(ps[:, 0, 0:NI * E], upper[:], m, start=True, stop=True)
            nc.tensor.matmul(ps[:, 1, 0:NI * E], ones[:], m, start=True, stop=True).then_inc(pe_done, 1)
            pe.wait_ge(val_done, 2)
            for n in range(2 * NI):
                if n % PART == 0:
                    pe.wait_ge(hot_done, n // PART + 1)
                mm = nc.tensor.matmul(ps[0:2 * NB, 2, 0:P], val[:, n].rearrange("p c j -> p (c j)"), hot[:, n, :],
                                      start=n == 0, stop=n == 2 * NI - 1)
            mm.then_inc(pe_done, 1)
            pe.wait_ge(found_done, 1)
            nc.tensor.transpose(ps[:, 3, 0:2 * NB], found_t[:], g["ident"][0:2 * NB, 0:2 * NB]).then_inc(pe_done, 1)

        @block.vector
        def _(dve):
            step = Steps(dve, steps, 0)
            V = nc.vector

            def whole(out_, in_):
                step(V.tensor_scalar(out_, in_, 1.0 / P, 0.5 / P - 0.5, ALU.mult, ALU.add))
                step(V.tensor_scalar(out_, out_, ROUND, None, ALU.add))
                step(V.tensor_scalar(out_, out_, ROUND, None, ALU.subtract))

            choose = top_two(nc, step, g["score"][:], (mx, ex, pr, cc, *pick, rank))
            next(choose)
            dve.wait_ge(exp_done, 1)
            dve.wait_ge(const, 4)
            for _ in choose:
                pass
            over = valid[:].to_broadcast([P, NI, E])
            for k in range(2):
                step(V.tensor_tensor(pick[k][:], pick[k][:], over, ALU.mult))
            V.tensor_tensor(both[:], pick[0][:], pick[1][:], ALU.add).then_inc(both_done, 1)
            for k in range(2):
                step(V.tensor_tensor(cc[:], pick[k][:], pr[:], ALU.mult))
                step(V.tensor_reduce(wk[:, k, :], cc[:], AX.X, ALU.add))
            dve.wait_ge(pe_done, 1)
            step(V.tensor_copy(cnt[:], ps[:, 1, 0:NI * E].rearrange("p (i e) -> p e i", e=E)))
            step(V.tensor_tensor_scan(cum[:].rearrange("p e i -> p (e i)"), keep[:].rearrange("p e i -> p (e i)"),
                                      cnt[:].rearrange("p e i -> p (e i)"), 0.0, ALU.mult, ALU.add))
            step(V.tensor_scalar(nblk[:], cum[:, :, NI - 1], float(P - 1), None, ALU.add))
            whole(nblk[:], nblk[:])
            step(V.tensor_tensor_scan(bend[:], ones[:, 0:E], nblk[:], 0.0, ALU.mult, ALU.add))
            step(V.tensor_tensor(base[:], bend[:], nblk[:], ALU.subtract))
            step(V.tensor_scalar(base[:], base[:], float(P), None, ALU.mult))
            step(V.tensor_tensor(cum[:], cum[:], cnt[:], ALU.subtract))
            step(V.tensor_tensor(cum[:], cum[:], base[:].rearrange("p (e a) -> p e a", a=1).to_broadcast([P, E, NI]),
                                 ALU.add))
            step(V.tensor_tensor(slot[:], ps[:, 0, 0:NI * E].rearrange("p (i e) -> p i e", e=E),
                                 cum[:].rearrange("p e i -> p i e"), ALU.add))
            for k in range(2):
                step(V.tensor_tensor(cc[:], pick[k][:], slot[:], ALU.mult))
                step(V.tensor_reduce(sk[:, k, :], cc[:], AX.X, ALU.add))
            whole(blk[:], sk[:])
            step(V.scalar_tensor_tensor(out=row[:], in0=blk[:], scalar=-float(P), in1=sk[:],
                                        op0=ALU.mult, op1=ALU.add))
            for k in range(2):
                step(V.scalar_tensor_tensor(out=blk[:, k, :], in0=blk[:, k, :], scalar=1.0, in1=valid[:, :, 0],
                                            op0=ALU.add, op1=ALU.mult))
            step(V.tensor_scalar(blk[:], blk[:], -1.0, None, ALU.add))
            def over(t, n):
                return t.rearrange("p k (i a) -> p (k i) a", a=1).to_broadcast([P, 2 * NI, n])

            blocks = cols[:, 0:NB].rearrange("p (a j) -> p a j", a=1).to_broadcast([P, 2 * NI, NB])
            rows = cols[:].rearrange("p (a j) -> p a j", a=1).to_broadcast([P, PART, P])
            V.tensor_tensor(one[:], blocks, over(blk[:], NB), ALU.is_equal).then_inc(one_done, 1)
            dve.wait_ge(one_done, 1)
            V.tensor_tensor(val[:, :, 0, :], one[:], over(dst[:], NB), ALU.mult).then_inc(val_done, 1)
            for n in range(0, 2 * NI, PART):
                V.tensor_tensor(hot[:, n:n + PART, :], rows,
                                row[:].rearrange("p k (i a) -> p (k i) a", a=1)[:, n:n + PART].to_broadcast(
                                    [P, PART, P]), ALU.is_equal).then_inc(hot_done, 1)
            step(V.tensor_scalar(bex[:], cols[:, 0:NB], bend[:, 0:1], None, ALU.is_ge))
            for e in range(1, E - 1):
                step(V.scalar_tensor_tensor(out=bex[:], in0=cols[:, 0:NB], scalar=bend[:, e:e + 1], in1=bex[:],
                                            op0=ALU.is_ge, op1=ALU.add))
            step(V.tensor_copy(g["bex_i"][:], bex[:]))
            dve.wait_ge(pe_done, 2)
            V.tensor_copy(found_t[:], ps[0:2 * NB, 2, 0:P]).then_inc(found_done, 1)
            dve.wait_ge(pe_done, 3)
            step(V.tensor_copy(found[:], ps[:, 3, 0:2 * NB]))
            step(V.tensor_copy(g["w_slot"][:], found[:, NB:2 * NB]))
            step(V.tensor_scalar(tok[:], found[:, 0:NB], 0.5, -0.75, ALU.mult, ALU.add))
            step(V.tensor_scalar(tok[:], tok[:], ROUND, None, ALU.add))
            step(V.tensor_scalar(tok[:], tok[:], ROUND, 0.0, ALU.subtract, ALU.max))
            step(V.tensor_copy(g["src_i"][:], tok[:]))
            step(V.tensor_scalar(isp[:], found[:, 0:NB], 0.0, pads[:], ALU.is_equal, ALU.mult))
            step(V.scalar_tensor_tensor(out=isp[:], in0=found[:, 0:NB], scalar=-1.0, in1=isp[:],
                                        op0=ALU.add, op1=ALU.add))
            step(V.tensor_copy(g["dst_i"][:], isp[:]))


def paired(eng, step, depth):
    total = NB + depth - 1
    first = depth + (depth % 2)

    def run(j, u):
        on = [True] * depth if not isinstance(j, int) else [0 <= j - s < NB for s in range(depth)]
        step(j, u, on)

    for j in range(first):
        run(j, j % 2)
    with eng.Fori(first // 2, NB // 2) as i:
        for u in range(2):
            run(2 * i + u, u)
    for j in range(NB, total):
        run(j, j % 2)


def expert_blocks(nc, g):
    with ExitStack() as ctx:
        def sb(name, shape, dt=F32):
            return ctx.enter_context(nc.sbuf_tensor(name, shape, dt))

        def sem(name):
            return ctx.enter_context(nc.semaphore(name))

        ps, ident = g["ps"], g["ident"]
        w1_hi, w1_lo, w2 = g["w1_hi"], g["w1_lo"], g["w2"]
        idx = [sb(f"f_idx{u}", [P, 1], U32) for u in range(2)]
        odx = [sb(f"f_odx{u}", [P, 1], U32) for u in range(2)]
        xg = [sb(f"f_xg{u}", [P, D]) for u in range(2)]
        yo = [sb(f"f_yo{u}", [P, D]) for u in range(2)]
        x_hi = sb("f_x_hi", [P, 2, D], F32R)
        x_lo = sb("f_x_lo", [P, 2, D], F32R)
        si = sb("f_si", [P, 2, HE])
        hg = sb("f_hg", [P, 2, 2 * P])
        ht = sb("f_ht", [HE // 2, 2, 2, P])
        tick = sb("f_tick", [P, 2])

        idx_set = sem("f_idx_set")
        odx_set = sem("f_odx_set")
        gathered = [sem(f"f_gathered{u}") for u in range(2)]
        scattered = [sem(f"f_scattered{u}") for u in range(2)]
        x_turned = sem("f_x_turned")
        hi_done = sem("f_hi_done")
        lo_done = sem("f_lo_done")
        h_done = sem("f_h_done")
        silu_done = sem("f_silu_done")
        hg_done = sem("f_hg_done")
        h_turned = sem("f_h_turned")
        ht_done = sem("f_ht_done")
        z_done = sem("f_z_done")
        yo_done = sem("f_yo_done")
        tick_set = sem("f_tick_set")

        DEPTH = 6
        block = ctx.enter_context(nc.Block())

        @block.tensor
        def _(pe):
            def turn_x(j, u):
                pe.wait_ge(gathered[u], 8 * (j - u) + 16)
                ge(pe, lo_done, j - 1)
                for fc in range(FC):
                    mm = nc.tensor.transpose(ps[:, u, fc * P:(fc + 1) * P], xg[u][:, fc * P:(fc + 1) * P], ident[:])
                mm.then_inc(x_turned, 1)

            def hidden(j, u, e):
                pe.wait_ge(lo_done, j + 1)
                ge(pe, hg_done, j - 1)
                for fc in range(FC):
                    cols = bass.ds(e * (2 * HE), 2 * HE)
                    rows = slice(fc * P, (fc + 1) * P)
                    mm = split_products(nc, ps[:, 2 + u, 0:2 * HE], x_hi[:, u, rows], x_lo[:, u, rows],
                                        w1_hi[:, fc, cols], w1_lo[:, fc, cols], fc == 0, fc == FC - 1)
                mm.then_inc(h_done, 1)

            def turn(j, u):
                pe.wait_ge(hg_done, j + 1)
                ge(pe, ht_done, j - 1)
                for k in range(2):
                    mm = nc.tensor.transpose(ps[0:HE // 2, 4 + u, k * P:(k + 1) * P],
                                             hg[:, u, k * P:k * P + HE // 2], ident[:])
                mm.then_inc(h_turned, 1)

            def second(j, u, e):
                pe.wait_ge(ht_done, j + 1)
                ge(pe, yo_done, j - 1)
                for k in range(2):
                    mm = nc.tensor.matmul(ps[:, 6 + u, 0:D], ht[:, u, k, :],
                                          w2[:, k, bass.ds(e, 1), :].rearrange("p a f -> p (a f)"),
                                          start=k == 0, stop=k == 1)
                mm.then_inc(z_done, 1)

            def expert(j):
                at = g["bex_i"][0:1, j:j + 1] if isinstance(j, int) else g["bex_i"][0:1, bass.ds(j, 1)]
                return pe.value_load(at, min_val=0, max_val=E - 1)

            def step(j, u, on):
                v = 1 - u
                hidden_of = expert(j - 2) if on[2] else None
                output_of = expert(j - 4) if on[4] else None
                if on[2]:
                    hidden(j - 2, u, hidden_of)
                if on[1]:
                    turn_x(j - 1, v)
                if on[4]:
                    second(j - 4, u, output_of)
                if on[3]:
                    turn(j - 3, v)

            paired(pe, step, DEPTH)

        @block.scalar
        def _(act):
            def step(j, u, on):
                v = 1 - u
                if on[2]:
                    act.wait_ge(h_done, j - 1)
                    ge(act, hg_done, j - 3)
                    nc.scalar.activation(si[:, u, :], ps[:, 2 + u, HE:2 * HE], ACT.Silu).then_inc(silu_done, 1)
                if on[1]:
                    act.wait_ge(x_turned, j)
                    ge(act, h_done, j - 2)
                    nc.scalar.copy(x_hi[:, v, :], ps[:, v, 0:D]).then_inc(hi_done, 1)
                if on[4]:
                    act.wait_ge(z_done, j - 3)
                    ge(act, scattered[u], 8 * (j - 4 - u))
                    nc.scalar.copy(yo[u][:], ps[:, 6 + u, 0:D]).then_inc(yo_done, 1)
                if on[3]:
                    act.wait_ge(h_turned, j - 2)
                    ge(act, z_done, j - 4)
                    nc.scalar.copy(ht[:, v].rearrange("p k m -> p (k m)"), ps[0:HE // 2, 4 + v, 0:2 * P]
                                   ).then_inc(ht_done, 1)

            paired(act, step, DEPTH)

        @block.vector
        def _(dve):
            def column(t, j):
                return t[:, j:j + 1] if isinstance(j, int) else t[:, bass.ds(j, 1)]

            def step(j, u, on):
                v = 1 - u
                if on[0]:
                    ge(dve, gathered[u], 8 * (j - u))
                    nc.vector.tensor_copy(idx[u][:], column(g["src_i"], j)).then_inc(idx_set, 1)
                if on[2]:
                    dve.wait_ge(silu_done, j - 1)
                    ge(dve, h_turned, j - 3)
                    nc.vector.scalar_tensor_tensor(
                        out=hg[:, u, :].rearrange("p (k m) -> p k m", k=2)[:, :, 0:HE // 2],
                        in0=ps[:, 2 + u, 0:HE].rearrange("p (k m) -> p k m", k=2),
                        scalar=column(g["w_slot"], j - 2),
                        in1=si[:, u, :].rearrange("p (k m) -> p k m", k=2),
                        op0=ALU.mult, op1=ALU.mult).then_inc(hg_done, 1)
                if on[1]:
                    dve.wait_ge(hi_done, j)
                    nc.vector.tensor_tensor(x_lo[:, v, :], ps[:, v, 0:D], x_hi[:, v, :].bitcast(F32),
                                            ALU.subtract).then_inc(lo_done, 1)
                if on[4]:
                    ge(dve, scattered[u], 8 * (j - 4 - u))
                    nc.vector.tensor_copy(odx[u][:], column(g["dst_i"], j - 4)).then_inc(odx_set, 1)

            paired(dve, step, DEPTH)

        @block.gpsimd
        def _(pool):
            nc.gpsimd.memset(tick[:], 0.0).then_inc(tick_set, 1)

            def ticks(j):
                return 1 + (min(j, NB) + max(0, j - 5) if isinstance(j, int) else 2 * j - 5)

            def hold(n):
                pool.wait_ge(tick_set, n)
                nc.gpsimd.tensor_tensor(tick[:, 1:2], tick[:, 0:1], tick[:, 0:1], ALU.add).then_inc(tick_set, 1)

            def step(j, u, on):
                v = 1 - u
                if on[0]:
                    pool.wait_ge(idx_set, j + 1)
                    ge(pool, x_turned, j - 1)
                    hold(ticks(j))
                    pool.indirect_dma_start(xg[u][:], None, g["x_rows"],
                                            bass.IndirectOffsetOnAxis(ap=idx[u][:], axis=0)
                                            ).then_inc(gathered[u], 16)
                if on[5]:
                    pool.wait_ge(yo_done, j - 4)
                    pool.wait_ge(odx_set, j - 4)
                    if not isinstance(j, int) or j > 5:
                        pool.wait_ge(scattered[u], 8 * (j - 6 - u) + 16)
                    hold(ticks(j) + (1 if on[0] else 0))
                    pool.indirect_dma_start(g["y_rows"], bass.IndirectOffsetOnAxis(ap=odx[v][:], axis=0),
                                            yo[v][:], None).then_inc(scattered[v], 16)

            paired(pool, step, DEPTH)
            for u in range(2):
                pool.wait_ge(scattered[u], 8 * NB)


def combine(nc, g, out):
    with ExitStack() as ctx:
        hres = g["hres"]
        RING = 4
        yin = ctx.enter_context(nc.sbuf_tensor("z_yin", [P, RING, NT, 2, D], F32))
        loaded = [ctx.enter_context(nc.semaphore(f"z_loaded{u}")) for u in range(RING)]
        half_done = ctx.enter_context(nc.semaphore("z_half_done"))
        added = ctx.enter_context(nc.semaphore("z_added"))
        stored = ctx.enter_context(nc.semaphore("z_stored"))
        block = ctx.enter_context(nc.Block())

        def parts(t, b):
            return t[:, NT * b:NT * b + 2], t[0:TXT, NT * b + 2]

        @block.sync
        def _(sp):
            for b in range(B):
                if b >= RING:
                    sp.wait_ge(added, 2 * (b - RING + 1))
                y = yin[:, b % RING]
                first = 2 * TP * b
                sp.dma_start(y[:, 0:2], g["y_rows"][first:first + 4 * P, :].rearrange(
                    "(t p k) f -> p t k f", t=2, k=2)).then_inc(loaded[b % RING], 16)
                sp.dma_start(y[0:TXT, 2], g["y_rows"][first + 4 * P:first + 4 * P + 2 * TXT, :].rearrange(
                    "(p k) f -> p k f", k=2)).then_inc(loaded[b % RING], 16)

        @block.scalar
        def _(act):
            for b in range(B):
                act.wait_ge(added, 2 * (b + 1))
                whole, rest = parts(hres, b)
                act.dma_start(out[b, 0:2 * P].rearrange("(t p) f -> p t f", t=2), whole).then_inc(stored, 16)
                act.dma_start(out[b, 2 * P:T], rest).then_inc(stored, 16)
            act.wait_ge(stored, 32 * B)

        @block.vector
        def _(dve):
            def rows(b):
                y = yin[:, b % RING]
                return y[:, 0:2], y[0:TXT, 2:3]

            for b in range(B + 1):
                if b < B:
                    dve.wait_ge(loaded[b % RING], 32 * (b // RING + 1))
                    for y in rows(b):
                        nc.vector.tensor_tensor(y[:, :, 0, :], y[:, :, 0, :], y[:, :, 1, :],
                                                ALU.add).then_inc(half_done, 1)
                if b >= 1:
                    dve.wait_ge(half_done, 2 * b)
                    h = hres[:, NT * (b - 1):NT * (b - 1) + 2], hres[0:TXT, NT * b - 1:NT * b]
                    for r, y in zip(h, rows(b - 1)):
                        nc.vector.tensor_tensor(r, r, y[:, :, 0, :], ALU.add).then_inc(added, 1)


def experts(nc, g, out):
    with ExitStack() as ctx:
        def sb(name, shape, dt=F32):
            return ctx.enter_context(nc.sbuf_tensor(name, shape, dt))

        g["score"] = sb("score", [P, NI, E])
        g["src_i"] = sb("src_i", [P, NB], U32)
        g["dst_i"] = sb("dst_i", [P, NB], U32)
        g["w_slot"] = sb("w_slot", [P, NB])
        g["bex_i"] = sb("bex_i", [P, NB], U32)
        g["x_rows"] = nc.dram_tensor("x_rows", (P * NI, D), F32, kind="Internal").ap()
        g["y_rows"] = nc.dram_tensor("y_rows", (2 * P * NI + P, D), F32, kind="Internal").ap()
        shared_expert(nc, g)
        route(nc, g)
        expert_blocks(nc, g)
        combine(nc, g, out)





def build(nc, ins, out):
    with ExitStack() as ctx:
        def sb(name, shape, dt=F32):
            return ctx.enter_context(nc.sbuf_tensor(name, shape, dt))

        g = {
            "ps": ctx.enter_context(nc.psum_tensor("ps", [P, 8, 512], F32)),
            "hres": sb("hres", [P, NT * B, D]),
            "ident": sb("ident", [P, P]),
            "mhalf": sb("mhalf", [P, 8]),
            "w1raw": sb("w1raw", [P, FC, NJ * 2 * HE]),
            "w2": sb("w2", [HE // 2, 2, E, D]),
            "ws2": sb("ws2", [P, HS // P, D]),
            "ident_ready": ctx.enter_context(nc.semaphore("ident_ready")),
        }
        setup(nc, g)
        with ExitStack() as attn:
            def sba(name, shape, dt=F32):
                return attn.enter_context(nc.sbuf_tensor(name, shape, dt))

            g["wa_hi"] = sba("wa_hi", [P, FC, 4 * DA], F32R)
            g["wa_lo"] = sba("wa_lo", [P, FC, 4 * DA], F32R)
            g["gam"] = sba("gam", [P, HA])
            g["W_g_b"] = ins["W_g_b"]
            g["wo"] = sba("wo", [P, DA // P, D])
            g["decay"] = sba("decay", [P, HA, SCORE_COLS])
            token_mixer(nc, g, ins)
            linear_attention(nc, g)
        phase_cd(nc, g, ins, out)


def kernel(**inputs):
    import numpy as np
    import concourse.bacc as bacc
    from concourse.bass_utils import run_bass_kernel_spmd

    nc = bacc.Bacc("TRN2", target_bir_lowering=False, num_devices=1)
    i = {k: np.asarray(v) for k, v in inputs.items()}
    x = i["x"]
    arrays = {
        "x_t": x.transpose(0, 1, 3, 2),
        "x_flat": x.transpose(0, 2, 3, 1).reshape(B, L, H0 * F),
        "txt": i["txt"],
        "wq_t": i["L0_tok_Wq_w"].T, "wk_t": i["L0_tok_Wk_w"].T, "wv_t": i["L0_tok_Wv_w"].T,
        "bq": i["L0_tok_Wq_b"], "bk": i["L0_tok_Wk_b"], "bv": i["L0_tok_Wv_b"],
        "w_bias_t": i["L0_tok_w_bias"].T,
        "mask_t": i["L0_tok_local_mask"].T,
        "out_w": i["L0_tok_out_w"], "out_b": i["L0_tok_out_b"],
        "ln_g": i["L0_tok_ln_g"], "ln_b": i["L0_tok_ln_b"],
        "W_Q_t": i["L0_attn_W_Q"].T, "W_K_t": i["L0_attn_W_K"].T,
        "W_V_t": i["L0_attn_W_V"].T, "W_g_t": i["L0_attn_W_g_w"].T,
        "W_g_b": i["L0_attn_W_g_b"], "W_O_t": i["L0_attn_W_O"].T,
        "decay_log": i["L0_attn_decay_log"],
        "ffn_w": i["L0_ffn_weight"],
        "Wq1": i["L1_attn_w_qkv"][0:D], "Wk1_t": i["L1_attn_w_qkv"][D:2 * D].T,
        "Wv1": i["L1_attn_w_qkv"][2 * D:], "Wv1_t": i["L1_attn_w_qkv"][2 * D:].T,
        "w_conv1": i["L1_attn_w_conv1"],
        "gate_t": i["L1_ffn_gate_w"].T,
        "W1_t": i["L1_ffn_W1"].transpose(0, 2, 1), "W2_t": i["L1_ffn_W2"].transpose(0, 2, 1),
        "Ws1_t": i["L1_ffn_Ws1"].T, "Ws2_t": i["L1_ffn_Ws2"].T,
        "hadamard": hadamard(np),
    }
    arrays = {f"in_{n}": np.ascontiguousarray(a) for n, a in arrays.items()}
    ins = {n[3:]: nc.dram_tensor(n, a.shape, mybir.dt.from_np(a.dtype), kind="ExternalInput").ap()
           for n, a in arrays.items()}
    out = nc.dram_tensor("out", (B, T, D), F32, kind="ExternalOutput").ap()
    build(nc, ins, out)
    return run_bass_kernel_spmd(nc, [arrays], core_ids=[0]).results[0]["out"]


def hadamard(np):
    h = np.array([[1.0]])
    while h.shape[0] < D:
        h = np.block([[h, h], [h, -h]])
    return (h / np.sqrt(D)).astype(np.float32)
```
